# Optimizing a Trainium2 kernel written in Bass

```python
import numpy as np
import jax
import jax.numpy as jnp

def _softmax(x, axis=-1):
    return jax.nn.softmax(x, axis=axis)

def _gelu(x):
    return jax.nn.gelu(x, approximate=True)

def _silu(x):
    return jax.nn.silu(x)

def _sigmoid(x):
    return jax.nn.sigmoid(x)

def _layernorm(x, axis=-1, eps=1e-05):
    m = jnp.mean(x, axis=axis, keepdims=True)
    v = jnp.var(x, axis=axis, keepdims=True)
    return (x - m) / jnp.sqrt(v + eps)

def _scatter_add(tgt, idx, src, axis=0):
    return tgt.at[idx].add(src)

def _segment_sum(src, seg, n):
    return jax.ops.segment_sum(src, seg, n)
kernel_name = 'mk_seq_postln_d2_jaxref_r4_cc34db'

def setup_inputs(seed: int=0):
    np.random.seed(seed)
    _w = jnp.asarray

    def _L0_attn_setup():
        import jax, jax.numpy as jnp
        import numpy as np
        B, L, D, H = (2, 1024, 512, 16)
        K = D // H
        V = D // H
        EPS = 1e-05

        def _gla_recurrence(q, k, v, g):
            qs = jnp.moveaxis(q, 1, 0)
            ks = jnp.moveaxis(k, 1, 0)
            vs = jnp.moveaxis(v, 1, 0)
            gs = jnp.moveaxis(g, 1, 0)

            def step(S, inp):
                qt, kt, vt, gt = inp
                S = S * jnp.exp(gt)[..., None] + kt[..., None] * vt[..., None, :]
                yt = jnp.einsum('bhk,bhkv->bhv', qt, S)
                return (S, yt)
            S0 = jnp.zeros((q.shape[0], H, K, V), q.dtype)
            S_final, ys = jax.lax.scan(step, S0, (qs, ks, vs, gs))
            return (jnp.moveaxis(ys, 0, 1), S_final)

        def _layernorm(x, gamma, beta):
            mu = jnp.mean(x, axis=-1, keepdims=True)
            var = jnp.mean(jnp.square(x - mu), axis=-1, keepdims=True)
            return (x - mu) * jax.lax.rsqrt(var + EPS) * gamma + beta

        def _reference_tuple_inner(x, Wq, Wk, Wv, Wg, Wo, gamma, beta):
            b, l, d = x.shape
            q = (x @ Wq.T).reshape(b, l, H, K) * K ** (-0.5)
            k = (x @ Wk.T).reshape(b, l, H, K)
            v = (x @ Wv.T).reshape(b, l, H, V)
            g = jax.nn.log_sigmoid(x @ Wg.T).reshape(b, l, H, K)
            y, final_state = _gla_recurrence(q, k, v, g)
            y = y.reshape(b, l, d)
            o = _layernorm(y, gamma, beta) @ Wo.T
            return (o, final_state)
        key = jax.random.key(seed)
        ks = jax.random.split(key, 7)
        s = D ** (-0.5)
        return {'x': jax.random.normal(ks[0], (B, L, D), jnp.float32), 'Wq': jax.random.normal(ks[1], (D, D), jnp.float32) * s, 'Wk': jax.random.normal(ks[2], (D, D), jnp.float32) * s, 'Wv': jax.random.normal(ks[3], (D, D), jnp.float32) * s, 'Wg': jax.random.normal(ks[4], (D, D), jnp.float32) * s, 'Wo': jax.random.normal(ks[5], (D, D), jnp.float32) * s, 'gamma': jnp.ones((D,), jnp.float32), 'beta': jnp.zeros((D,), jnp.float32)}
    _L0_attn_in = _L0_attn_setup()

    def _L0_ffn_setup():
        import jax, jax.numpy as jnp
        import numpy as np
        B, S, D_IN, D_OUT, E, R = (4, 512, 512, 512, 8, 16)
        SCALING = 32.0 / 16.0
        key = jax.random.key(seed)
        ks = jax.random.split(key, 7)
        return {'x': jax.random.normal(ks[0], (B, S, D_IN), jnp.float32), 'base_w': jax.random.normal(ks[1], (D_OUT, D_IN), jnp.float32) * 0.02, 'base_b': jax.random.normal(ks[2], (D_OUT,), jnp.float32) * 0.02, 'router_w': jax.random.normal(ks[3], (E, D_IN), jnp.float32) * 0.02, 'router_b': jax.random.normal(ks[4], (E,), jnp.float32) * 0.02, 'lora_A': jax.random.normal(ks[5], (E, D_IN, R), jnp.float32) * 0.02, 'lora_B': jax.random.normal(ks[6], (E, R, D_OUT), jnp.float32) * 0.02}
    _L0_ffn_in = _L0_ffn_setup()

    def _L1_attn_setup():
        import jax, jax.numpy as jnp
        import numpy as np
        EPS = 1e-06
        CHUNK = 16

        def _ln(x, g, b):
            mu = jnp.mean(x, -1, keepdims=True)
            var = jnp.var(x, -1, keepdims=True)
            xhat = (x - mu) * jax.lax.rsqrt(var + EPS)
            return g * xhat + b

        def chunk_ttt_linear(q, k, v, w, b, eta, scale=1.0):
            B, T, H, D = q.shape
            NC = T // CHUNK
            q = q * scale
            qc = q.reshape(B, NC, CHUNK, H, D).swapaxes(0, 1)
            kc = k.reshape(B, NC, CHUNK, H, D).swapaxes(0, 1)
            vc = v.reshape(B, NC, CHUNK, H, D).swapaxes(0, 1)
            ec = eta.reshape(B, NC, CHUNK, H).swapaxes(0, 1)
            tri = jnp.tril(jnp.ones((CHUNK, CHUNK), bool))
            S0 = jnp.zeros((B, H, D, D), q.dtype)

            def step(S, inp):
                qi, ki, vi, ei = inp
                kh = jnp.einsum('bchd,bhde->bche', ki, S)
                target = vi - ki
                mu = jnp.mean(kh, -1, keepdims=True)
                rstd = jax.lax.rsqrt(jnp.var(kh, -1, keepdims=True) + EPS)
                kh_hat = (kh - mu) * rstd
                g = w * kh_hat + b - target
                gw = g * w
                v_new = (gw - jnp.mean(gw, -1, keepdims=True) - kh_hat * jnp.mean(gw * kh_hat, -1, keepdims=True)) * rstd
                A = jnp.einsum('bchd,bshd->bhcs', qi, ki)
                A = jnp.where(tri, A, 0.0) * jnp.transpose(ei, (0, 2, 1))[:, :, None, :]
                qh = jnp.einsum('bchd,bhde->bche', qi, S) - jnp.einsum('bhcs,bshe->bche', A, v_new)
                o = qi + _ln(qh, w, b)
                S = S - jnp.einsum('bchd,bche->bhde', ki * ei[..., None], v_new)
                return (S, o)
            S_fin, o = jax.lax.scan(step, S0, (qc, kc, vc, ec))
            o = o.swapaxes(0, 1).reshape(B, T, H, D)
            return (o, S_fin)
        key = jax.random.key(seed)
        ks = jax.random.split(key, 11)
        B, T, D, H = (2, 1024, 512, 16)
        Dh = D // H
        std = 0.02
        x = jax.random.normal(ks[0], (B, T, D), jnp.float32)
        Wq = jax.random.normal(ks[1], (D, D), jnp.float32) * std
        Wk = jax.random.normal(ks[2], (D, D), jnp.float32) * std
        Wv = jax.random.normal(ks[3], (D, D), jnp.float32) * std
        Wo = jax.random.normal(ks[4], (D, D), jnp.float32) * std
        Wbeta = jax.random.normal(ks[5], (D, H), jnp.float32) * std
        ln_w = 1.0 + jax.random.normal(ks[6], (H, Dh), jnp.float32) * std
        ln_b = jax.random.normal(ks[7], (H, Dh), jnp.float32) * std
        Wg1 = jax.random.normal(ks[8], (D, Dh), jnp.float32) * std
        Wg2 = jax.random.normal(ks[9], (Dh, D), jnp.float32) * std
        norm_w = 1.0 + jax.random.normal(ks[10], (D,), jnp.float32) * std
        return dict(x=x, Wq=Wq, Wk=Wk, Wv=Wv, Wo=Wo, Wbeta=Wbeta, ln_w=ln_w, ln_b=ln_b, Wg1=Wg1, Wg2=Wg2, norm_w=norm_w)
    _L1_attn_in = _L1_attn_setup()

    def _L1_ffn_setup():
        import jax, jax.numpy as jnp
        import numpy as np
        H = 512
        I = 352
        E = 16
        G = 4
        TOPK_GROUP = 2
        TOP_K = 6
        N_SHARED = 2
        SCALE_FACTOR = 2.5
        B, S = (2, 512)

        def _gate(hs_flat, gate_weight, bias):
            T = hs_flat.shape[0]
            logits = hs_flat @ gate_weight.T
            scores = jax.nn.sigmoid(logits)
            scores_for_choice = scores + bias[None, :]
            gs = scores_for_choice.reshape(T, G, E // G)
            group_scores = jnp.sum(jax.lax.top_k(gs, 2)[0], axis=-1)
            _, group_idx = jax.lax.top_k(group_scores, TOPK_GROUP)
            group_mask = jnp.zeros((T, G), scores.dtype).at[jnp.arange(T)[:, None], group_idx].set(1.0)
            score_mask = jnp.repeat(group_mask, E // G, axis=1)
            tmp_scores = jnp.where(score_mask > 0, scores_for_choice, 0.0)
            _, topk_idx = jax.lax.top_k(tmp_scores, TOP_K)
            topk_weight = jnp.take_along_axis(scores, topk_idx, axis=1)
            topk_weight = topk_weight / (jnp.sum(topk_weight, axis=-1, keepdims=True) + 1e-20)
            topk_weight = topk_weight * SCALE_FACTOR
            return (topk_idx, topk_weight)
        key = jax.random.key(seed)
        ks = jax.random.split(key, 8)
        scale = 0.01
        SI = I * N_SHARED
        return {'hidden_states': jax.random.normal(ks[0], (B, S, H), jnp.float32), 'gate_weight': jax.random.uniform(ks[1], (E, H), jnp.float32, -0.05, 0.05), 'e_score_correction_bias': jnp.zeros((E,), jnp.float32), 'gate_proj': jax.random.normal(ks[2], (E, I, H), jnp.float32) * scale, 'up_proj': jax.random.normal(ks[3], (E, I, H), jnp.float32) * scale, 'down_proj': jax.random.normal(ks[4], (E, H, I), jnp.float32) * scale, 'shared_gate_w': jax.random.normal(ks[5], (SI, H), jnp.float32) * scale, 'shared_up_w': jax.random.normal(ks[6], (SI, H), jnp.float32) * scale, 'shared_down_w': jax.random.normal(ks[7], (H, SI), jnp.float32) * scale}
    _L1_ffn_in = _L1_ffn_setup()
    _d = {'L0_attn_x': _L0_attn_in['x'], 'L0_attn_Wq': _L0_attn_in['Wq'], 'L0_attn_Wk': _L0_attn_in['Wk'], 'L0_attn_Wv': _L0_attn_in['Wv'], 'L0_attn_Wg': _L0_attn_in['Wg'], 'L0_attn_Wo': _L0_attn_in['Wo'], 'L0_attn_gamma': _L0_attn_in['gamma'], 'L0_attn_beta': _L0_attn_in['beta'], 'L0_ffn_base_w': _L0_ffn_in['base_w'], 'L0_ffn_base_b': _L0_ffn_in['base_b'], 'L0_ffn_router_w': _L0_ffn_in['router_w'], 'L0_ffn_router_b': _L0_ffn_in['router_b'], 'L0_ffn_lora_A': _L0_ffn_in['lora_A'], 'L0_ffn_lora_B': _L0_ffn_in['lora_B'], 'L1_attn_Wq': _L1_attn_in['Wq'], 'L1_attn_Wk': _L1_attn_in['Wk'], 'L1_attn_Wv': _L1_attn_in['Wv'], 'L1_attn_Wo': _L1_attn_in['Wo'], 'L1_attn_Wbeta': _L1_attn_in['Wbeta'], 'L1_attn_ln_w': _L1_attn_in['ln_w'], 'L1_attn_ln_b': _L1_attn_in['ln_b'], 'L1_attn_Wg1': _L1_attn_in['Wg1'], 'L1_attn_Wg2': _L1_attn_in['Wg2'], 'L1_attn_norm_w': _L1_attn_in['norm_w'], 'L1_ffn_gate_weight': _L1_ffn_in['gate_weight'], 'L1_ffn_e_score_correction_bias': _L1_ffn_in['e_score_correction_bias'], 'L1_ffn_gate_proj': _L1_ffn_in['gate_proj'], 'L1_ffn_up_proj': _L1_ffn_in['up_proj'], 'L1_ffn_down_proj': _L1_ffn_in['down_proj'], 'L1_ffn_shared_gate_w': _L1_ffn_in['shared_gate_w'], 'L1_ffn_shared_up_w': _L1_ffn_in['shared_up_w'], 'L1_ffn_shared_down_w': _L1_ffn_in['shared_down_w']}
    _x0 = _d['L0_attn_x']
    _d['L0_attn_x'] = jax.random.normal(jax.random.fold_in(jax.random.key(seed), 1), (2, 1024, 512), dtype=_x0.dtype)
    del _x0
    return _d

def reference(L0_attn_x, L0_attn_Wq, L0_attn_Wk, L0_attn_Wv, L0_attn_Wg, L0_attn_Wo, L0_attn_gamma, L0_attn_beta, L0_ffn_base_w, L0_ffn_base_b, L0_ffn_router_w, L0_ffn_router_b, L0_ffn_lora_A, L0_ffn_lora_B, L1_attn_Wq, L1_attn_Wk, L1_attn_Wv, L1_attn_Wo, L1_attn_Wbeta, L1_attn_ln_w, L1_attn_ln_b, L1_attn_Wg1, L1_attn_Wg2, L1_attn_norm_w, L1_ffn_gate_weight, L1_ffn_e_score_correction_bias, L1_ffn_gate_proj, L1_ffn_up_proj, L1_ffn_down_proj, L1_ffn_shared_gate_w, L1_ffn_shared_up_w, L1_ffn_shared_down_w):

    def _L0_attn_ref(x, Wq, Wk, Wv, Wg, Wo, gamma, beta):
        import jax, jax.numpy as jnp
        import numpy as np
        B, L, D, H = (2, 1024, 512, 16)
        K = D // H
        V = D // H
        EPS = 1e-05

        def _gla_recurrence(q, k, v, g):
            qs = jnp.moveaxis(q, 1, 0)
            ks = jnp.moveaxis(k, 1, 0)
            vs = jnp.moveaxis(v, 1, 0)
            gs = jnp.moveaxis(g, 1, 0)

            def step(S, inp):
                qt, kt, vt, gt = inp
                S = S * jnp.exp(gt)[..., None] + kt[..., None] * vt[..., None, :]
                yt = jnp.einsum('bhk,bhkv->bhv', qt, S)
                return (S, yt)
            S0 = jnp.zeros((q.shape[0], H, K, V), q.dtype)
            S_final, ys = jax.lax.scan(step, S0, (qs, ks, vs, gs))
            return (jnp.moveaxis(ys, 0, 1), S_final)

        def _layernorm(x, gamma, beta):
            mu = jnp.mean(x, axis=-1, keepdims=True)
            var = jnp.mean(jnp.square(x - mu), axis=-1, keepdims=True)
            return (x - mu) * jax.lax.rsqrt(var + EPS) * gamma + beta

        def _reference_tuple_inner(x, Wq, Wk, Wv, Wg, Wo, gamma, beta):
            b, l, d = x.shape
            q = (x @ Wq.T).reshape(b, l, H, K) * K ** (-0.5)
            k = (x @ Wk.T).reshape(b, l, H, K)
            v = (x @ Wv.T).reshape(b, l, H, V)
            g = jax.nn.log_sigmoid(x @ Wg.T).reshape(b, l, H, K)
            y, final_state = _gla_recurrence(q, k, v, g)
            y = y.reshape(b, l, d)
            o = _layernorm(y, gamma, beta) @ Wo.T
            return (o, final_state)
        return _reference_tuple_inner(x, Wq, Wk, Wv, Wg, Wo, gamma, beta)[0]

    def _L0_ffn_ref(x, base_w, base_b, router_w, router_b, lora_A, lora_B):
        import jax, jax.numpy as jnp
        import numpy as np
        B, S, D_IN, D_OUT, E, R = (4, 512, 512, 512, 8, 16)
        SCALING = 32.0 / 16.0
        b, s, d_in = x.shape
        n = b * s
        e = lora_A.shape[0]
        d_out = lora_B.shape[-1]
        result = jnp.einsum('bsd,od->bso', x, base_w) + base_b
        logits = jnp.einsum('bsd,ed->bse', x, router_w) + router_b
        probs = jax.nn.softmax(logits.astype(jnp.float32), axis=-1)
        top_vals, top_idx = jax.lax.top_k(probs, 2)
        top_vals = top_vals / jnp.sum(top_vals, axis=-1, keepdims=True)
        top_vals = top_vals.astype(x.dtype)
        flat_idx = top_idx.reshape(n, 2)
        flat_val = top_vals.reshape(n, 2)
        gate = jnp.zeros((n, e), x.dtype).at[jnp.arange(n)[:, None], flat_idx].set(flat_val)
        xf = x.reshape(n, d_in)
        mid = jnp.einsum('nd,edr->ner', xf, lora_A)
        mid = mid * gate[:, :, None]
        lora_out = jnp.einsum('ner,erd->nd', mid, lora_B)
        return result + SCALING * lora_out.reshape(b, s, d_out)

    def _L1_attn_ref(x, Wq, Wk, Wv, Wo, Wbeta, ln_w, ln_b, Wg1, Wg2, norm_w):
        import jax, jax.numpy as jnp
        import numpy as np
        EPS = 1e-06
        CHUNK = 16

        def _ln(x, g, b):
            mu = jnp.mean(x, -1, keepdims=True)
            var = jnp.var(x, -1, keepdims=True)
            xhat = (x - mu) * jax.lax.rsqrt(var + EPS)
            return g * xhat + b

        def chunk_ttt_linear(q, k, v, w, b, eta, scale=1.0):
            B, T, H, D = q.shape
            NC = T // CHUNK
            q = q * scale
            qc = q.reshape(B, NC, CHUNK, H, D).swapaxes(0, 1)
            kc = k.reshape(B, NC, CHUNK, H, D).swapaxes(0, 1)
            vc = v.reshape(B, NC, CHUNK, H, D).swapaxes(0, 1)
            ec = eta.reshape(B, NC, CHUNK, H).swapaxes(0, 1)
            tri = jnp.tril(jnp.ones((CHUNK, CHUNK), bool))
            S0 = jnp.zeros((B, H, D, D), q.dtype)

            def step(S, inp):
                qi, ki, vi, ei = inp
                kh = jnp.einsum('bchd,bhde->bche', ki, S)
                target = vi - ki
                mu = jnp.mean(kh, -1, keepdims=True)
                rstd = jax.lax.rsqrt(jnp.var(kh, -1, keepdims=True) + EPS)
                kh_hat = (kh - mu) * rstd
                g = w * kh_hat + b - target
                gw = g * w
                v_new = (gw - jnp.mean(gw, -1, keepdims=True) - kh_hat * jnp.mean(gw * kh_hat, -1, keepdims=True)) * rstd
                A = jnp.einsum('bchd,bshd->bhcs', qi, ki)
                A = jnp.where(tri, A, 0.0) * jnp.transpose(ei, (0, 2, 1))[:, :, None, :]
                qh = jnp.einsum('bchd,bhde->bche', qi, S) - jnp.einsum('bhcs,bshe->bche', A, v_new)
                o = qi + _ln(qh, w, b)
                S = S - jnp.einsum('bchd,bche->bhde', ki * ei[..., None], v_new)
                return (S, o)
            S_fin, o = jax.lax.scan(step, S0, (qc, kc, vc, ec))
            o = o.swapaxes(0, 1).reshape(B, T, H, D)
            return (o, S_fin)
        B, T, D = x.shape
        H, Dh = ln_w.shape
        q = jax.nn.silu(x @ Wq).reshape(B, T, H, Dh)
        k = (x @ Wk).reshape(B, T, H, Dh)
        k = k * jax.lax.rsqrt(jnp.sum(k * k, -1, keepdims=True) + EPS)
        v = (x @ Wv).reshape(B, T, H, Dh)
        beta = jax.nn.sigmoid(x @ Wbeta) * 2.0
        o, _ = chunk_ttt_linear(q, k, v, ln_w, ln_b, beta, 1.0)
        gate = x @ Wg1 @ Wg2
        og = o * jax.nn.sigmoid(gate.reshape(B, T, H, Dh))
        og = og * jax.lax.rsqrt(jnp.mean(og * og, -1, keepdims=True) + EPS)
        o = og.reshape(B, T, D) * norm_w
        return o @ Wo

    def _L1_ffn_ref(hidden_states, gate_weight, e_score_correction_bias, gate_proj, up_proj, down_proj, shared_gate_w, shared_up_w, shared_down_w):
        import jax, jax.numpy as jnp
        import numpy as np
        H = 512
        I = 352
        E = 16
        G = 4
        TOPK_GROUP = 2
        TOP_K = 6
        N_SHARED = 2
        SCALE_FACTOR = 2.5
        B, S = (2, 512)

        def _gate(hs_flat, gate_weight, bias):
            T = hs_flat.shape[0]
            logits = hs_flat @ gate_weight.T
            scores = jax.nn.sigmoid(logits)
            scores_for_choice = scores + bias[None, :]
            gs = scores_for_choice.reshape(T, G, E // G)
            group_scores = jnp.sum(jax.lax.top_k(gs, 2)[0], axis=-1)
            _, group_idx = jax.lax.top_k(group_scores, TOPK_GROUP)
            group_mask = jnp.zeros((T, G), scores.dtype).at[jnp.arange(T)[:, None], group_idx].set(1.0)
            score_mask = jnp.repeat(group_mask, E // G, axis=1)
            tmp_scores = jnp.where(score_mask > 0, scores_for_choice, 0.0)
            _, topk_idx = jax.lax.top_k(tmp_scores, TOP_K)
            topk_weight = jnp.take_along_axis(scores, topk_idx, axis=1)
            topk_weight = topk_weight / (jnp.sum(topk_weight, axis=-1, keepdims=True) + 1e-20)
            topk_weight = topk_weight * SCALE_FACTOR
            return (topk_idx, topk_weight)
        b, s, h = hidden_states.shape
        hs = hidden_states.reshape(-1, h)
        T = hs.shape[0]
        topk_idx, topk_weight = _gate(hs, gate_weight, e_score_correction_bias)
        comb = jnp.zeros((T, E), hs.dtype).at[jnp.arange(T)[:, None], topk_idx].add(topk_weight)
        out = jnp.zeros_like(hs)
        for e in range(E):
            g = hs @ gate_proj[e].T
            u = hs @ up_proj[e].T
            inter = jax.nn.silu(g) * u
            out = out + comb[:, e:e + 1] * (inter @ down_proj[e].T)
        y = out.reshape(b, s, h)
        sg = hidden_states @ shared_gate_w.T
        su = hidden_states @ shared_up_w.T
        shared_out = jax.nn.silu(sg) * su @ shared_down_w.T
        return y + shared_out
    x = L0_attn_x
    x = _layernorm(x + _L0_attn_ref(x, L0_attn_Wq, L0_attn_Wk, L0_attn_Wv, L0_attn_Wg, L0_attn_Wo, L0_attn_gamma, L0_attn_beta), axis=-1)
    x = _layernorm(x + _L0_ffn_ref(x, L0_ffn_base_w, L0_ffn_base_b, L0_ffn_router_w, L0_ffn_router_b, L0_ffn_lora_A, L0_ffn_lora_B), axis=-1)
    x = _layernorm(x + _L1_attn_ref(x, L1_attn_Wq, L1_attn_Wk, L1_attn_Wv, L1_attn_Wo, L1_attn_Wbeta, L1_attn_ln_w, L1_attn_ln_b, L1_attn_Wg1, L1_attn_Wg2, L1_attn_norm_w), axis=-1)
    x = _layernorm(x + _L1_ffn_ref(x, L1_ffn_gate_weight, L1_ffn_e_score_correction_bias, L1_ffn_gate_proj, L1_ffn_up_proj, L1_ffn_down_proj, L1_ffn_shared_gate_w, L1_ffn_shared_up_w, L1_ffn_shared_down_w), axis=-1)
    return x

_drawn_inputs = setup_inputs


def setup_inputs(seed=0):
    import zlib

    import numpy as np

    out = dict(_drawn_inputs(seed))
    spreads = {'L0_attn_gamma': (1.0, 0.2),
     'L0_attn_beta': (0.0, 0.1),
     'L1_ffn_e_score_correction_bias': (0.0, 0.8)}
    factors = {'L0_ffn_base_b': 2.726,
     'L0_ffn_router_b': 5.115,
     'L1_attn_ln_w': 3.519,
     'L1_attn_ln_b': 3.208,
     'L1_attn_Wg1': 5.589,
     'L1_attn_Wg2': 5.594,
     'L1_attn_norm_w': 6.502,
     'L1_ffn_gate_weight': 8.0,
     'L1_ffn_gate_proj': 8.0,
     'L1_ffn_up_proj': 8.0,
     'L1_ffn_down_proj': 8.0,
     'L1_ffn_shared_gate_w': 8.0,
     'L1_ffn_shared_up_w': 8.0,
     'L1_ffn_shared_down_w': 8.0}
    for name, (base, spread) in spreads.items():
        noise = np.random.default_rng([zlib.crc32(name.encode()), seed]).standard_normal(out[name].shape)
        drawn = base * np.exp(spread * noise) if base else spread * noise
        out[name] = jnp.asarray(drawn.astype(out[name].dtype))
    for name, factor in factors.items():
        out[name] = (out[name] * factor).astype(out[name].dtype)
    return out
```

```python
from contextlib import ExitStack

import numpy as np
import concourse.bass as bass
from concourse import mybir

ALU = mybir.AluOpType
ACT = mybir.ActivationFunctionType
F32 = mybir.dt.float32
F32R = mybir.dt.float32r
U32 = mybir.dt.uint32
AX = mybir.AxisListType.X

P = 128
B, L, D, H = 2, 1024, 512, 16
DH = D // H
KC = D // P
NT = L // P
HG = P // DH
SUB = 32
NSUB = P // SUB
EXPERTS, RANK = 8, 16
TTT = 16
NCH = P // TTT
MOE_E, MOE_I, MOE_G = 16, 352, 4
ICH = [(0, 128), (128, 128), (256, 96)]


class Counter:

    def __init__(self, nc, name, per):
        self.sem, self.per = nc.alloc_semaphore(name=name), per

    def now(self, i):
        return i * self.per + self.per

    def last(self, i):
        return i * self.per

    def part(self, i, k):
        return i * self.per + k


class Phase:

    def __init__(self, nc, name):
        self.nc, self.name, self.counters, self.stack = nc, name, [], ExitStack()

    def counter(self, name, per=1):
        s = Counter(self.nc, f"{self.name}_{name}", per)
        self.counters.append(s)
        return s

    def counters_of_two(self, name, per=1):
        return [self.counter(f"{name}{b}", per) for b in range(2)]

    def sb(self, name, shape, dt=F32):
        return self.stack.enter_context(self.nc.sbuf_tensor(f"{self.name}_{name}", shape, dt))

    def sb2(self, name, shape, dt=F32):
        return [self.sb(f"{name}{b}", shape, dt) for b in range(2)]

    def credit(self, eng):
        for s in self.counters:
            eng.sem_inc(s.sem, s.per)

    def end(self):
        self.nc.clear_and_free_semaphores([s.sem for s in self.counters])
        self.nc.all_engine_barrier()
        self.stack.close()


def exact3(pe, out, hi, lo, whi, wlo, start=True, stop=True, n=KC):
    for c in range(n):
        pe.matmul(out, hi(c), whi(c), start=start and c == 0, stop=False, skip_group_check=True)
        pe.matmul(out, lo(c), whi(c), start=False, stop=False, skip_group_check=True)
        last = pe.matmul(out, hi(c), wlo(c), start=False, stop=stop and c == n - 1, skip_group_check=True)
    return last


def load_split(nc, name, parts, stage_cols=D * KC):
    stack = ExitStack()
    stage = [stack.enter_context(nc.sbuf_tensor(f"{name}_stage{k}", [P, stage_cols], F32)) for k in range(2)]
    landed = [nc.alloc_semaphore(name=f"{name}_landed{k}") for k in range(2)]
    leading = nc.alloc_semaphore(name=f"{name}_leading")
    trailing = nc.alloc_semaphore(name=f"{name}_trailing")

    def view(n, src, like):
        v = stage[n % 2][0:src.shape[0], 0:src.shape[1]]
        return v.rearrange("p (c t) -> p c t", c=like.shape[1]) if len(like.shape) == 3 else v

    with nc.Block() as block:
        @block.sync
        def _(sp):
            for n, (src, hi, lo) in enumerate(parts):
                if n >= 2:
                    sp.wait_ge(trailing, n - 1)
                sp.dma_start(stage[n % 2][0:src.shape[0], 0:src.shape[1]], src).then_inc(landed[n % 2], 16)

        @block.scalar
        def _(act):
            for n, (src, hi, lo) in enumerate(parts):
                act.wait_ge(landed[n % 2], 16 * (n // 2 + 1))
                nc.scalar.copy(hi, view(n, src, hi)).then_inc(leading, 1)

        @block.vector
        def _(dve):
            for n, (src, hi, lo) in enumerate(parts):
                dve.wait_ge(leading, n + 1)
                dve.wait_ge(landed[n % 2], 16 * (n // 2 + 1))
                nc.vector.tensor_tensor(lo, view(n, src, hi), hi.bitcast(F32),
                                        ALU.subtract).then_inc(trailing, 1)
            dve.wait_ge(trailing, len(parts))
    nc.clear_and_free_semaphores([*landed, leading, trailing])
    nc.all_engine_barrier()
    stack.close()


class Norm:

    def __init__(self, ph, name, b, eps):
        self.eps = eps
        self.st = ph.sb(f"{name}_st{b}", [P, 6])
        self.mv = ph.sb(f"{name}_mv{b}", [P, 2])
        self.w = ph.sb(f"{name}_w{b}", [P, 5])
        self.stat, self.mean, self.var, self.log, self.guess, self.n1, self.n2, self.rstd = (
            ph.counter(f"{name}_{n}{b}") for n in ("stat", "mean", "var", "log", "guess", "n1", "n2", "rstd"))

    def stats(self, nc, dve, i, src):
        nc.vector.bn_stats(self.st[:], src).then_inc(self.stat.sem, 1)
        dve.wait_ge(self.stat.sem, self.stat.now(i))
        nc.vector.memset(self.w[:, 0:1], 0.0)
        nc.vector.bn_aggr(self.mv[:], self.st[:]).then_inc(self.mean.sem, 1)
        dve.wait_ge(self.mean.sem, self.mean.now(i))
        nc.vector.tensor_scalar(self.w[:, 0:1], self.mv[:, 1:2], self.eps, None, ALU.add).then_inc(self.var.sem, 1)

    def guesses(self, nc, act, i):
        act.wait_ge(self.var.sem, self.var.now(i))
        nc.scalar.activation(self.w[:, 1:2], self.w[:, 0:1], ACT.Ln).then_inc(self.log.sem, 1)
        act.wait_ge(self.log.sem, self.log.now(i))
        nc.scalar.activation(self.w[:, 2:3], self.w[:, 1:2], ACT.Exp, scale=-0.5).then_inc(self.guess.sem, 1)

    def newton(self, nc, dve, i):
        dve.wait_ge(self.guess.sem, self.guess.now(i))
        nc.vector.scalar_tensor_tensor(self.w[:, 3:4], self.w[:, 2:3], self.w[:, 0:1], self.w[:, 2:3],
                                       ALU.mult, ALU.mult).then_inc(self.n1.sem, 1)
        dve.wait_ge(self.n1.sem, self.n1.now(i))
        nc.vector.tensor_scalar(self.w[:, 3:4], self.w[:, 3:4], -0.5, 1.5, ALU.mult, ALU.add).then_inc(self.n2.sem, 1)
        dve.wait_ge(self.n2.sem, self.n2.now(i))
        nc.vector.tensor_tensor(self.w[:, 4:5], self.w[:, 3:4], self.w[:, 2:3], ALU.mult).then_inc(self.rstd.sem, 1)
        dve.wait_ge(self.rstd.sem, self.rstd.now(i))

    def apply(self, nc, out, src):
        return nc.vector.tensor_scalar(out, src, self.mv[:, 0:1], self.w[:, 4:5], ALU.subtract, ALU.mult)


def gated_recurrence(nc, K, bank, a):
    top = ExitStack()
    names = ["Wg", "Wv", "Wq", "Wk", "Wo"]
    wh = {n: top.enter_context(nc.sbuf_tensor(f"gla_{n}_hi", [P, KC, D], F32R)) for n in names}
    wl = {n: top.enter_context(nc.sbuf_tensor(f"gla_{n}_lo", [P, KC, D], F32R)) for n in names}
    load_split(nc, "gla_w", [(a[n], wh[n][:].rearrange("p c n -> p (c n)"), wl[n][:].rearrange("p c n -> p (c n)"))
                             for n in names])
    ph = Phase(nc, "gla")
    PJ, BK = bank[0:4], bank[4:8]
    ident = ph.sb("ident", [P, P])
    cum = ph.sb("cum", [P, P])
    sel = ph.sb("sel", [P, NSUB + 1])
    causal = ph.sb("causal", [P, P])
    heads = ph.sb("heads", [P, P])
    gamma = ph.sb("gamma", [P, KC])
    beta = ph.sb("beta", [P, KC])
    xT, xTh, xTl = ph.sb2("xT", [P, KC, P]), ph.sb2("xTh", [P, KC, P], F32R), ph.sb2("xTl", [P, KC, P], F32R)
    xt, az, g = ph.sb2("xt", [P, D]), ph.sb2("az", [P, D]), ph.sb2("g", [P, D])
    eR, enR = ph.sb2("eR", [P, D]), ph.sb2("enR", [P, D])
    Qr, Kr, V = ph.sb2("Qr", [P, D]), ph.sb2("Kr", [P, D]), ph.sb2("V", [P, D])
    QT, KT = ph.sb2("QT", [P, KC, P]), ph.sb2("KT", [P, KC, P])
    Am = ph.sb2("Am", [P, HG, KC, P])
    kvm = ph.sb2("kvm", [P, KC, P])
    Sh = ph.sb2("Sh", [P, NSUB, KC, P])
    carry = ph.sb2("carry", [P, KC, P])
    decay = ph.sb2("decay", [P, KC, NSUB + 1])
    yTh, yTl = ph.sb2("yTh", [P, KC, P], F32R), ph.sb2("yTl", [P, KC, P], F32R)

    s = {}
    for n, per in [("xT_in", 16), ("xt_in", 16), ("xh", 1), ("xl", 1), ("z", 1), ("v", 1), ("q", 1), ("k", 1),
                   ("az", 1), ("ez", 1), ("lz", 1), ("g", 1), ("R", 1), ("eR", 1), ("enR", 1), ("decay", 1),
                   ("V", 1), ("Qr", 1), ("Kr", 1), ("QTp", 1), ("KTp", 1), ("QT", 1), ("KT", 1),
                   ("kv", NSUB), ("kvm", NSUB), ("sum", NSUB), ("Sh", NSUB + 1), ("A", HG), ("Am", HG),
                   ("y", 1), ("yn", 1), ("yTp", 1), ("yT", 1), ("yTh", 1), ("yTl", 1), ("o", 1), ("r", 1),
                   ("x1", 1), ("x1_out", 16)]:
        s[n] = ph.counters_of_two(n, per)
    n1 = [Norm(ph, "ny", b, 1e-5) for b in range(2)]
    n2 = [Norm(ph, "nx", b, 1e-5) for b in range(2)]
    consts = ph.counter("consts", 16 * 7)
    zeroed = ph.counter("zeroed", 2)

    def x1_rows(i, b):
        return a["x1"][bass.ds((i * 2 + (b - 2)) * P, P), :]

    with nc.Block() as block:
        @block.sync
        def _(sp):
            for t, src in ((ident, K["ident"]), (cum, K["cum"]), (sel, K["sel"]), (causal, K["causal"]),
                           (heads, K["heads"]), (gamma, a["gamma"]), (beta, a["beta"])):
                sp.dma_start(t[:], src).then_inc(consts.sem, 16)
            with sp.Fori(1, NT + 1) as i:
                for b in range(2):
                    sp.wait_ge(s["xh"][b].sem, s["xh"][b].last(i))
                    sp.wait_ge(s["xl"][b].sem, s["xl"][b].last(i))
                    row = (i * 2 + (b - 2)) * P
                    sp.dma_start(xT[b][:].rearrange("p c t -> p (c t)"), a["xT"][bass.ds(row, P), :]).then_inc(s["xT_in"][b].sem, 16)
                    sp.wait_ge(s["r"][b].sem, s["r"][b].last(i))
                    sp.dma_start(xt[b][:], a["x"][bass.ds(row, P), :]).then_inc(s["xt_in"][b].sem, 16)
            for b in range(2):
                sp.wait_ge(s["x1_out"][b].sem, s["x1_out"][b].now(NT))

        @block.gpsimd
        def _(pool):
            ph.credit(pool)
            for b in range(2):
                nc.gpsimd.memset(carry[b][:], 0.0).then_inc(zeroed.sem, 1)
            pool.wait_ge(zeroed.sem, 4)
            with pool.Fori(1, NT + 1) as i:
                for b in range(2):
                    def scale(out, in_, c, k):
                        nc.gpsimd.tensor_tensor(out, in_, decay[b][:, :, c:c + 1].to_broadcast([P, KC, P]),
                                                ALU.mult).then_inc(s["Sh"][b].sem, 1)
                    pool.wait_ge(s["decay"][b].sem, s["decay"][b].now(i))
                    pool.wait_ge(s["y"][b].sem, s["y"][b].last(i))
                    pool.wait_ge(s["Sh"][b].sem, s["Sh"][b].last(i))
                    scale(Sh[b][:, 0], carry[b][:], 0, 0)
                    for c in range(NSUB):
                        pool.wait_ge(s["Sh"][b].sem, s["Sh"][b].part(i, c + 1))
                        pool.wait_ge(s["kvm"][b].sem, s["kvm"][b].part(i, c + 1))
                        nc.gpsimd.tensor_tensor(kvm[b][:], kvm[b][:], Sh[b][:, c], ALU.add).then_inc(s["sum"][b].sem, 1)
                        pool.wait_ge(s["sum"][b].sem, s["sum"][b].part(i, c + 1))
                        scale(Sh[b][:, c + 1] if c < NSUB - 1 else carry[b][:], kvm[b][:], c + 1, c + 1)

        @block.scalar
        def _(act):
            act.wait_ge(consts.sem, consts.now(1))
            nc.scalar.preload_act_table_set("natural_log_exp_and_others")
            with act.Fori(1, NT + 1) as i:
                def gates(b):
                    act.wait_ge(s["z"][b].sem, s["z"][b].now(i))
                    nc.scalar.activation(az[b][:], PJ[0][:], ACT.Abs).then_inc(s["az"][b].sem, 1)
                    act.wait_ge(s["az"][b].sem, s["az"][b].now(i))
                    nc.scalar.activation(az[b][:], az[b][:], ACT.Exp, scale=-1.0).then_inc(s["ez"][b].sem, 1)
                    act.wait_ge(s["ez"][b].sem, s["ez"][b].now(i))
                    nc.scalar.activation(az[b][:], az[b][:], ACT.Ln, bias=1.0).then_inc(s["lz"][b].sem, 1)
                    act.wait_ge(s["v"][b].sem, s["v"][b].now(i))
                    act.wait_ge(s["y"][b].sem, s["y"][b].last(i))
                    nc.scalar.copy(V[b][:], PJ[1][:]).then_inc(s["V"][b].sem, 1)

                def decays(b):
                    act.wait_ge(s["R"][b].sem, s["R"][b].now(i))
                    act.wait_ge(s["yTp"][b].sem, s["yTp"][b].last(i))
                    nc.scalar.activation(eR[b][:], BK[0][:], ACT.Exp).then_inc(s["eR"][b].sem, 1)
                    act.wait_ge(s["yTl"][b].sem, s["yTl"][b].last(i))
                    nc.scalar.activation(enR[b][:], BK[0][:], ACT.Exp, scale=-1.0).then_inc(s["enR"][b].sem, 1)
                    act.wait_ge(s["Sh"][b].sem, s["Sh"][b].part(i, 0))
                    nc.scalar.activation(decay[b][:].rearrange("p c n -> p (c n)"), BK[1][:, 0:KC * (NSUB + 1)],
                                         ACT.Exp).then_inc(s["decay"][b].sem, 1)

                def turned(b):
                    act.wait_ge(s["QTp"][b].sem, s["QTp"][b].now(i))
                    act.wait_ge(s["y"][b].sem, s["y"][b].last(i))
                    nc.scalar.copy(QT[b][:].rearrange("p c t -> p (c t)"), BK[2][:]).then_inc(s["QT"][b].sem, 1)
                    act.wait_ge(s["KTp"][b].sem, s["KTp"][b].now(i))
                    nc.scalar.copy(KT[b][:].rearrange("p c t -> p (c t)"), BK[3][:]).then_inc(s["KT"][b].sem, 1)

                def scaled(b):
                    act.wait_ge(s["yTp"][b].sem, s["yTp"][b].now(i))
                    for c in range(KC):
                        last = nc.scalar.activation(enR[b][:, c * P:(c + 1) * P], BK[(0, 3)[b]][:, c * P:(c + 1) * P],
                                                    ACT.Identity, scale=gamma[:, c:c + 1], bias=beta[:, c:c + 1])
                    last.then_inc(s["yT"][b].sem, 1)

                gates(0)
                decays(0)
                gates(1)
                turned(0)
                decays(1)
                turned(1)
                n1[0].guesses(nc, act, i)
                scaled(0)
                n1[1].guesses(nc, act, i)
                n2[0].guesses(nc, act, i)
                scaled(1)
                n2[1].guesses(nc, act, i)
                for b in range(2):
                    act.wait_ge(s["x1"][b].sem, s["x1"][b].now(i))
                    act.dma_start(x1_rows(i, b), g[b][:]).then_inc(s["x1_out"][b].sem, 16)

        @block.vector
        def _(dve):
            dve.wait_ge(consts.sem, consts.now(1))
            with dve.Fori(1, NT + 1) as i:
                def split_x(b):
                    dve.wait_ge(s["xT_in"][b].sem, s["xT_in"][b].now(i))
                    dve.wait_ge(s["k"][b].sem, s["k"][b].last(i))
                    nc.vector.tensor_copy(xTh[b][:], xT[b][:]).then_inc(s["xh"][b].sem, 1)
                    dve.wait_ge(s["xh"][b].sem, s["xh"][b].now(i))
                    nc.vector.tensor_tensor(xTl[b][:], xT[b][:], xTh[b][:].bitcast(F32), ALU.subtract).then_inc(s["xl"][b].sem, 1)

                def gate(b):
                    dve.wait_ge(s["lz"][b].sem, s["lz"][b].now(i))
                    dve.wait_ge(s["x1_out"][b].sem, s["x1_out"][b].last(i))
                    nc.vector.scalar_tensor_tensor(g[b][:], PJ[0][:], 0.0, az[b][:], ALU.min, ALU.subtract).then_inc(s["g"][b].sem, 1)

                def decayed(b):
                    dve.wait_ge(s["q"][b].sem, s["q"][b].now(i))
                    dve.wait_ge(s["eR"][b].sem, s["eR"][b].now(i))
                    nc.vector.scalar_tensor_tensor(Qr[b][:], PJ[2][:], float(DH) ** -0.5, eR[b][:], ALU.mult, ALU.mult).then_inc(s["Qr"][b].sem, 1)
                    dve.wait_ge(s["k"][b].sem, s["k"][b].now(i))
                    dve.wait_ge(s["enR"][b].sem, s["enR"][b].now(i))
                    nc.vector.tensor_tensor(Kr[b][:], PJ[3][:], enR[b][:], ALU.mult).then_inc(s["Kr"][b].sem, 1)

                def states(b):
                    for c in range(NSUB):
                        dve.wait_ge(s["kv"][b].sem, s["kv"][b].part(i, c + 1))
                        dve.wait_ge(s["Sh"][b].sem, s["Sh"][b].part(i, c + 1))
                        nc.vector.tensor_tensor(kvm[b][:], BK[2 + c % 2][:].rearrange("p (c n) -> p c n", c=KC),
                                                heads[:].unsqueeze(1).to_broadcast([P, KC, P]), ALU.mult).then_inc(s["kvm"][b].sem, 1)

                def masked(b, banks):
                    for j in range(HG):
                        dve.wait_ge(s["A"][b].sem, s["A"][b].part(i, j + 1))
                        nc.vector.tensor_tensor(Am[b][:, j], BK[banks[j]][:].rearrange("p (c n) -> p c n", c=KC),
                                                causal[:].unsqueeze(1).to_broadcast([P, KC, P]), ALU.mult).then_inc(s["Am"][b].sem, 1)

                def norm_y(b):
                    dve.wait_ge(s["y"][b].sem, s["y"][b].now(i))
                    n1[b].stats(nc, dve, i, BK[(0, 1)[b]][:])
                    n1[b].newton(nc, dve, i)
                    n1[b].apply(nc, eR[b][:], BK[(0, 1)[b]][:]).then_inc(s["yn"][b].sem, 1)

                def split_y(b):
                    dve.wait_ge(s["yT"][b].sem, s["yT"][b].now(i))
                    nc.vector.tensor_copy(yTh[b][:].rearrange("p c t -> p (c t)"), enR[b][:]).then_inc(s["yTh"][b].sem, 1)
                    dve.wait_ge(s["yTh"][b].sem, s["yTh"][b].now(i))
                    nc.vector.tensor_tensor(yTl[b][:].rearrange("p c t -> p (c t)"), enR[b][:],
                                            yTh[b][:].bitcast(F32).rearrange("p c t -> p (c t)"), ALU.subtract).then_inc(s["yTl"][b].sem, 1)

                def norm_x(b):
                    dve.wait_ge(s["o"][b].sem, s["o"][b].now(i))
                    dve.wait_ge(s["xt_in"][b].sem, s["xt_in"][b].now(i))
                    dve.wait_ge(s["KTp"][b].sem, s["KTp"][b].now(i))
                    nc.vector.tensor_tensor(Qr[b][:], BK[(2, 1)[b]][:], xt[b][:], ALU.add).then_inc(s["r"][b].sem, 1)
                    dve.wait_ge(s["r"][b].sem, s["r"][b].now(i))
                    n2[b].stats(nc, dve, i, Qr[b][:])
                    n2[b].newton(nc, dve, i)
                    n2[b].apply(nc, g[b][:], Qr[b][:]).then_inc(s["x1"][b].sem, 1)

                split_x(0)
                split_x(1)
                gate(0)
                decayed(0)
                gate(1)
                decayed(1)
                states(0)
                masked(0, (0, 1, 0, 1))
                states(1)
                norm_y(0)
                masked(1, (1, 2, 3, 1))
                split_y(0)
                norm_y(1)
                norm_x(0)
                split_y(1)
                norm_x(1)

        @block.tensor
        def _(pe):
            pe.wait_ge(consts.sem, consts.now(1))
            with pe.Fori(1, NT + 1) as i:
                def project(b, name, m, used):
                    pe.wait_ge(s[used][1 - b].sem, s[used][1 - b].now(i) if b else s[used][1 - b].last(i))
                    exact3(pe, PJ[m][:], lambda c: xTh[b][:, c, :], lambda c: xTl[b][:, c, :],
                           lambda c: wh[name][:, c, :], lambda c: wl[name][:, c, :]).then_inc(s[("z", "v", "q", "k")[m]][b].sem, 1)

                def projections(b):
                    pe.wait_ge(s["xl"][b].sem, s["xl"][b].now(i))
                    project(b, "Wg", 0, "g")
                    project(b, "Wv", 1, "V")
                    project(b, "Wq", 2, "Qr")
                    project(b, "Wk", 3, "Kr")

                def log_decays(b):
                    pe.wait_ge(s["g"][b].sem, s["g"][b].now(i))
                    if b == 0:
                        pe.wait_ge(s["yT"][0].sem, s["yT"][0].last(i))
                        pe.wait_ge(s["r"][1].sem, s["r"][1].last(i))
                    else:
                        pe.wait_ge(s["enR"][0].sem, s["enR"][0].now(i))
                        pe.wait_ge(s["decay"][0].sem, s["decay"][0].now(i))
                    pe.matmul(BK[0][:], cum[:], g[b][:], start=True, stop=True)
                    for c in range(KC):
                        last = pe.matmul(BK[1][:, c * (NSUB + 1):(c + 1) * (NSUB + 1)], g[b][:, c * P:(c + 1) * P], sel[:],
                                         start=True, stop=True, skip_group_check=True)
                    last.then_inc(s["R"][b].sem, 1)

                def turn(b):
                    pe.wait_ge(s["Qr"][b].sem, s["Qr"][b].now(i))
                    if b == 0:
                        pe.wait_ge(s["r"][0].sem, s["r"][0].last(i))
                        pe.wait_ge(s["yT"][1].sem, s["yT"][1].last(i))
                    else:
                        pe.wait_ge(s["kvm"][0].sem, s["kvm"][0].part(i, NSUB))
                    for c in range(KC):
                        last = pe.transpose(BK[2][:, c * P:(c + 1) * P], Qr[b][:, c * P:(c + 1) * P], ident[:])
                    last.then_inc(s["QTp"][b].sem, 1)
                    pe.wait_ge(s["Kr"][b].sem, s["Kr"][b].now(i))
                    for c in range(KC):
                        last = pe.transpose(BK[3][:, c * P:(c + 1) * P], Kr[b][:, c * P:(c + 1) * P], ident[:])
                    last.then_inc(s["KTp"][b].sem, 1)

                def key_values(b):
                    pe.wait_ge(s["V"][b].sem, s["V"][b].now(i))
                    pe.wait_ge(s["KT"][b].sem, s["KT"][b].now(i))
                    pe.wait_ge(s["QT"][b].sem, s["QT"][b].now(i))
                    for c in range(NSUB):
                        if c >= 2:
                            pe.wait_ge(s["kvm"][b].sem, s["kvm"][b].part(i, c - 1))
                        for m in range(KC):
                            last = pe.matmul(BK[2 + c % 2][:, m * P:(m + 1) * P],
                                             Kr[b][c * SUB:(c + 1) * SUB, m * P:(m + 1) * P],
                                             V[b][c * SUB:(c + 1) * SUB, m * P:(m + 1) * P], start=True, stop=True,
                                             skip_group_check=True)
                        last.then_inc(s["kv"][b].sem, 1)

                def scores(b, banks, free):
                    pe.wait_ge(s["KT"][b].sem, s["KT"][b].now(i))
                    for j in range(HG):
                        free(j)
                        for m in range(KC):
                            last = pe.matmul(BK[banks[j]][:, m * P:(m + 1) * P], KT[b][j * DH:(j + 1) * DH, m, :],
                                             QT[b][j * DH:(j + 1) * DH, m, :], start=True, stop=True, skip_group_check=True)
                        last.then_inc(s["A"][b].sem, 1)

                def free_0(j):
                    if j == 0:
                        pe.wait_ge(s["enR"][1].sem, s["enR"][1].now(i))
                    if j == 1:
                        pe.wait_ge(s["decay"][1].sem, s["decay"][1].now(i))
                    if j >= 2:
                        pe.wait_ge(s["Am"][0].sem, s["Am"][0].part(i, j - 1))

                def free_1(j):
                    if j == 0:
                        pe.wait_ge(s["Am"][0].sem, s["Am"][0].part(i, 4))
                    if j == 1:
                        pe.wait_ge(s["kvm"][1].sem, s["kvm"][1].part(i, 3))
                    if j == 2:
                        pe.wait_ge(s["kvm"][1].sem, s["kvm"][1].part(i, 4))
                    if j == 3:
                        pe.wait_ge(s["Am"][1].sem, s["Am"][1].part(i, 1))

                def outputs(b):
                    bk = BK[(0, 1)[b]]
                    pe.wait_ge(s["Am"][b].sem, s["Am"][b].part(i, HG))
                    for m in range(KC):
                        for j in range(HG):
                            h = m * HG + j
                            pe.matmul(bk[:, h * DH:(h + 1) * DH], Am[b][:, j, m, :], V[b][:, h * DH:(h + 1) * DH],
                                      start=(h == 0), stop=False, skip_group_check=True)
                    pe.wait_ge(s["Sh"][b].sem, s["Sh"][b].part(i, NSUB))
                    for c in range(NSUB):
                        for m in range(KC):
                            last = pe.matmul(bk[c * SUB:(c + 1) * SUB, m * P:(m + 1) * P],
                                             QT[b][:, m, c * SUB:(c + 1) * SUB], Sh[b][:, c, m, :],
                                             start=False, stop=(m == KC - 1), skip_group_check=True)
                    last.then_inc(s["y"][b].sem, 1)

                def turn_y(b):
                    pe.wait_ge(s["yn"][b].sem, s["yn"][b].now(i))
                    if b == 1:
                        pe.wait_ge(s["Am"][1].sem, s["Am"][1].part(i, 3))
                    for c in range(KC):
                        last = pe.transpose(BK[(0, 3)[b]][:, c * P:(c + 1) * P], eR[b][:, c * P:(c + 1) * P], ident[:])
                    last.then_inc(s["yTp"][b].sem, 1)

                def out_proj(b):
                    pe.wait_ge(s["yTl"][b].sem, s["yTl"][b].now(i))
                    if b == 0:
                        pe.wait_ge(s["Am"][1].sem, s["Am"][1].part(i, 2))
                    exact3(pe, BK[(2, 1)[b]][:], lambda c: yTh[b][:, c, :], lambda c: yTl[b][:, c, :],
                           lambda c: wh["Wo"][:, c, :], lambda c: wl["Wo"][:, c, :]).then_inc(s["o"][b].sem, 1)

                projections(0)
                log_decays(0)
                projections(1)
                turn(0)
                log_decays(1)
                key_values(0)
                scores(0, (0, 1, 0, 1), free_0)
                turn(1)
                outputs(0)
                key_values(1)
                scores(1, (1, 2, 3, 1), free_1)
                turn_y(0)
                out_proj(0)
                outputs(1)
                turn_y(1)
                out_proj(1)
    ph.end()
    top.close()


def by_chunk(t):
    return t.rearrange("p (g j d) -> p g j d", g=KC, j=HG)


def heads_of(t):
    return t.rearrange("p (h d) -> p h d", h=H)


def lora_and_projections(nc, K, bank, a):
    top = ExitStack()
    wide = {"base": D, "Wq3": D, "Wk3": D, "Wv3": D, "AR": EXPERTS * RANK + EXPERTS, "BG": H + DH}
    wh = {n: top.enter_context(nc.sbuf_tensor(f"ffn_{n}_hi", [P, KC, w], F32R)) for n, w in wide.items()}
    wl = {n: top.enter_context(nc.sbuf_tensor(f"ffn_{n}_lo", [P, KC, w], F32R)) for n, w in wide.items()}
    lbh = top.enter_context(nc.sbuf_tensor("ffn_loraB_hi", [P, D], F32R))
    lbl = top.enter_context(nc.sbuf_tensor("ffn_loraB_lo", [P, D], F32R))
    load_split(nc, "ffn_w", [(a[n], wh[n][:].rearrange("p c n -> p (c n)"), wl[n][:].rearrange("p c n -> p (c n)"))
                             for n in wide] + [(a["loraB"], lbh[:], lbl[:])])
    ph = Phase(nc, "ffn")
    bk = [bank[0:4], bank[4:8]]
    ident = ph.sb("ident", [P, P])
    base_b, router_b = ph.sb("base_b", [P, D]), ph.sb("router_b", [P, EXPERTS])
    order = ph.sb("order", [P, EXPERTS])
    wg2 = ph.sb("wg2", [DH, D])
    x1, xb = ph.sb2("x1", [P, D]), ph.sb2("xb", [P, D])
    xh, xl = ph.sb2("xh", [P, KC, P], F32R), ph.sb2("xl", [P, KC, P], F32R)
    lg, top8 = ph.sb2("lg", [P, EXPERTS]), ph.sb2("top8", [P, 8])
    idx, idf = ph.sb2("idx", [P, 8], U32), ph.sb2("idf", [P, 8])
    mask, ex, tot, neg = ph.sb2("mask", [P, EXPERTS]), ph.sb2("ex", [P, EXPERTS]), ph.sb2("tot", [P, 2]), ph.sb2("neg", [P, 1])
    mid, mh, ml = ph.sb2("mid", [P, P]), ph.sb2("mh", [P, P], F32R), ph.sb2("ml", [P, P], F32R)
    x2 = ph.sb2("x2", [P, D])
    q3, kn, sq, sg = ph.sb2("q3", [P, D]), ph.sb2("kn", [P, D]), ph.sb2("sq", [P, D]), ph.sb2("sg", [P, D])
    kw = ph.sb2("kw", [P, 6, H])
    te = ph.sb2("te", [P, HG, KC, DH + 1])
    g1, g1T = ph.sb2("g1", [P, DH]), ph.sb2("g1T", [DH, P])
    qT, kT = ph.sb2("qT", [P, D]), ph.sb2("kT", [P, D])
    s = {}
    for n, per in [("x1_in", 16), ("xb", 1), ("x1T", 1), ("x1h", 1), ("x1l", 1), ("lm", 1), ("lg", 1), ("top", 1),
                   ("idx", 1), ("idf", 1), ("m1", 1), ("mask", 1), ("neg", 1), ("ex", 1), ("em", 1), ("tot", 1), ("inv", 1),
                   ("gate", 1), ("mid", 1), ("midT", 1), ("mh", 1), ("ml", 1), ("ffn", 1), ("r", 1), ("x2", 1),
                   ("x2T", 1), ("x2h", 1), ("x2l", 1), ("bg", 1), ("q", 1), ("k", 1), ("v", 1), ("q3", 1), ("eta", 1),
                   ("sq", 1), ("ss", 1), ("kn1", 1), ("kn2", 1), ("kn3", 1), ("kn4", 1), ("m1b", 1), ("m2b", 1), ("kr", 1), ("kn", 1), ("te", 1),
                   ("eta2", 1), ("qTp", 1), ("kTp", 1), ("qT", 1), ("kT", 1), ("g1", 1), ("g1Tp", 1), ("g1T", 1), ("gt", 1), ("sg", 1),
                   ("stored", 16 * 6)]:
        s[n] = ph.counters_of_two(n, per)
    nx = [Norm(ph, "nx", b, 1e-5) for b in range(2)]
    consts = ph.counter("consts", 16 * 5)

    with nc.Block() as block:
        def rows(name, i, b):
            return a[name][bass.ds((i * 2 + (b - 2)) * P, P), :]

        @block.sync
        def _(sp):
            for t, src in ((ident, K["ident"]), (base_b, a["base_b"]), (router_b, a["router_b"]), (order, K["order"]),
                           (wg2, a["Wg2"])):
                sp.dma_start(t[:], src).then_inc(consts.sem, 16)
            with sp.Fori(1, NT + 1) as i:
                for b in range(2):
                    sp.wait_ge(s["x1T"][b].sem, s["x1T"][b].last(i))
                    sp.wait_ge(s["xb"][b].sem, s["xb"][b].last(i))
                    sp.dma_start(x1[b][:], rows("x1", i, b)).then_inc(s["x1_in"][b].sem, 16)
                for b in range(2):
                    for made, buf, name in (("x2", x2, "x2"), ("q3", q3, "q3"), ("qT", qT, "qT"), ("kT", kT, "kT")):
                        sp.wait_ge(s[made][b].sem, s[made][b].now(i))
                        sp.dma_start(rows(name, i, b), buf[b][:]).then_inc(s["stored"][b].sem, 16)
                    sp.wait_ge(s["te"][b].sem, s["te"][b].now(i))
                    sp.wait_ge(s["eta2"][b].sem, s["eta2"][b].now(i))
                    sp.dma_start(rows("te", i, b), te[b][:].rearrange("p j g d -> p (j g d)")).then_inc(s["stored"][b].sem, 16)
                    sp.wait_ge(s["sg"][b].sem, s["sg"][b].now(i))
                    sp.dma_start(rows("sg", i, b), sg[b][:]).then_inc(s["stored"][b].sem, 16)
            for b in range(2):
                sp.wait_ge(s["stored"][b].sem, s["stored"][b].now(NT))

        @block.gpsimd
        def _(pool):
            ph.credit(pool)
            pool.wait_ge(consts.sem, consts.now(1))
            with pool.Fori(1, NT + 1) as i:
                for b in range(2):
                    pool.wait_ge(s["x1_in"][b].sem, s["x1_in"][b].now(i))
                    pool.wait_ge(s["r"][b].sem, s["r"][b].last(i))
                    nc.gpsimd.tensor_tensor(xb[b][:], x1[b][:], base_b[:], ALU.add).then_inc(s["xb"][b].sem, 1)
                for b in range(2):
                    pool.wait_ge(s["eta"][b].sem, s["eta"][b].now(i))
                    sig = kw[b][:, 5].rearrange("p (g j) -> p g j", g=KC)
                    pool.wait_ge(s["stored"][b].sem, s["stored"][b].last(i))
                    nc.gpsimd.tensor_tensor(te[b][:, :, :, DH].rearrange("p j g -> p g j"), sig, sig,
                                            ALU.add).then_inc(s["eta2"][b].sem, 1)

        @block.scalar
        def _(act):
            act.wait_ge(consts.sem, consts.now(1))
            with act.Fori(1, NT + 1) as i:
                def lead_x1(b):
                    act.wait_ge(s["x1T"][b].sem, s["x1T"][b].now(i))
                    nc.scalar.copy(xh[b][:].rearrange("p c t -> p (c t)"), bk[b][0][:]).then_inc(s["x1h"][b].sem, 1)

                def soft(b):
                    act.wait_ge(s["neg"][b].sem, s["neg"][b].now(i))
                    nc.scalar.activation(ex[b][:], lg[b][:], ACT.Exp, bias=neg[b][:, 0:1]).then_inc(s["ex"][b].sem, 1)

                def lead_mid(b):
                    act.wait_ge(s["midT"][b].sem, s["midT"][b].now(i))
                    nc.scalar.copy(mh[b][:], bk[b][3][:, 0:P]).then_inc(s["mh"][b].sem, 1)

                def lead_x2(b):
                    act.wait_ge(s["x2T"][b].sem, s["x2T"][b].now(i))
                    nc.scalar.copy(xh[b][:].rearrange("p c t -> p (c t)"), bk[b][0][:]).then_inc(s["x2h"][b].sem, 1)

                def squares(b):
                    act.wait_ge(s["bg"][b].sem, s["bg"][b].now(i))
                    nc.scalar.copy(g1[b][:], bk[b][1][:, H:H + DH]).then_inc(s["g1"][b].sem, 1)
                    act.wait_ge(s["k"][b].sem, s["k"][b].now(i))
                    nc.scalar.activation(sq[b][:], bk[b][3][:], ACT.Square).then_inc(s["sq"][b].sem, 1)
                    act.wait_ge(s["kn1"][b].sem, s["kn1"][b].now(i))
                    nc.scalar.activation(kw[b][:, 1], kw[b][:, 0], ACT.Ln).then_inc(s["kn2"][b].sem, 1)
                    act.wait_ge(s["kn2"][b].sem, s["kn2"][b].now(i))
                    nc.scalar.activation(kw[b][:, 2], kw[b][:, 1], ACT.Exp, scale=-0.5).then_inc(s["kn3"][b].sem, 1)

                def silus(b):
                    act.wait_ge(s["q"][b].sem, s["q"][b].now(i))
                    act.wait_ge(s["stored"][b].sem, s["stored"][b].last(i))
                    nc.scalar.activation(q3[b][:], bk[b][2][:], ACT.Silu).then_inc(s["q3"][b].sem, 1)
                    nc.scalar.activation(kw[b][:, 5], bk[b][1][:, 0:H], ACT.Sigmoid).then_inc(s["eta"][b].sem, 1)

                def turned(b):
                    act.wait_ge(s["qTp"][b].sem, s["qTp"][b].now(i))
                    nc.scalar.copy(qT[b][:], bk[b][1][:]).then_inc(s["qT"][b].sem, 1)
                    act.wait_ge(s["kTp"][b].sem, s["kTp"][b].now(i))
                    nc.scalar.copy(kT[b][:], bk[b][2][:]).then_inc(s["kT"][b].sem, 1)
                    act.wait_ge(s["g1Tp"][b].sem, s["g1Tp"][b].now(i))
                    nc.scalar.copy(g1T[b][:], bk[b][3][0:DH, 0:P]).then_inc(s["g1T"][b].sem, 1)
                    act.wait_ge(s["gt"][b].sem, s["gt"][b].now(i))
                    nc.scalar.activation(sg[b][:], bk[b][0][:], ACT.Sigmoid).then_inc(s["sg"][b].sem, 1)

                lead_x1(0)
                lead_x1(1)
                soft(0)
                lead_mid(0)
                soft(1)
                lead_mid(1)
                nx[0].guesses(nc, act, i)
                lead_x2(0)
                nx[1].guesses(nc, act, i)
                lead_x2(1)
                squares(0)
                squares(1)
                silus(0)
                turned(0)
                silus(1)
                turned(1)

        @block.vector
        def _(dve):
            dve.wait_ge(consts.sem, consts.now(1))
            with dve.Fori(1, NT + 1) as i:
                def trail_x1(b):
                    dve.wait_ge(s["x1h"][b].sem, s["x1h"][b].now(i))
                    nc.vector.tensor_tensor(xl[b][:].rearrange("p c t -> p (c t)"), bk[b][0][:],
                                            xh[b][:].bitcast(F32).rearrange("p c t -> p (c t)"), ALU.subtract).then_inc(s["x1l"][b].sem, 1)

                def step(name, b, ins):
                    ins.then_inc(s[name][b].sem, 1)
                    dve.wait_ge(s[name][b].sem, s[name][b].now(i))

                def route(b):
                    dve.wait_ge(s["lm"][b].sem, s["lm"][b].now(i))
                    step("lg", b, nc.vector.tensor_tensor(lg[b][:], bk[b][1][:, P:P + EXPERTS], router_b[:], ALU.add))
                    nc.vector.memset(neg[b][:], 0.0)
                    step("top", b, nc.vector.max(top8[b][:], lg[b][:]))
                    nc.vector.tensor_scalar(neg[b][:], top8[b][:, 0:1], -1.0, None, ALU.mult).then_inc(s["neg"][b].sem, 1)
                    step("idx", b, nc.vector.max_index(idx[b][:], top8[b][:], lg[b][:]))
                    step("idf", b, nc.vector.tensor_copy(idf[b][:], idx[b][:]))
                    step("m1", b, nc.vector.tensor_scalar(mask[b][:], order[:], idf[b][:, 0:1], None, ALU.is_equal))
                    step("mask", b, nc.vector.scalar_tensor_tensor(mask[b][:], order[:], idf[b][:, 1:2], mask[b][:], ALU.is_equal, ALU.add))
                    dve.wait_ge(s["ex"][b].sem, s["ex"][b].now(i))
                    step("em", b, nc.vector.tensor_tensor(ex[b][:], ex[b][:], mask[b][:], ALU.mult))
                    step("tot", b, nc.vector.tensor_reduce(tot[b][:, 0:1], ex[b][:], AX, ALU.add))
                    step("inv", b, nc.vector.reciprocal(tot[b][:, 1:2], tot[b][:, 0:1]))
                    step("gate", b, nc.vector.tensor_scalar(ex[b][:], ex[b][:], tot[b][:, 1:2], 2.0, ALU.mult, ALU.mult))
                    nc.vector.tensor_tensor(mid[b][:].rearrange("p (e r) -> p e r", e=EXPERTS),
                                            bk[b][1][:, 0:P].rearrange("p (e r) -> p e r", e=EXPERTS),
                                            ex[b][:].unsqueeze(2).to_broadcast([P, EXPERTS, RANK]), ALU.mult).then_inc(s["mid"][b].sem, 1)

                def trail_mid(b):
                    dve.wait_ge(s["mh"][b].sem, s["mh"][b].now(i))
                    nc.vector.tensor_tensor(ml[b][:], bk[b][3][:, 0:P], mh[b][:].bitcast(F32), ALU.subtract).then_inc(s["ml"][b].sem, 1)

                def norm_x(b):
                    dve.wait_ge(s["ffn"][b].sem, s["ffn"][b].now(i))
                    dve.wait_ge(s["xb"][b].sem, s["xb"][b].now(i))
                    dve.wait_ge(s["stored"][b].sem, s["stored"][b].last(i))
                    step("r", b, nc.vector.tensor_tensor(x2[b][:], bk[b][2][:], xb[b][:], ALU.add))
                    nx[b].stats(nc, dve, i, x2[b][:])
                    nx[b].newton(nc, dve, i)
                    nx[b].apply(nc, x2[b][:], x2[b][:]).then_inc(s["x2"][b].sem, 1)

                def trail_x2(b):
                    dve.wait_ge(s["x2h"][b].sem, s["x2h"][b].now(i))
                    nc.vector.tensor_tensor(xl[b][:].rearrange("p c t -> p (c t)"), bk[b][0][:],
                                            xh[b][:].bitcast(F32).rearrange("p c t -> p (c t)"), ALU.subtract).then_inc(s["x2l"][b].sem, 1)

                def keys(b):
                    dve.wait_ge(s["sq"][b].sem, s["sq"][b].now(i))
                    step("ss", b, nc.vector.tensor_reduce(kw[b][:, 0], heads_of(sq[b][:]), AX, ALU.add))
                    nc.vector.tensor_scalar(kw[b][:, 0], kw[b][:, 0], 1e-6, None, ALU.add).then_inc(s["kn1"][b].sem, 1)
                    dve.wait_ge(s["kn3"][b].sem, s["kn3"][b].now(i))
                    step("kn4", b, nc.vector.tensor_tensor(kw[b][:, 3], kw[b][:, 2], kw[b][:, 2], ALU.mult))
                    step("m1b", b, nc.vector.tensor_tensor(kw[b][:, 3], kw[b][:, 3], kw[b][:, 0], ALU.mult))
                    step("m2b", b, nc.vector.tensor_scalar(kw[b][:, 3], kw[b][:, 3], -0.5, 1.5, ALU.mult, ALU.add))
                    step("kr", b, nc.vector.tensor_tensor(kw[b][:, 4], kw[b][:, 3], kw[b][:, 2], ALU.mult))
                    step("kn", b, nc.vector.tensor_tensor(heads_of(kn[b][:]), heads_of(bk[b][3][:]),
                                                          kw[b][:, 4].unsqueeze(2).to_broadcast([P, H, DH]), ALU.mult))
                    dve.wait_ge(s["v"][b].sem, s["v"][b].now(i))
                    nc.vector.tensor_tensor(te[b][:, :, :, 0:DH].rearrange("p j g d -> p g j d"), by_chunk(bk[b][0][:]),
                                            by_chunk(kn[b][:]), ALU.subtract).then_inc(s["te"][b].sem, 1)

                trail_x1(0)
                trail_x1(1)
                route(0)
                trail_mid(0)
                route(1)
                trail_mid(1)
                norm_x(0)
                trail_x2(0)
                norm_x(1)
                trail_x2(1)
                keys(0)
                keys(1)

        @block.tensor
        def _(pe):
            pe.wait_ge(consts.sem, consts.now(1))
            with pe.Fori(1, NT + 1) as i:
                def turn(b, src, dst, got, made):
                    pe.wait_ge(s[got][b].sem, s[got][b].now(i))
                    for c in range(KC):
                        last = pe.transpose(dst[:, c * P:(c + 1) * P], src[:, c * P:(c + 1) * P], ident[:])
                    last.then_inc(s[made][b].sem, 1)

                def times(out, b, name, stop=True):
                    return exact3(pe, out, lambda c: xh[b][:, c, :], lambda c: xl[b][:, c, :],
                                  lambda c: wh[name][:, c, :], lambda c: wl[name][:, c, :], stop=stop)

                def ffn(b):
                    pe.wait_ge(s["x1l"][b].sem, s["x1l"][b].now(i))
                    pe.wait_ge(s["qT"][b].sem, s["qT"][b].last(i))
                    times(bk[b][1][:, 0:P + EXPERTS], b, "AR").then_inc(s["lm"][b].sem, 1)
                    pe.wait_ge(s["kT"][b].sem, s["kT"][b].last(i))
                    times(bk[b][2][:], b, "base", stop=False)

                def lora(b):
                    pe.wait_ge(s["mid"][b].sem, s["mid"][b].now(i))
                    pe.wait_ge(s["g1T"][b].sem, s["g1T"][b].last(i))
                    pe.transpose(bk[b][3][:, 0:P], mid[b][:], ident[:]).then_inc(s["midT"][b].sem, 1)
                    pe.wait_ge(s["ml"][b].sem, s["ml"][b].now(i))
                    exact3(pe, bk[b][2][:], lambda c: mh[b][:], lambda c: ml[b][:], lambda c: lbh[:], lambda c: lbl[:],
                           start=False, n=1).then_inc(s["ffn"][b].sem, 1)

                def projections(b):
                    pe.wait_ge(s["x2l"][b].sem, s["x2l"][b].now(i))
                    pe.wait_ge(s["mid"][b].sem, s["mid"][b].now(i))
                    times(bk[b][1][:, 0:H + DH], b, "BG").then_inc(s["bg"][b].sem, 1)
                    times(bk[b][3][:], b, "Wk3").then_inc(s["k"][b].sem, 1)
                    times(bk[b][2][:], b, "Wq3").then_inc(s["q"][b].sem, 1)
                    times(bk[b][0][:], b, "Wv3").then_inc(s["v"][b].sem, 1)

                def turns(b):
                    pe.wait_ge(s["g1"][b].sem, s["g1"][b].now(i))
                    pe.wait_ge(s["eta"][b].sem, s["eta"][b].now(i))
                    turn(b, q3[b], bk[b][1], "q3", "qTp")
                    turn(b, kn[b], bk[b][2], "kn", "kTp")
                    pe.transpose(bk[b][3][0:DH, 0:P], g1[b][:], ident[:]).then_inc(s["g1Tp"][b].sem, 1)
                    pe.wait_ge(s["g1T"][b].sem, s["g1T"][b].now(i))
                    pe.wait_ge(s["te"][b].sem, s["te"][b].now(i))
                    pe.matmul(bk[b][0][:], g1T[b][:], wg2[:], start=True, stop=True).then_inc(s["gt"][b].sem, 1)

                for b in range(2):
                    pe.wait_ge(s["sg"][b].sem, s["sg"][b].last(i))
                    turn(b, x1[b], bk[b][0], "x1_in", "x1T")
                ffn(0)
                ffn(1)
                lora(0)
                lora(1)
                turn(0, x2[0], bk[0][0], "x2", "x2T")
                projections(0)
                turn(1, x2[1], bk[1][0], "x2", "x2T")
                projections(1)
                turns(0)
                turns(1)
    ph.end()
    top.close()


def ttt_recurrence(nc, K, bank, a):
    ST, NI = NCH, NT
    HALF = ST // 2
    ph = Phase(nc, "ttt")
    bS, bH, bQ, bA, bK, bC = bank[0:6]
    G = KC
    R64 = HG * TTT
    ident = ph.sb("ident", [P, P])
    tri = ph.sb("tri", [P, R64])
    w_row, b_row, w2 = ph.sb("w_row", [P, G, DH]), ph.sb("b_row", [P, G, DH]), ph.sb("w2", [P, G, DH])
    seq, own = ph.sb("seq", [P, 2]), ph.sb("own", [P, HG])
    zero = ph.sb("zero", [P, 2 * P])
    cK, cQ = ph.sb("cK", [P, B, G, ST * TTT]), ph.sb("cQ", [P, B, G, ST * TTT])
    te = ph.sb("te", [P, ST, G, DH + 1])
    bw = ph.sb("bw", [P, ST, G, DH])
    neta = ph.sb("neta", [P, ST, G])
    KB = [ph.sb(f"KB{r}", [P, G, B, HG, TTT]) for r in range(ST)]
    QB = [ph.sb(f"QB{r}", [P, G, B, HG, TTT]) for r in range(ST)]
    S = ph.sb("S", [P, G, B, DH])
    kb = ph.sb("kb", [P, G, P])
    am = ph.sb("am", [P, G, R64])
    u = ph.sb("u", [P, G, DH])
    ub = ph.sb("ub", [P, G, B, DH])
    cross = ph.sb("cross", [P, G, P])
    qh = ph.sb("qh", [R64, ST, B, G, DH])
    c1, c2, c3, c4, c5, c6 = (ph.sb(f"c{k}", [P, G, DH]) for k in range(6))
    eps = ph.sb("eps", [P, 1])
    m = ph.sb("m", [P, 8, G])
    re = ph.sb("re", [P, G])
    s = {n: ph.counter(n, per) for n, per in
         [("cK", 16 * 4), ("te", 16 * 8), ("bw1", 2), ("bw", 2), ("neta", 2), ("blocks", ST), ("S", ST), ("KH", ST), ("QS", ST),
          ("A", ST), ("KT", ST), ("kb", ST), ("am", ST), ("s1", ST), ("xc", ST), ("sq", ST), ("s2", ST), ("sd", ST), ("rs", ST),
          ("re", ST), ("xw", ST), ("hat", ST), ("t", ST), ("gw", ST), ("r1", ST), ("p", ST), ("r2", ST), ("v1", ST), ("q", ST),
          ("v2", ST), ("u", ST), ("ub", ST), ("KK", ST), ("cross", ST), ("KS", ST), ("SU", ST), ("AU", ST), ("qh", ST), ("stored0", 16 * 8), ("stored1", 16 * 8)]}
    consts = ph.counter("consts", 16 * 6)
    zeroed = ph.counter("zeroed", 2)
    w2_made = ph.counter("w2", 1)
    s0_made = ph.counter("s0", 1)

    with nc.Block() as block:
        @block.sync
        def _(sp):
            for t, src in ((ident, K["ident"]), (tri, K["tri"]), (w_row, a["ln_w"]), (b_row, a["ln_b"]), (seq, K["seq"]),
                           (own, K["own"])):
                sp.dma_start(t[:] if len(t.shape) < 3 else t[:].rearrange("p g d -> p (g d)"), src).then_inc(consts.sem, 16)

            def load(i):
                sp.wait_ge(s["blocks"].sem, s["blocks"].last(i))
                for b in range(B):
                    for dst, name in ((cK, "kT"), (cQ, "qT")):
                        sp.dma_start(dst[:, b].rearrange("p g t -> p (g t)"), a[name][bass.ds((i * 2 + (b - 2)) * P, P), :]).then_inc(s["cK"].sem, 16)
                sp.wait_ge(s["bw"].sem, s["bw"].last(i))
                sp.wait_ge(s["neta"].sem, s["neta"].last(i))
                for b in range(B):
                    for j in range(HG):
                        rows = a["te"][bass.ds((i * 2 + (b - 2)) * P, P), :]
                        src = rows.rearrange("(c t) (j e) -> j t c e", t=TTT, j=HG)[j]
                        r = b * R64 + j * TTT
                        sp.dma_start(te[r:r + TTT].rearrange("t c g e -> t c (g e)"), src).then_inc(s["te"].sem, 16)

            def store(i):
                for f in range(2):
                    sp.wait_ge(s["qh"].sem, s["qh"].part(i, (f + 1) * HALF))
                    for b in range(B):
                        for j in range(HG):
                            rows = a["qh"][bass.ds((i * 2 + (b - 2)) * P + f * HALF * TTT, HALF * TTT), :]
                            sp.dma_start(rows.rearrange("(c t) (j e) -> j t c e", t=TTT, j=HG)[j],
                                         qh[j * TTT:(j + 1) * TTT, f * HALF:(f + 1) * HALF, b].rearrange("t c g e -> t c (g e)")).then_inc(s[f"stored{f}"].sem, 16)

            load(1)
            with sp.Fori(2, NI + 1) as i:
                load(i)
                store(i - 1)
            store(NI)
            for f in range(2):
                sp.wait_ge(s[f"stored{f}"].sem, s[f"stored{f}"].now(NI))

        @block.gpsimd
        def _(pool):
            ph.credit(pool)
            nc.gpsimd.memset(zero[:], 0.0).then_inc(zeroed.sem, 1)
            nc.gpsimd.memset(cross[:], 0.0).then_inc(zeroed.sem, 1)
            pool.wait_ge(zeroed.sem, zeroed.now(1))
            pool.wait_ge(consts.sem, consts.now(1))

            def spread(n):
                for b in range(B):
                    for src, dst in ((cK, KB[n]), (cQ, QB[n])):
                        shape = [P, G, HG, TTT]
                        last = nc.gpsimd.tensor_tensor(
                            dst[:, :, b], src[:, b, :, n * TTT:(n + 1) * TTT].unsqueeze(2).to_broadcast(shape),
                            own[:].unsqueeze(1).unsqueeze(3).to_broadcast(shape), ALU.mult)
                last.then_inc(s["blocks"].sem, 1)

            with pool.Fori(1, NI + 1) as i:
                pool.wait_ge(s["te"].sem, s["te"].now(i))
                pool.wait_ge(s["cK"].sem, s["cK"].now(i))
                for f in range(2):
                    pool.wait_ge(s["re"].sem, s["re"].part(i, (f + 1) * HALF - ST))
                    pool.wait_ge(s["gw"].sem, s["gw"].part(i, (f + 1) * HALF - ST))
                    c = slice(f * HALF, (f + 1) * HALF)
                    nc.gpsimd.tensor_tensor(bw[:, c], b_row[:].unsqueeze(1).to_broadcast([P, HALF, G, DH]), te[:, c, :, 0:DH],
                                            ALU.subtract).then_inc(s["bw1"].sem, 1)
                    nc.gpsimd.tensor_tensor(neta[:, c], zero[:, 0:HALF * G].rearrange("p (c g) -> p c g", g=G), te[:, c, :, DH],
                                            ALU.subtract).then_inc(s["neta"].sem, 1)
                    pool.wait_ge(s["bw1"].sem, s["bw1"].part(i, f + 1))
                    nc.gpsimd.tensor_tensor(bw[:, c], bw[:, c], w_row[:].unsqueeze(1).to_broadcast([P, HALF, G, DH]),
                                            ALU.mult).then_inc(s["bw"].sem, 1)
                    for n in range(f * HALF, (f + 1) * HALF):
                        pool.wait_ge(s["QS"].sem, s["QS"].part(i, n + 1 - ST))
                        spread(n)
            for n in range(2):
                pool.wait_ge(s["QS"].sem, s["QS"].part(NI + 1, n + 1 - ST))
                spread(n)

        @block.scalar
        def _(act):
            act.wait_ge(consts.sem, consts.now(1))
            act.wait_ge(s0_made.sem, s0_made.now(1))
            act.wait_ge(w2_made.sem, 3)
            act.wait_ge(zeroed.sem, zeroed.now(1))
            nc.scalar.preload_act_table_set("sqrt_and_others")
            nc.scalar.copy(S[:].rearrange("p g b e -> p (g b e)"), bS[:, 0:2 * P]).then_inc(s["S"].sem, 1)
            act.wait_ge(s["s2"].sem, s["s2"].part(1, 1))
            nc.scalar.activation(m[:, 2], m[:, 1], ACT.Sqrt, scale=1.0 / DH, bias=eps[:, 0:1]).then_inc(s["sd"].sem, 1)
            with act.Fori(1, NI + 1) as i:
                for n in range(ST):
                    act.wait_ge(s["KT"].sem, s["KT"].part(i, n + 1))
                    nc.scalar.copy(kb[:].rearrange("p g n -> p (g n)"), bK[:]).then_inc(s["kb"].sem, 1)
                    act.wait_ge(s["KK"].sem, s["KK"].part(i, n + 1))
                    act.wait_ge(s["KH"].sem, s["KH"].part(i, n + 1))
                    for b in range(B):
                        r = slice(b * R64, (b + 1) * R64)
                        last = nc.scalar.copy(cross[r, :, r], bC[r, :].rearrange("p (g n) -> p g n", g=G)[:, :, r])
                    last.then_inc(s["cross"].sem, 1)
                    act.wait_ge(s["SU"].sem, s["SU"].part(i, n + 1))
                    act.wait_ge(s["QS"].sem, s["QS"].part(i, n + 1))
                    act.wait_ge(s["KS"].sem, s["KS"].part(i, n + 1))
                    nc.scalar.copy(S[:].rearrange("p g b e -> p (g b e)"), bS[:, 0:2 * P]).then_inc(s["S"].sem, 1)
                    act.wait_ge(s["s2"].sem, s["s2"].part(i, n + 2))
                    nc.scalar.activation(m[:, 2], m[:, 1], ACT.Sqrt, scale=1.0 / DH, bias=eps[:, 0:1]).then_inc(s["sd"].sem, 1)
                    act.wait_ge(s["AU"].sem, s["AU"].part(i, n + 1))
                    if n % HALF == 0:
                        act.wait_ge(s[f"stored{n // HALF}"].sem, s[f"stored{n // HALF}"].last(i))
                    nc.scalar.copy(qh[:, n].rearrange("p b g e -> p (b g e)"), bQ[0:R64, 0:2 * P]).then_inc(s["qh"].sem, 1)

        @block.vector
        def _(dve):
            dve.wait_ge(consts.sem, consts.now(1))
            nc.vector.memset(eps[:], 1e-6).then_inc(w2_made.sem, 1)
            nc.vector.tensor_tensor(w2[:], w_row[:], w_row[:], ALU.mult).then_inc(w2_made.sem, 1)
            dve.wait_ge(w2_made.sem, 3)
            with dve.Fori(1, NI + 1) as i:
                for n in range(ST):
                    def step(name, ins):
                        ins.then_inc(s[name].sem, 1)
                        dve.wait_ge(s[name].sem, s[name].part(i, n + 1))

                    def over_e(t):
                        return t.unsqueeze(2).to_broadcast([P, G, DH])
                    kh = bH[:, 0:P].rearrange("p (g e) -> p g e", g=G)
                    dve.wait_ge(s["KH"].sem, s["KH"].part(i, n + 1))
                    step("s1", nc.vector.tensor_reduce(m[:, 0], kh, AX, ALU.add))
                    step("xc", nc.vector.scalar_tensor_tensor(c1[:], over_e(m[:, 0]), -1.0 / DH, kh, ALU.mult, ALU.add))
                    step("sq", nc.vector.tensor_tensor(c2[:], c1[:], c1[:], ALU.mult))
                    step("s2", nc.vector.tensor_reduce(m[:, 1], c2[:], AX, ALU.add))
                    nc.vector.tensor_tensor(c3[:], c1[:], w2[:], ALU.mult).then_inc(s["xw"].sem, 1)
                    dve.wait_ge(s["sd"].sem, s["sd"].part(i, n + 1))
                    step("rs", nc.vector.reciprocal(m[:, 3], m[:, 2]))
                    if n % HALF == 0:
                        dve.wait_ge(s["neta"].sem, s["neta"].part(i, n // HALF + 1))
                        dve.wait_ge(s["bw"].sem, s["bw"].part(i, n // HALF + 1))
                    nc.vector.tensor_tensor(re[:], m[:, 3], neta[:, n], ALU.mult).then_inc(s["re"].sem, 1)
                    nc.vector.tensor_tensor(c1[:], c1[:], over_e(m[:, 3]), ALU.mult).then_inc(s["hat"].sem, 1)
                    dve.wait_ge(s["xw"].sem, s["xw"].part(i, n + 1))
                    step("t", nc.vector.tensor_tensor(c3[:], c3[:], over_e(m[:, 3]), ALU.mult))
                    step("gw", nc.vector.tensor_tensor(c3[:], c3[:], bw[:, n], ALU.add))
                    dve.wait_ge(s["hat"].sem, s["hat"].part(i, n + 1))
                    nc.vector.tensor_tensor(c2[:], c3[:], c1[:], ALU.mult).then_inc(s["p"].sem, 1)
                    nc.vector.tensor_reduce(m[:, 4], c3[:], AX, ALU.add).then_inc(s["r1"].sem, 1)
                    dve.wait_ge(s["p"].sem, s["p"].part(i, n + 1))
                    step("r2", nc.vector.tensor_reduce(m[:, 5], c2[:], AX, ALU.add))
                    dve.wait_ge(s["r1"].sem, s["r1"].part(i, n + 1))
                    nc.vector.scalar_tensor_tensor(c4[:], over_e(m[:, 4]), -1.0 / DH, c3[:], ALU.mult, ALU.add).then_inc(s["v1"].sem, 1)
                    step("q", nc.vector.tensor_tensor(c5[:], c1[:], over_e(m[:, 5]), ALU.mult))
                    dve.wait_ge(s["v1"].sem, s["v1"].part(i, n + 1))
                    step("v2", nc.vector.scalar_tensor_tensor(c6[:], c5[:], -1.0 / DH, c4[:], ALU.mult, ALU.add))
                    dve.wait_ge(s["re"].sem, s["re"].part(i, n + 1))
                    dve.wait_ge(s["SU"].sem, s["SU"].part(i, n))
                    dve.wait_ge(s["AU"].sem, s["AU"].part(i, n))
                    step("u", nc.vector.tensor_tensor(u[:], c6[:], over_e(re[:]), ALU.mult))
                    nc.vector.tensor_tensor(ub[:], u[:].unsqueeze(2).to_broadcast([P, G, B, DH]),
                                            seq[:].unsqueeze(1).unsqueeze(3).to_broadcast([P, G, B, DH]), ALU.mult).then_inc(s["ub"].sem, 1)
                    dve.wait_ge(s["A"].sem, s["A"].part(i, n + 1))
                    nc.vector.tensor_tensor(am[:], bA[:, 0:2 * P].rearrange("p (g n) -> p g n", g=G),
                                            tri[:].unsqueeze(1).to_broadcast([P, G, R64]), ALU.mult).then_inc(s["am"].sem, 1)
            nc.vector.memset(m[:, 1], 1.0).then_inc(s["s2"].sem, 1)

        @block.tensor
        def _(pe):
            pe.wait_ge(consts.sem, consts.now(1))
            pe.wait_ge(zeroed.sem, zeroed.now(1))
            pe.matmul(bS[:, 0:2 * P], zero[:, 0:P], zero[:], start=True, stop=False, skip_group_check=True).then_inc(s0_made.sem, 1)

            def keys_times_state(n):
                for g in range(G):
                    for b in range(B):
                        last = pe.matmul(bH[b * R64:(b + 1) * R64, g * DH:(g + 1) * DH], KB[n][:, g, b].rearrange("p j t -> p (j t)"),
                                         S[:, g, b, :], start=(g == 0), stop=False, skip_group_check=True)
                return last

            def scores(n, g, b):
                return pe.matmul(bA[b * R64:(b + 1) * R64, g * R64:(g + 1) * R64], KB[n][:, g, b].rearrange("p j t -> p (j t)"),
                                 QB[n][:, g, b].rearrange("p j t -> p (j t)"), start=True, stop=True, skip_group_check=True)

            def keys_times_next(n, g):
                return pe.matmul(bC[:, g * P:(g + 1) * P], KB[n][:].rearrange(both)[:, g],
                                 KB[(n + 1) % ST][:].rearrange(both)[:, g], start=True, stop=True, skip_group_check=True)

            both = "p g b j t -> p g (b j t)"

            pe.wait_ge(s["blocks"].sem, s["blocks"].part(1, 2))
            pe.wait_ge(s["S"].sem, s["S"].part(1, 1))
            keys_times_state(0)
            pe.matmul(bH[:, 0:P], zero[:, 0:P], zero[:, 0:P], start=False, stop=True, skip_group_check=True).then_inc(s["KH"].sem, 1)
            for g in range(G):
                for b in range(B):
                    last = scores(0, g, b)
            last.then_inc(s["A"].sem, 1)
            for g in range(G):
                last = pe.transpose(bK[:, g * P:(g + 1) * P], KB[0][:].rearrange(both)[:, g], ident[:])
            last.then_inc(s["KT"].sem, 1)
            for g in range(G):
                last = keys_times_next(0, g)
            last.then_inc(s["KK"].sem, 1)
            with pe.Fori(1, NI + 1) as i:
                for n in range(ST):
                    QBf = QB[n][:].rearrange("p g b j t -> p g b (j t)")
                    pe.wait_ge(s["S"].sem, s["S"].part(i, n + 1))
                    pe.wait_ge(s["xc"].sem, s["xc"].part(i, n + 1))
                    pe.wait_ge(s["blocks"].sem, s["blocks"].part(i, n + 2))
                    keys_times_state((n + 1) % ST).then_inc(s["KS"].sem, 1)
                    pe.wait_ge(s["qh"].sem, s["qh"].part(i, n))
                    for g in range(G):
                        for b in range(B):
                            last = pe.matmul(bQ[0:R64, (b * G + g) * DH:(b * G + g + 1) * DH], QBf[:, g, b, :], S[:, g, b, :],
                                             start=(g == 0 and b == 0), stop=False, skip_group_check=True)
                    last.then_inc(s["QS"].sem, 1)
                    pe.wait_ge(s["u"].sem, s["u"].part(i, n + 1))
                    pe.wait_ge(s["cross"].sem, s["cross"].part(i, n + 1))
                    for g in range(G):
                        last = pe.matmul(bH[:, g * DH:(g + 1) * DH], cross[:, g, :], u[:, g, :], start=False, stop=True, skip_group_check=True)
                    last.then_inc(s["KH"].sem, 1)
                    pe.wait_ge(s["ub"].sem, s["ub"].part(i, n + 1))
                    pe.wait_ge(s["kb"].sem, s["kb"].part(i, n + 1))
                    for g in range(G):
                        last = pe.matmul(bS[:, g * B * DH:(g + 1) * B * DH], kb[:, g, :], ub[:, g].rearrange("p b e -> p (b e)"),
                                         start=False, stop=False, skip_group_check=True)
                    last.then_inc(s["SU"].sem, 1)
                    pe.wait_ge(s["am"].sem, s["am"].part(i, n + 1))
                    for g in range(G):
                        last = pe.matmul(bQ[0:R64, 0:2 * P].rearrange("p (b g e) -> p g b e", b=B, g=G)[:, g], am[:, g, :],
                                         ub[:, g].rearrange("p b e -> p (b e)"),
                                         start=False, stop=(g == G - 1), skip_group_check=True)
                    last.then_inc(s["AU"].sem, 1)
                    for g in range(G):
                        for b in range(B):
                            last = scores((n + 1) % ST, g, b)
                    last.then_inc(s["A"].sem, 1)
                    for g in range(G):
                        last = pe.transpose(bK[:, g * P:(g + 1) * P], KB[(n + 1) % ST][:].rearrange(both)[:, g], ident[:])
                    last.then_inc(s["KT"].sem, 1)
                    pe.wait_ge(s["blocks"].sem, s["blocks"].part(i, n + 3))
                    for g in range(G):
                        last = keys_times_next((n + 1) % ST, g)
                    last.then_inc(s["KK"].sem, 1)
    ph.end()


def attention_output(nc, K, bank, a):
    top = ExitStack()
    wh = top.enter_context(nc.sbuf_tensor("out_w_hi", [P, KC, D], F32R))
    wl = top.enter_context(nc.sbuf_tensor("out_w_lo", [P, KC, D], F32R))
    load_split(nc, "out_w", [(a["Wo3"], wh[:].rearrange("p c n -> p (c n)"), wl[:].rearrange("p c n -> p (c n)"))])
    ph = Phase(nc, "out")
    bk = [bank[0:4], bank[4:8]]
    ident = ph.sb("ident", [P, P])
    w_all, b_all, norm_w = ph.sb("w_all", [P, D]), ph.sb("b_all", [P, D]), ph.sb("norm_w", [P, KC])
    eps6, eps5 = ph.sb("eps6", [P, 1]), ph.sb("eps5", [P, 1])
    names = ["qh", "q3", "sg", "x2"]
    t = {n: ph.sb2(n, [P, D]) for n in names}
    xc, sq, og, oT, r, x3T = (ph.sb2(n, [P, D]) for n in ("xc", "sq", "og", "oT", "r", "x3T"))
    oh, ol = ph.sb2("oh", [P, KC, P], F32R), ph.sb2("ol", [P, KC, P], F32R)
    w = ph.sb2("w", [P, 8, H])
    st, mv = ph.sb2("st", [P, 6]), ph.sb2("mv", [P, 4])
    s = {}
    for n, per in [("in", 16 * 4), ("s1", 1), ("xc", 1), ("sq", 1), ("s2", 1), ("sd", 1), ("rs", 1), ("hat", 1), ("ow", 1), ("ob", 1),
                   ("oq", 1), ("og", 1), ("sq2", 1), ("s3", 1), ("sd2", 1), ("rs2", 1), ("o5", 1), ("oTp", 1), ("oT", 1), ("oh", 1), ("ol", 1),
                   ("o", 1), ("r", 1), ("st", 1), ("mv", 1), ("sd3", 1), ("rs3", 1), ("x3", 1), ("x3Tp", 1), ("x3T", 1), ("stored", 32)]:
        s[n] = ph.counters_of_two(n, per)
    consts = ph.counter("consts", 16 * 4)
    epsed = ph.counter("eps", 2)

    def rows(name, i, b):
        return a[name][bass.ds((i * 2 + (b - 2)) * P, P), :]

    def by_place(v):
        return v.rearrange("p (g j e) -> p j g e", g=KC, j=HG)

    def placed(v):
        return v.rearrange("p (j g e) -> p j g e", g=KC, j=HG)

    def each_head(v):
        return v.unsqueeze(2).to_broadcast([P, H, DH])

    with nc.Block() as block:
        @block.sync
        def _(sp):
            for dst, src in ((ident, K["ident"]), (w_all, a["w_all"]), (b_all, a["b_all"]), (norm_w, a["norm_w"])):
                sp.dma_start(dst[:], src).then_inc(consts.sem, 16)
            with sp.Fori(1, NT + 1) as i:
                for b in range(2):
                    sp.wait_ge(s["og"][b].sem, s["og"][b].last(i))
                    sp.wait_ge(s["r"][b].sem, s["r"][b].last(i))
                    for n in names:
                        sp.dma_start(t[n][b][:], rows(n, i, b)).then_inc(s["in"][b].sem, 16)
                for b in range(2):
                    sp.wait_ge(s["x3"][b].sem, s["x3"][b].now(i))
                    sp.dma_start(rows("x3", i, b), r[b][:]).then_inc(s["stored"][b].sem, 16)
                    sp.wait_ge(s["x3T"][b].sem, s["x3T"][b].now(i))
                    sp.dma_start(rows("x3T", i, b), x3T[b][:]).then_inc(s["stored"][b].sem, 16)
            for b in range(2):
                sp.wait_ge(s["stored"][b].sem, s["stored"][b].now(NT))

        @block.gpsimd
        def _(pool):
            ph.credit(pool)
            nc.gpsimd.memset(eps6[:], 1e-6).then_inc(epsed.sem, 1)
            nc.gpsimd.memset(eps5[:], 1e-5).then_inc(epsed.sem, 1)
            pool.wait_ge(consts.sem, consts.now(1))
            with pool.Fori(1, NT + 1) as i:
                for b in range(2):
                    def step(name, ins):
                        ins.then_inc(s[name][b].sem, 1)
                        pool.wait_ge(s[name][b].sem, s[name][b].now(i))
                    pool.wait_ge(s["hat"][b].sem, s["hat"][b].now(i))
                    step("ow", nc.gpsimd.tensor_tensor(xc[b][:], xc[b][:], w_all[:], ALU.mult))
                    step("ob", nc.gpsimd.tensor_tensor(xc[b][:], xc[b][:], b_all[:], ALU.add))
                    step("oq", nc.gpsimd.tensor_tensor(placed(xc[b][:]), placed(xc[b][:]), by_place(t["q3"][b][:]), ALU.add))
                    pool.wait_ge(s["oTp"][b].sem, s["oTp"][b].last(i))
                    nc.gpsimd.tensor_tensor(by_place(og[b][:]), placed(xc[b][:]), by_place(t["sg"][b][:]), ALU.mult).then_inc(s["og"][b].sem, 1)

        @block.scalar
        def _(act):
            act.wait_ge(consts.sem, consts.now(1))
            act.wait_ge(epsed.sem, epsed.now(1))
            with act.Fori(1, NT + 1) as i:
                def square(b, src, got, made):
                    act.wait_ge(s[got][b].sem, s[got][b].now(i))
                    nc.scalar.activation(sq[b][:], src[b][:], ACT.Square).then_inc(s[made][b].sem, 1)

                def root(b, col, got, made):
                    act.wait_ge(s[got][b].sem, s[got][b].now(i))
                    nc.scalar.activation(w[b][:, col + 1], w[b][:, col], ACT.Sqrt, scale=1.0 / DH, bias=eps6[:, 0:1]).then_inc(s[made][b].sem, 1)

                def scaled(b):
                    act.wait_ge(s["oTp"][b].sem, s["oTp"][b].now(i))
                    for c in range(KC):
                        last = nc.scalar.activation(oT[b][:, c * P:(c + 1) * P], bk[b][0][:, c * P:(c + 1) * P], ACT.Identity,
                                                    scale=norm_w[:, c:c + 1])
                    last.then_inc(s["oT"][b].sem, 1)

                def root_x(b):
                    act.wait_ge(s["mv"][b].sem, s["mv"][b].now(i))
                    nc.scalar.activation(mv[b][:, 2:3], mv[b][:, 1:2], ACT.Sqrt, bias=eps5[:, 0:1]).then_inc(s["sd3"][b].sem, 1)

                def turned(b):
                    act.wait_ge(s["x3Tp"][b].sem, s["x3Tp"][b].now(i))
                    act.wait_ge(s["stored"][b].sem, s["stored"][b].last(i))
                    nc.scalar.copy(x3T[b][:], bk[b][2][:]).then_inc(s["x3T"][b].sem, 1)

                for b in range(2):
                    square(b, xc, "xc", "sq")
                    root(b, 1, "s2", "sd")
                for b in range(2):
                    square(b, og, "og", "sq2")
                    root(b, 4, "s3", "sd2")
                scaled(0)
                scaled(1)
                root_x(0)
                root_x(1)
                turned(0)
                turned(1)

        @block.vector
        def _(dve):
            dve.wait_ge(consts.sem, consts.now(1))
            with dve.Fori(1, NT + 1) as i:
                def step(name, b, ins):
                    ins.then_inc(s[name][b].sem, 1)
                    dve.wait_ge(s[name][b].sem, s[name][b].now(i))

                def centre(b):
                    dve.wait_ge(s["in"][b].sem, s["in"][b].now(i))
                    dve.wait_ge(s["og"][b].sem, s["og"][b].last(i))
                    step("s1", b, nc.vector.tensor_reduce(w[b][:, 0], heads_of(t["qh"][b][:]), AX, ALU.add))
                    step("xc", b, nc.vector.scalar_tensor_tensor(heads_of(xc[b][:]), each_head(w[b][:, 0]), -1.0 / DH,
                                                                 heads_of(t["qh"][b][:]), ALU.mult, ALU.add))

                def unit(b):
                    dve.wait_ge(s["sq"][b].sem, s["sq"][b].now(i))
                    step("s2", b, nc.vector.tensor_reduce(w[b][:, 1], heads_of(sq[b][:]), AX, ALU.add))
                    dve.wait_ge(s["sd"][b].sem, s["sd"][b].now(i))
                    step("rs", b, nc.vector.reciprocal(w[b][:, 3], w[b][:, 2]))
                    nc.vector.tensor_tensor(heads_of(xc[b][:]), heads_of(xc[b][:]), each_head(w[b][:, 3]), ALU.mult).then_inc(s["hat"][b].sem, 1)

                def rms(b):
                    dve.wait_ge(s["sq2"][b].sem, s["sq2"][b].now(i))
                    step("s3", b, nc.vector.tensor_reduce(w[b][:, 4], heads_of(sq[b][:]), AX, ALU.add))
                    dve.wait_ge(s["sd2"][b].sem, s["sd2"][b].now(i))
                    step("rs2", b, nc.vector.reciprocal(w[b][:, 6], w[b][:, 5]))
                    nc.vector.tensor_tensor(heads_of(og[b][:]), heads_of(og[b][:]), each_head(w[b][:, 6]), ALU.mult).then_inc(s["o5"][b].sem, 1)

                def split(b):
                    dve.wait_ge(s["oT"][b].sem, s["oT"][b].now(i))
                    step("oh", b, nc.vector.tensor_copy(oh[b][:].rearrange("p c t -> p (c t)"), oT[b][:]))
                    nc.vector.tensor_tensor(ol[b][:].rearrange("p c t -> p (c t)"), oT[b][:],
                                            oh[b][:].bitcast(F32).rearrange("p c t -> p (c t)"), ALU.subtract).then_inc(s["ol"][b].sem, 1)

                def norm(b):
                    dve.wait_ge(s["o"][b].sem, s["o"][b].now(i))
                    dve.wait_ge(s["stored"][b].sem, s["stored"][b].last(i))
                    step("r", b, nc.vector.tensor_tensor(r[b][:], bk[b][1][:], t["x2"][b][:], ALU.add))
                    step("st", b, nc.vector.bn_stats(st[b][:], r[b][:]))
                    nc.vector.memset(mv[b][:, 3:4], 0.0)
                    nc.vector.bn_aggr(mv[b][:, 0:2], st[b][:]).then_inc(s["mv"][b].sem, 1)
                    dve.wait_ge(s["sd3"][b].sem, s["sd3"][b].now(i))
                    step("rs3", b, nc.vector.reciprocal(mv[b][:, 3:4], mv[b][:, 2:3]))
                    nc.vector.tensor_scalar(r[b][:], r[b][:], mv[b][:, 0:1], mv[b][:, 3:4], ALU.subtract, ALU.mult).then_inc(s["x3"][b].sem, 1)

                for stage in (centre, unit, rms, split, norm):
                    stage(0)
                    stage(1)

        @block.tensor
        def _(pe):
            pe.wait_ge(consts.sem, consts.now(1))
            with pe.Fori(1, NT + 1) as i:
                for b in range(2):
                    pe.wait_ge(s["o5"][b].sem, s["o5"][b].now(i))
                    for c in range(KC):
                        last = pe.transpose(bk[b][0][:, c * P:(c + 1) * P], og[b][:, c * P:(c + 1) * P], ident[:])
                    last.then_inc(s["oTp"][b].sem, 1)
                for b in range(2):
                    pe.wait_ge(s["ol"][b].sem, s["ol"][b].now(i))
                    exact3(pe, bk[b][1][:], lambda c: oh[b][:, c, :], lambda c: ol[b][:, c, :],
                           lambda c: wh[:, c, :], lambda c: wl[:, c, :]).then_inc(s["o"][b].sem, 1)
                for b in range(2):
                    pe.wait_ge(s["x3"][b].sem, s["x3"][b].now(i))
                    for c in range(KC):
                        last = pe.transpose(bk[b][2][:, c * P:(c + 1) * P], r[b][:, c * P:(c + 1) * P], ident[:])
                    last.then_inc(s["x3Tp"][b].sem, 1)
    ph.end()
    top.close()


def route(nc, K, bank, a, comb, xh, xl):
    N = B * NT
    ph = Phase(nc, "route")
    gh, gl, gf = ph.sb("gh", [P, KC, MOE_E], F32R), ph.sb("gl", [P, KC, MOE_E], F32R), ph.sb("gf", [P, KC * MOE_E])
    bias = ph.sb("bias", [P, MOE_E])
    low4, low16 = ph.sb("low4", [P, 16]), ph.sb("low16", [P, MOE_E * MOE_E])
    sc, sfc = ph.sb("sc", [P, N, MOE_E]), ph.sb("sfc", [P, N, MOE_E])
    pairs, gs = ph.sb("pairs", [P, N * MOE_G, 6]), ph.sb("gs", [P, N, MOE_G])
    c1, c2 = ph.sb("c1", [P, N, MOE_E, MOE_E]), ph.sb("c2", [P, N, MOE_E, MOE_E])
    rank, sel, tot, inv = ph.sb("rank", [P, N, MOE_E]), ph.sb("sel", [P, N, MOE_E]), ph.sb("tot", [P, N]), ph.sb("inv", [P, N])
    landed, lead, trail, logits, scored, chain = (nc.alloc_semaphore(name=f"route_{n}") for n in
                                                  ("landed", "lead", "trail", "logits", "scored", "chain"))
    with nc.Block() as block:
        @block.sync
        def _(sp):
            for dst, src in ((gf, a["gate_w"]), (bias, a["gate_b"]), (low4, K["low4"]), (low16, K["low16"])):
                sp.dma_start(dst[:], src).then_inc(landed, 16)

        @block.scalar
        def _(act):
            act.wait_ge(logits, 1)
            nc.scalar.activation(sc[:].rearrange("p n e -> p (n e)"), bank[0][:, 0:N * MOE_E], ACT.Sigmoid).then_inc(scored, 1)

        @block.tensor
        def _(pe):
            pe.wait_ge(trail, 1)
            for n in range(N):
                last = exact3(pe, bank[0][:, n * MOE_E:(n + 1) * MOE_E], lambda c: xh[:, c, n * P:(n + 1) * P],
                              lambda c: xl[:, c, n * P:(n + 1) * P], lambda c: gh[:, c, :], lambda c: gl[:, c, :])
            last.then_inc(logits, 1)

        @block.vector
        def _(dve):
            count = [0]

            def link(ins):
                count[0] += 1
                ins.then_inc(chain, 1)
                dve.wait_ge(chain, count[0])
            dve.wait_ge(landed, 64)
            flat = "p c e -> p (c e)"
            nc.vector.tensor_copy(gh[:].rearrange(flat), gf[:]).then_inc(lead, 1)
            dve.wait_ge(lead, 1)
            nc.vector.tensor_tensor(gl[:].rearrange(flat), gf[:], gh[:].bitcast(F32).rearrange(flat), ALU.subtract).then_inc(trail, 1)
            nc.vector.memset(comb[:, MOE_E:], 1.0)
            dve.wait_ge(scored, 1)
            link(nc.vector.tensor_tensor(sfc[:], sc[:], bias[:].unsqueeze(1).to_broadcast([P, N, MOE_E]), ALU.add))
            v = sfc[:].rearrange("p n (g k) -> p (n g) k", g=MOE_G)
            nc.vector.tensor_tensor(pairs[:, :, 0:3], v[:, :, 0:3], v[:, :, 1:4], ALU.add)
            nc.vector.tensor_tensor(pairs[:, :, 3:5], v[:, :, 0:2], v[:, :, 2:4], ALU.add)
            link(nc.vector.tensor_tensor(pairs[:, :, 5:6], v[:, :, 0:1], v[:, :, 3:4], ALU.add))
            link(nc.vector.tensor_reduce(gs[:].rearrange("p n g -> p (n g)"), pairs[:], AX, ALU.max))

            def ranked(vals, m, lower):
                shape = [P, N, m, m]
                others, own = vals.unsqueeze(2).to_broadcast(shape), vals.unsqueeze(3).to_broadcast(shape)
                a1 = c1[:].rearrange("p n e f -> p (n e f)")[:, 0:N * m * m].rearrange("p (n e f) -> p n e f", n=N, e=m)
                a2 = c2[:].rearrange("p n e f -> p (n e f)")[:, 0:N * m * m].rearrange("p (n e f) -> p n e f", n=N, e=m)
                link(nc.vector.tensor_tensor(a1, others, own, ALU.is_equal))
                link(nc.vector.tensor_tensor(a1.rearrange("p n e f -> p n (e f)"), a1.rearrange("p n e f -> p n (e f)"),
                                             lower[:].unsqueeze(1).to_broadcast([P, N, m * m]), ALU.mult))
                link(nc.vector.tensor_tensor(a2, others, own, ALU.is_gt))
                link(nc.vector.tensor_tensor(a1, a1, a2, ALU.add))
                link(nc.vector.tensor_reduce(rank[:].rearrange("p n e -> p (n e)")[:, 0:N * m].rearrange("p (n e) -> p n e", n=N), a1, AX, ALU.add))

            ranked(gs[:], MOE_G, low4)
            g_rank = rank[:].rearrange("p n e -> p (n e)")[:, 0:N * MOE_G]
            link(nc.vector.tensor_scalar(gs[:].rearrange("p n g -> p (n g)"), g_rank, 1.5, None, ALU.is_lt))
            g_sel = gs[:].rearrange("p n g -> p (n g)").unsqueeze(2).to_broadcast([P, N * MOE_G, MOE_E // MOE_G])
            link(nc.vector.tensor_tensor(v, v, g_sel, ALU.mult))
            ranked(sfc[:], MOE_E, low16)
            link(nc.vector.tensor_scalar(sel[:], rank[:], 5.5, None, ALU.is_lt))
            link(nc.vector.tensor_tensor(sel[:], sel[:], sc[:], ALU.mult))
            link(nc.vector.tensor_reduce(tot[:], sel[:], AX, ALU.add))
            link(nc.vector.tensor_scalar(tot[:], tot[:], 1e-20, None, ALU.add))
            link(nc.vector.reciprocal(inv[:], tot[:]))
            link(nc.vector.tensor_scalar(inv[:], inv[:], 2.5, None, ALU.mult))
            link(nc.vector.tensor_tensor(comb[:, 0:MOE_E].rearrange("p e n -> p n e"), sel[:],
                                         inv[:].unsqueeze(2).to_broadcast([P, N, MOE_E]), ALU.mult))
    nc.clear_and_free_semaphores([landed, lead, trail, logits, scored, chain])
    nc.all_engine_barrier()
    ph.stack.close()


def experts(nc, K, bank, a):
    N, NE, NB = B * NT, MOE_E + 2, 4
    TB = N * P // NB
    top = ExitStack()
    xh = top.enter_context(nc.sbuf_tensor("moe_xh", [P, KC, N * P], F32R))
    xl = top.enter_context(nc.sbuf_tensor("moe_xl", [P, KC, N * P], F32R))
    comb = top.enter_context(nc.sbuf_tensor("moe_comb", [P, NE, N], F32))
    load_split(nc, "moe_x", [(a["x3T"][n * P:(n + 1) * P, :], xh[:, :, n * P:(n + 1) * P], xl[:, :, n * P:(n + 1) * P])
                             for n in range(N)], stage_cols=D)
    route(nc, K, bank, a, comb, xh, xl)
    ph = Phase(nc, "moe")
    acc = ph.sb("acc", [P, N, D])
    GU, DN = 2 * KC * MOE_I, 3 * D
    guf, guh, gul = ph.sb("guf", [P, GU]), ph.sb("guh", [P, 2, KC, MOE_I], F32R), ph.sb("gul", [P, 2, KC, MOE_I], F32R)
    dnf, dnh, dnl = ph.sb("dnf", [P, DN]), ph.sb("dnh", [P, 3, D], F32R), ph.sb("dnl", [P, 3, D], F32R)
    ih, il = ph.sb("ih", [P, 3, N * P], F32R), ph.sb("il", [P, 3, N * P], F32R)
    sil = ph.sb2("sil", [P, TB])
    NH = 3 * NB
    s = {n: ph.counter(n, per) for n, per in
         [("acc_in", 16), ("gu_in", 16), ("dn_in", 16), ("guh", 1), ("gul", 1), ("dnh", 1), ("dnl", 1), ("gu", NH), ("sil", NH), ("prod", NH),
          ("ih", NH), ("il", NH), ("dn", N), ("acc", N)]}
    with nc.Block() as block:
        @block.sync
        def _(sp):
            sp.dma_start(acc[:], a["x3"].rearrange("(n p) d -> p n d", p=P)).then_inc(s["acc_in"].sem, 16)
            with sp.Fori(1, NE + 1) as i:
                sp.wait_ge(s["gul"].sem, s["gul"].last(i))
                sp.wait_ge(s["guh"].sem, s["guh"].last(i))
                sp.dma_start(guf[:], a["GU"][bass.ds((i - 1) * P, P), :]).then_inc(s["gu_in"].sem, 16)
                sp.wait_ge(s["dnl"].sem, s["dnl"].last(i))
                sp.wait_ge(s["dnh"].sem, s["dnh"].last(i))
                sp.dma_start(dnf[:], a["DN"][bass.ds((i - 1) * P, P), :]).then_inc(s["dn_in"].sem, 16)

        @block.gpsimd
        def _(pool):
            ph.credit(pool)

        def hidden():
            k = 0
            for blk in range(NB):
                for c, (at_, m) in enumerate(ICH):
                    yield k, blk, c, at_, m
                    k += 1

        @block.scalar
        def _(act):
            with act.Fori(1, NE + 1) as i:
                act.wait_ge(s["gu_in"].sem, s["gu_in"].now(i))
                act.wait_ge(s["gu"].sem, s["gu"].part(i, 0))
                nc.scalar.copy(guh[:].rearrange("p a c n -> p (a c n)"), guf[:]).then_inc(s["guh"].sem, 1)
                for k, blk, c, o, m in hidden():
                    act.wait_ge(s["gu"].sem, s["gu"].part(i, k + 1))
                    act.wait_ge(s["il"].sem, s["il"].part(i, k - 1))
                    nc.scalar.activation(sil[k % 2][0:m], bank[2 * (k % 3)][0:m, :], ACT.Silu).then_inc(s["sil"].sem, 1)
                    act.wait_ge(s["prod"].sem, s["prod"].part(i, k + 1))
                    act.wait_ge(s["dn"].sem, s["dn"].part(i, 0))
                    nc.scalar.copy(ih[0:m, c, blk * TB:(blk + 1) * TB], sil[k % 2][0:m]).then_inc(s["ih"].sem, 1)
                    if k == 1:
                        act.wait_ge(s["dn_in"].sem, s["dn_in"].now(i))
                        nc.scalar.copy(dnh[:].rearrange("p c n -> p (c n)"), dnf[:]).then_inc(s["dnh"].sem, 1)

        @block.vector
        def _(dve):
            dve.wait_ge(s["acc_in"].sem, s["acc_in"].now(1))
            with dve.Fori(1, NE + 1) as i:
                dve.wait_ge(s["guh"].sem, s["guh"].now(i))
                nc.vector.tensor_tensor(gul[:].rearrange("p a c n -> p (a c n)"), guf[:],
                                        guh[:].bitcast(F32).rearrange("p a c n -> p (a c n)"), ALU.subtract).then_inc(s["gul"].sem, 1)
                for k, blk, c, o, m in hidden():
                    dve.wait_ge(s["sil"].sem, s["sil"].part(i, k + 1))
                    nc.vector.tensor_tensor(sil[k % 2][0:m], sil[k % 2][0:m], bank[2 * (k % 3) + 1][0:m, :], ALU.mult).then_inc(s["prod"].sem, 1)
                    dve.wait_ge(s["ih"].sem, s["ih"].part(i, k + 1))
                    nc.vector.tensor_tensor(il[0:m, c, blk * TB:(blk + 1) * TB], sil[k % 2][0:m],
                                            ih[0:m, c, blk * TB:(blk + 1) * TB].bitcast(F32), ALU.subtract).then_inc(s["il"].sem, 1)
                    if k == 1:
                        dve.wait_ge(s["dnh"].sem, s["dnh"].now(i))
                        nc.vector.tensor_tensor(dnl[:].rearrange("p c n -> p (c n)"), dnf[:],
                                                dnh[:].bitcast(F32).rearrange("p c n -> p (c n)"), ALU.subtract).then_inc(s["dnl"].sem, 1)
                for n in range(N):
                    dve.wait_ge(s["dn"].sem, s["dn"].part(i, n + 1))
                    dve.wait_ge(s["acc"].sem, s["acc"].part(i, n + 1 - N))
                    nc.vector.scalar_tensor_tensor(acc[:, n], bank[6 + n % 2][:], comb[:, bass.ds(i - 1, 1), n], acc[:, n],
                                                   ALU.mult, ALU.add).then_inc(s["acc"].sem, 1)
            dve.wait_ge(s["acc"].sem, s["acc"].now(NE))

        @block.tensor
        def _(pe):
            with pe.Fori(1, NE + 1) as i:
                pe.wait_ge(s["gul"].sem, s["gul"].now(i))
                for k, blk, c, o, m in hidden():
                    pe.wait_ge(s["prod"].sem, s["prod"].part(i, k - 2))
                    for u in range(2):
                        last = exact3(pe, bank[2 * (k % 3) + u][0:m, :], lambda q: guh[:, u, q, o:o + m], lambda q: gul[:, u, q, o:o + m],
                                      lambda q: xh[:, q, blk * TB:(blk + 1) * TB], lambda q: xl[:, q, blk * TB:(blk + 1) * TB])
                    last.then_inc(s["gu"].sem, 1)
                pe.wait_ge(s["dnl"].sem, s["dnl"].now(i))
                for n in range(N):
                    pe.wait_ge(s["il"].sem, s["il"].part(i, 3 * (n * P // TB + 1)))
                    pe.wait_ge(s["acc"].sem, s["acc"].part(i, n - 1))
                    t = slice(n * P, (n + 1) * P)
                    for c, (o, m) in enumerate(ICH):
                        last = exact3(pe, bank[6 + n % 2][:], lambda q: ih[0:m, c, t], lambda q: il[0:m, c, t],
                                      lambda q: dnh[0:m, c, :], lambda q: dnl[0:m, c, :], start=(c == 0), stop=(c == 2), n=1)
                    last.then_inc(s["dn"].sem, 1)
    nc.clear_and_free_semaphores([x.sem for x in ph.counters])
    nc.all_engine_barrier()

    st, mv, rs, eps = ph.sb("st", [P, N, 6]), ph.sb("mv", [P, N, 2]), ph.sb("rs", [P, 2, N]), ph.sb("eps", [P, 1])
    stats, root, inv, done, stored = (nc.alloc_semaphore(name=f"last_{n}") for n in ("stats", "root", "inv", "done", "stored"))
    with nc.Block() as block:
        @block.vector
        def _(dve):
            nc.vector.memset(eps[:], 1e-5)
            for n in range(N):
                nc.vector.bn_stats(st[:, n], acc[:, n]).then_inc(stats, 1)
            dve.wait_ge(stats, N)
            for n in range(N):
                nc.vector.bn_aggr(mv[:, n], st[:, n]).then_inc(stats, 1)
            dve.wait_ge(root, 1)
            nc.vector.reciprocal(rs[:, 1], rs[:, 0]).then_inc(inv, 1)
            dve.wait_ge(inv, 1)
            for n in range(N):
                nc.vector.tensor_scalar(acc[:, n], acc[:, n], mv[:, n, 0:1], rs[:, 1, n:n + 1], ALU.subtract, ALU.mult).then_inc(done, 1)

        @block.scalar
        def _(act):
            act.wait_ge(stats, 2 * N)
            nc.scalar.activation(rs[:, 0], mv[:, :, 1], ACT.Sqrt, bias=eps[:, 0:1]).then_inc(root, 1)

        @block.sync
        def _(sp):
            for n in range(N):
                sp.wait_ge(done, n + 1)
                i, b = n // B, n % B
                sp.dma_start(a["out"][b, i * P:(i + 1) * P, :], acc[:, n]).then_inc(stored, 16)
            sp.wait_ge(stored, 16 * N)
    ph.stack.close()
    top.close()


def shape_constants():
    tok = np.arange(P)
    sub, mid = tok // SUB, (tok // SUB) * SUB + SUB // 2 - 1
    src, dst = tok[:, None], tok[None, :]
    same = sub[:, None] == sub[None, :]
    m = mid[None, :]
    cum = same * (((src > m) & (src <= dst)) * 1.0 - ((src > dst) & (src <= m)) * 1.0)
    edges = [-1, *(np.arange(NSUB) * SUB + SUB // 2 - 1), P - 1]
    sel = np.stack([(tok > lo) & (tok <= hi) for lo, hi in zip(edges[:-1], edges[1:])], 1)
    return {
        "ident": np.eye(P),
        "cum": cum,
        "sel": sel,
        "causal": same & (src <= dst),
        "tri": ((tok[:, None] // TTT) % HG == tok[None, :HG * TTT] // TTT) & (tok[:, None] % TTT <= tok[None, :HG * TTT] % TTT),
        "seq": tok[:, None] // (HG * TTT) == np.arange(2)[None, :],
        "low4": np.broadcast_to(np.tri(MOE_G, k=-1).reshape(1, -1), (P, MOE_G ** 2)),
        "low16": np.broadcast_to(np.tri(MOE_E, k=-1).reshape(1, -1), (P, MOE_E ** 2)),
        "own": tok[:, None] // DH == np.arange(HG)[None, :],
        "order": np.broadcast_to(np.arange(EXPERTS), (P, EXPERTS)),
        "heads": (tok[:, None] // DH) == (tok[None, :] // DH),
    }


def by_feature(w):
    n = w.shape[0] // P
    return np.ascontiguousarray(w.reshape(n, P, -1).transpose(1, 0, 2).reshape(P, -1))


def layout(x):
    x = {k: np.asarray(v) for k, v in x.items()}
    tok = x["L0_attn_x"].reshape(B, NT, P, D).transpose(1, 0, 2, 3)
    a = {"x": tok.reshape(-1, D)}
    a["xT"] = tok.reshape(NT, B, P, KC, P).transpose(0, 1, 4, 3, 2).reshape(-1, D)
    for n in ("Wq", "Wk", "Wv", "Wg", "Wo"):
        a[n] = by_feature(x[f"L0_attn_{n}"].T)
    for n in ("gamma", "beta"):
        a[n] = x[f"L0_attn_{n}"].reshape(KC, P).T
    def on_all(v):
        return np.broadcast_to(v, (P, v.size))
    a["base"] = by_feature(x["L0_ffn_base_w"].T)
    a["base_b"], a["router_b"] = on_all(x["L0_ffn_base_b"]), on_all(x["L0_ffn_router_b"])
    a["AR"] = by_feature(np.concatenate([x["L0_ffn_lora_A"].transpose(1, 0, 2).reshape(D, -1), x["L0_ffn_router_w"].T], 1))
    a["loraB"] = x["L0_ffn_lora_B"].reshape(EXPERTS * RANK, D)
    for n in ("Wq", "Wk", "Wv"):
        a[n + "3"] = by_feature(x[f"L1_attn_{n}"])
    a["Wo3"] = by_feature(x["L1_attn_Wo"])
    a["BG"] = by_feature(np.concatenate([x["L1_attn_Wbeta"], x["L1_attn_Wg1"]], 1))
    a["Wg2"] = x["L1_attn_Wg2"]
    for n in ("ln_w", "ln_b"):
        v = x[f"L1_attn_{n}"].reshape(KC, HG, DH).transpose(1, 0, 2).reshape(1, HG, 1, KC * DH)
        a[n] = np.broadcast_to(v, (B, HG, TTT, KC * DH)).reshape(P, KC * DH)
    for n in ("w", "b"):
        a[n + "_all"] = on_all(x["L1_attn_ln_" + n].reshape(KC, HG, DH).transpose(1, 0, 2).reshape(-1))
    a["gate_w"], a["gate_b"] = by_feature(x["L1_ffn_gate_weight"].T), on_all(x["L1_ffn_e_score_correction_bias"])
    f = "L1_ffn_"
    gu = [np.concatenate([x[f + n], x[f + "shared_" + m].reshape(2, MOE_I, D)]) for n, m in (("gate_proj", "gate_w"), ("up_proj", "up_w"))]
    gu = np.stack(gu, 1).reshape(-1, 2, MOE_I, KC, P)
    a["GU"] = gu.transpose(0, 4, 1, 3, 2).reshape(-1, 2 * KC * MOE_I)
    dn = np.concatenate([x[f + "down_proj"], x[f + "shared_down_w"].reshape(D, 2, MOE_I).transpose(1, 0, 2)]).transpose(0, 2, 1)
    dn = np.pad(dn, ((0, 0), (0, 3 * P - MOE_I), (0, 0))).reshape(-1, 3, P, D)
    a["DN"] = dn.transpose(0, 2, 1, 3).reshape(-1, 3 * D)
    a["norm_w"] = x["L1_attn_norm_w"].reshape(KC, P).T
    a = {k: np.ascontiguousarray(v) for k, v in a.items()}
    a.update({k: np.ascontiguousarray(v.astype(np.float32)) for k, v in shape_constants().items()})
    return a


def build(nc, a, out):
    N = B * L
    for name, cols in (("x1", D), ("x2", D), ("q3", D), ("qT", D), ("kT", D), ("te", H * (DH + 1)), ("sg", D), ("qh", D),
                       ("x3", D), ("x3T", D)):
        a[name] = nc.dram_tensor(f"mid_{name}", (N, cols), F32).ap()
    a["out"] = out
    with ExitStack() as ctx:
        bank = [ctx.enter_context(nc.psum_tensor(f"bank{k}", [P, D], F32)) for k in range(8)]
        gated_recurrence(nc, a, bank, a)
        lora_and_projections(nc, a, bank, a)
        ttt_recurrence(nc, a, bank, a)
        attention_output(nc, a, bank, a)
        experts(nc, a, bank, a)


def kernel(**inputs):
    import concourse.bacc as bacc
    from concourse.bass_utils import run_bass_kernel_spmd

    nc = bacc.Bacc("TRN2", target_bir_lowering=False, num_devices=1)
    arrays = layout(inputs)
    a = {n: nc.dram_tensor(f"in_{n}", v.shape, F32, kind="ExternalInput").ap() for n, v in arrays.items()}
    out = nc.dram_tensor("out", (B, L, D), F32, kind="ExternalOutput").ap()
    build(nc, a, out)
    r = run_bass_kernel_spmd(nc, [{f"in_{n}": v for n, v in arrays.items()}], core_ids=[0])
    return r.results[0]["out"]
```

```python
from contextlib import ExitStack

import numpy as np
import concourse.bass as bass
from concourse import mybir

ALU = mybir.AluOpType
ACT = mybir.ActivationFunctionType
F32 = mybir.dt.float32
F32R = mybir.dt.float32r
U32 = mybir.dt.uint32
AX = mybir.AxisListType.X

P = 128
B, L, D, H = 2, 1024, 512, 16
DH = D // H
KC = D // P
NT = L // P
HG = P // DH
SUB = 32
NSUB = P // SUB
EXPERTS, RANK = 8, 16
TTT = 16
NCH = P // TTT
MOE_E, MOE_I, MOE_G, TOP = 16, 352, 4, 6
NS = 2
SLOTS = 2 * P
FULL = (B * L * TOP + MOE_E * (SLOTS - 1)) // SLOTS
PAIRS = (FULL + 2) // 2
TILES = 2 * PAIRS + 2
NOWHERE = 1 << 16
ICH = [(0, 128), (128, 128), (256, 96)]


class Counter:

    def __init__(self, nc, name, per):
        self.sem, self.per = nc.alloc_semaphore(name=name), per

    def now(self, i):
        return i * self.per + self.per

    def last(self, i):
        return i * self.per

    def part(self, i, k):
        return i * self.per + k


class Phase:

    def __init__(self, nc, name):
        self.nc, self.name, self.counters, self.stack = nc, name, [], ExitStack()

    def counter(self, name, per=1):
        s = Counter(self.nc, f"{self.name}_{name}", per)
        self.counters.append(s)
        return s

    def counters_of_two(self, name, per=1):
        return [self.counter(f"{name}{b}", per) for b in range(2)]

    def sb(self, name, shape, dt=F32):
        return self.stack.enter_context(self.nc.sbuf_tensor(f"{self.name}_{name}", shape, dt))

    def sb2(self, name, shape, dt=F32):
        return [self.sb(f"{name}{b}", shape, dt) for b in range(2)]

    def credit(self, eng):
        for s in self.counters:
            eng.sem_inc(s.sem, s.per)

    def end(self):
        self.nc.clear_and_free_semaphores([s.sem for s in self.counters])
        self.nc.all_engine_barrier()
        self.stack.close()


def exact3(pe, out, hi, lo, whi, wlo, start=True, stop=True, n=KC):
    for c in range(n):
        pe.matmul(out, hi(c), whi(c), start=start and c == 0, stop=False, skip_group_check=True)
        pe.matmul(out, lo(c), whi(c), start=False, stop=False, skip_group_check=True)
        last = pe.matmul(out, hi(c), wlo(c), start=False, stop=stop and c == n - 1, skip_group_check=True)
    return last


def load_split(nc, name, parts, stage_cols=D * KC):
    stack = ExitStack()
    stage = [stack.enter_context(nc.sbuf_tensor(f"{name}_stage{k}", [P, stage_cols], F32)) for k in range(2)]
    landed = [nc.alloc_semaphore(name=f"{name}_landed{k}") for k in range(2)]
    leading = nc.alloc_semaphore(name=f"{name}_leading")
    trailing = nc.alloc_semaphore(name=f"{name}_trailing")

    def view(n, src, like):
        v = stage[n % 2][0:src.shape[0], 0:src.shape[1]]
        return v.rearrange("p (c t) -> p c t", c=like.shape[1]) if len(like.shape) == 3 else v

    with nc.Block() as block:
        @block.sync
        def _(sp):
            for n, (src, hi, lo) in enumerate(parts):
                if n >= 2:
                    sp.wait_ge(trailing, n - 1)
                sp.dma_start(stage[n % 2][0:src.shape[0], 0:src.shape[1]], src).then_inc(landed[n % 2], 16)

        @block.scalar
        def _(act):
            for n, (src, hi, lo) in enumerate(parts):
                act.wait_ge(landed[n % 2], 16 * (n // 2 + 1))
                nc.scalar.copy(hi, view(n, src, hi)).then_inc(leading, 1)

        @block.vector
        def _(dve):
            for n, (src, hi, lo) in enumerate(parts):
                dve.wait_ge(leading, n + 1)
                dve.wait_ge(landed[n % 2], 16 * (n // 2 + 1))
                nc.vector.tensor_tensor(lo, view(n, src, hi), hi.bitcast(F32),
                                        ALU.subtract).then_inc(trailing, 1)
            dve.wait_ge(trailing, len(parts))
    nc.clear_and_free_semaphores([*landed, leading, trailing])
    nc.all_engine_barrier()
    stack.close()


class Norm:

    def __init__(self, ph, name, b, eps):
        self.eps = eps
        self.st = ph.sb(f"{name}_st{b}", [P, 6])
        self.mv = ph.sb(f"{name}_mv{b}", [P, 2])
        self.w = ph.sb(f"{name}_w{b}", [P, 5])
        self.stat, self.mean, self.var, self.log, self.guess, self.n1, self.n2, self.rstd = (
            ph.counter(f"{name}_{n}{b}") for n in ("stat", "mean", "var", "log", "guess", "n1", "n2", "rstd"))

    def stats(self, nc, dve, i, src):
        nc.vector.bn_stats(self.st[:], src).then_inc(self.stat.sem, 1)
        dve.wait_ge(self.stat.sem, self.stat.now(i))
        nc.vector.memset(self.w[:, 0:1], 0.0)
        nc.vector.bn_aggr(self.mv[:], self.st[:]).then_inc(self.mean.sem, 1)
        dve.wait_ge(self.mean.sem, self.mean.now(i))
        nc.vector.tensor_scalar(self.w[:, 0:1], self.mv[:, 1:2], self.eps, None, ALU.add).then_inc(self.var.sem, 1)

    def guesses(self, nc, act, i):
        act.wait_ge(self.var.sem, self.var.now(i))
        nc.scalar.activation(self.w[:, 1:2], self.w[:, 0:1], ACT.Ln).then_inc(self.log.sem, 1)
        act.wait_ge(self.log.sem, self.log.now(i))
        nc.scalar.activation(self.w[:, 2:3], self.w[:, 1:2], ACT.Exp, scale=-0.5).then_inc(self.guess.sem, 1)

    def newton(self, nc, dve, i):
        dve.wait_ge(self.guess.sem, self.guess.now(i))
        nc.vector.scalar_tensor_tensor(self.w[:, 3:4], self.w[:, 2:3], self.w[:, 0:1], self.w[:, 2:3],
                                       ALU.mult, ALU.mult).then_inc(self.n1.sem, 1)
        dve.wait_ge(self.n1.sem, self.n1.now(i))
        nc.vector.tensor_scalar(self.w[:, 3:4], self.w[:, 3:4], -0.5, 1.5, ALU.mult, ALU.add).then_inc(self.n2.sem, 1)
        dve.wait_ge(self.n2.sem, self.n2.now(i))
        nc.vector.tensor_tensor(self.w[:, 4:5], self.w[:, 3:4], self.w[:, 2:3], ALU.mult).then_inc(self.rstd.sem, 1)
        dve.wait_ge(self.rstd.sem, self.rstd.now(i))

    def apply(self, nc, out, src):
        return nc.vector.tensor_scalar(out, src, self.mv[:, 0:1], self.w[:, 4:5], ALU.subtract, ALU.mult)


def gated_recurrence(nc, K, bank, a):
    top = ExitStack()
    names = ["Wg", "Wv", "Wq", "Wk", "Wo"]
    wh = {n: top.enter_context(nc.sbuf_tensor(f"gla_{n}_hi", [P, KC, D], F32R)) for n in names}
    wl = {n: top.enter_context(nc.sbuf_tensor(f"gla_{n}_lo", [P, KC, D], F32R)) for n in names}
    load_split(nc, "gla_w", [(a[n], wh[n][:].rearrange("p c n -> p (c n)"), wl[n][:].rearrange("p c n -> p (c n)"))
                             for n in names])
    ph = Phase(nc, "gla")
    PJ, BK = bank[0:4], bank[4:8]
    ident = ph.sb("ident", [P, P])
    cum = ph.sb("cum", [P, P])
    sel = ph.sb("sel", [P, NSUB + 1])
    causal = ph.sb("causal", [P, P])
    heads = ph.sb("heads", [P, P])
    gamma = ph.sb("gamma", [P, KC])
    beta = ph.sb("beta", [P, KC])
    xT, xTh, xTl = ph.sb2("xT", [P, KC, P]), ph.sb2("xTh", [P, KC, P], F32R), ph.sb2("xTl", [P, KC, P], F32R)
    xt, az, g = ph.sb2("xt", [P, D]), ph.sb2("az", [P, D]), ph.sb2("g", [P, D])
    eR, enR = ph.sb2("eR", [P, D]), ph.sb2("enR", [P, D])
    Qr, Kr, V = ph.sb2("Qr", [P, D]), ph.sb2("Kr", [P, D]), ph.sb2("V", [P, D])
    QT, KT = ph.sb2("QT", [P, KC, P]), ph.sb2("KT", [P, KC, P])
    Am = ph.sb2("Am", [P, HG, KC, P])
    kvm = ph.sb2("kvm", [P, KC, P])
    Sh = ph.sb2("Sh", [P, NSUB, KC, P])
    carry = ph.sb2("carry", [P, KC, P])
    decay = ph.sb2("decay", [P, KC, NSUB + 1])
    yTh, yTl = ph.sb2("yTh", [P, KC, P], F32R), ph.sb2("yTl", [P, KC, P], F32R)

    s = {}
    for n, per in [("xT_in", 16), ("xt_in", 16), ("xh", 1), ("xl", 1), ("z", 1), ("v", 1), ("q", 1), ("k", 1),
                   ("az", 1), ("ez", 1), ("lz", 1), ("g", 1), ("R", 1), ("eR", 1), ("enR", 1), ("decay", 1),
                   ("V", 1), ("Qr", 1), ("Kr", 1), ("QTp", 1), ("KTp", 1), ("QT", 1), ("KT", 1),
                   ("kv", NSUB), ("kvm", NSUB), ("sum", NSUB), ("Sh", NSUB + 1), ("A", HG), ("Am", HG),
                   ("y", 1), ("yn", 1), ("yTp", 1), ("yT", 1), ("yTh", 1), ("yTl", 1), ("o", 1), ("r", 1),
                   ("x1", 1), ("x1_out", 16)]:
        s[n] = ph.counters_of_two(n, per)
    n1 = [Norm(ph, "ny", b, 1e-5) for b in range(2)]
    n2 = [Norm(ph, "nx", b, 1e-5) for b in range(2)]
    consts = ph.counter("consts", 16 * 7)
    zeroed = ph.counter("zeroed", 2)

    def x1_rows(i, b):
        return a["x1"][bass.ds((i * 2 + (b - 2)) * P, P), :]

    with nc.Block() as block:
        @block.sync
        def _(sp):
            for t, src in ((ident, K["ident"]), (cum, K["cum"]), (sel, K["sel"]), (causal, K["causal"]),
                           (heads, K["heads"]), (gamma, a["gamma"]), (beta, a["beta"])):
                sp.dma_start(t[:], src).then_inc(consts.sem, 16)
            with sp.Fori(1, NT + 1) as i:
                for b in range(2):
                    sp.wait_ge(s["xh"][b].sem, s["xh"][b].last(i))
                    sp.wait_ge(s["xl"][b].sem, s["xl"][b].last(i))
                    row = (i * 2 + (b - 2)) * P
                    sp.dma_start(xT[b][:].rearrange("p c t -> p (c t)"), a["xT"][bass.ds(row, P), :]).then_inc(s["xT_in"][b].sem, 16)
                    sp.wait_ge(s["r"][b].sem, s["r"][b].last(i))
                    sp.dma_start(xt[b][:], a["x"][bass.ds(row, P), :]).then_inc(s["xt_in"][b].sem, 16)
            for b in range(2):
                sp.wait_ge(s["x1_out"][b].sem, s["x1_out"][b].now(NT))

        @block.gpsimd
        def _(pool):
            ph.credit(pool)
            for b in range(2):
                nc.gpsimd.memset(carry[b][:], 0.0).then_inc(zeroed.sem, 1)
            pool.wait_ge(zeroed.sem, 4)
            with pool.Fori(1, NT + 1) as i:
                for b in range(2):
                    def scale(out, in_, c, k):
                        nc.gpsimd.tensor_tensor(out, in_, decay[b][:, :, c:c + 1].to_broadcast([P, KC, P]),
                                                ALU.mult).then_inc(s["Sh"][b].sem, 1)
                    pool.wait_ge(s["decay"][b].sem, s["decay"][b].now(i))
                    pool.wait_ge(s["y"][b].sem, s["y"][b].last(i))
                    pool.wait_ge(s["Sh"][b].sem, s["Sh"][b].last(i))
                    scale(Sh[b][:, 0], carry[b][:], 0, 0)
                    for c in range(NSUB):
                        pool.wait_ge(s["Sh"][b].sem, s["Sh"][b].part(i, c + 1))
                        pool.wait_ge(s["kvm"][b].sem, s["kvm"][b].part(i, c + 1))
                        nc.gpsimd.tensor_tensor(kvm[b][:], kvm[b][:], Sh[b][:, c], ALU.add).then_inc(s["sum"][b].sem, 1)
                        pool.wait_ge(s["sum"][b].sem, s["sum"][b].part(i, c + 1))
                        scale(Sh[b][:, c + 1] if c < NSUB - 1 else carry[b][:], kvm[b][:], c + 1, c + 1)

        @block.scalar
        def _(act):
            act.wait_ge(consts.sem, consts.now(1))
            nc.scalar.preload_act_table_set("natural_log_exp_and_others")
            with act.Fori(1, NT + 1) as i:
                def gates(b):
                    act.wait_ge(s["z"][b].sem, s["z"][b].now(i))
                    nc.scalar.activation(az[b][:], PJ[0][:], ACT.Abs).then_inc(s["az"][b].sem, 1)
                    act.wait_ge(s["az"][b].sem, s["az"][b].now(i))
                    nc.scalar.activation(az[b][:], az[b][:], ACT.Exp, scale=-1.0).then_inc(s["ez"][b].sem, 1)
                    act.wait_ge(s["ez"][b].sem, s["ez"][b].now(i))
                    nc.scalar.activation(az[b][:], az[b][:], ACT.Ln, bias=1.0).then_inc(s["lz"][b].sem, 1)
                    act.wait_ge(s["v"][b].sem, s["v"][b].now(i))
                    act.wait_ge(s["y"][b].sem, s["y"][b].last(i))
                    nc.scalar.copy(V[b][:], PJ[1][:]).then_inc(s["V"][b].sem, 1)

                def decays(b):
                    act.wait_ge(s["R"][b].sem, s["R"][b].now(i))
                    act.wait_ge(s["yTp"][b].sem, s["yTp"][b].last(i))
                    nc.scalar.activation(eR[b][:], BK[0][:], ACT.Exp).then_inc(s["eR"][b].sem, 1)
                    act.wait_ge(s["yTl"][b].sem, s["yTl"][b].last(i))
                    nc.scalar.activation(enR[b][:], BK[0][:], ACT.Exp, scale=-1.0).then_inc(s["enR"][b].sem, 1)
                    act.wait_ge(s["Sh"][b].sem, s["Sh"][b].part(i, 0))
                    nc.scalar.activation(decay[b][:].rearrange("p c n -> p (c n)"), BK[1][:, 0:KC * (NSUB + 1)],
                                         ACT.Exp).then_inc(s["decay"][b].sem, 1)

                def turned(b):
                    act.wait_ge(s["QTp"][b].sem, s["QTp"][b].now(i))
                    act.wait_ge(s["y"][b].sem, s["y"][b].last(i))
                    nc.scalar.copy(QT[b][:].rearrange("p c t -> p (c t)"), BK[2][:]).then_inc(s["QT"][b].sem, 1)
                    act.wait_ge(s["KTp"][b].sem, s["KTp"][b].now(i))
                    nc.scalar.copy(KT[b][:].rearrange("p c t -> p (c t)"), BK[3][:]).then_inc(s["KT"][b].sem, 1)

                def scaled(b):
                    act.wait_ge(s["yTp"][b].sem, s["yTp"][b].now(i))
                    for c in range(KC):
                        last = nc.scalar.activation(enR[b][:, c * P:(c + 1) * P], BK[(0, 3)[b]][:, c * P:(c + 1) * P],
                                                    ACT.Identity, scale=gamma[:, c:c + 1], bias=beta[:, c:c + 1])
                    last.then_inc(s["yT"][b].sem, 1)

                gates(0)
                decays(0)
                gates(1)
                turned(0)
                decays(1)
                turned(1)
                n1[0].guesses(nc, act, i)
                scaled(0)
                n1[1].guesses(nc, act, i)
                n2[0].guesses(nc, act, i)
                scaled(1)
                n2[1].guesses(nc, act, i)
                for b in range(2):
                    act.wait_ge(s["x1"][b].sem, s["x1"][b].now(i))
                    act.dma_start(x1_rows(i, b), g[b][:]).then_inc(s["x1_out"][b].sem, 16)

        @block.vector
        def _(dve):
            dve.wait_ge(consts.sem, consts.now(1))
            with dve.Fori(1, NT + 1) as i:
                def split_x(b):
                    dve.wait_ge(s["xT_in"][b].sem, s["xT_in"][b].now(i))
                    dve.wait_ge(s["k"][b].sem, s["k"][b].last(i))
                    nc.vector.tensor_copy(xTh[b][:], xT[b][:]).then_inc(s["xh"][b].sem, 1)
                    dve.wait_ge(s["xh"][b].sem, s["xh"][b].now(i))
                    nc.vector.tensor_tensor(xTl[b][:], xT[b][:], xTh[b][:].bitcast(F32), ALU.subtract).then_inc(s["xl"][b].sem, 1)

                def gate(b):
                    dve.wait_ge(s["lz"][b].sem, s["lz"][b].now(i))
                    dve.wait_ge(s["x1_out"][b].sem, s["x1_out"][b].last(i))
                    nc.vector.scalar_tensor_tensor(g[b][:], PJ[0][:], 0.0, az[b][:], ALU.min, ALU.subtract).then_inc(s["g"][b].sem, 1)

                def decayed(b):
                    dve.wait_ge(s["q"][b].sem, s["q"][b].now(i))
                    dve.wait_ge(s["eR"][b].sem, s["eR"][b].now(i))
                    nc.vector.scalar_tensor_tensor(Qr[b][:], PJ[2][:], float(DH) ** -0.5, eR[b][:], ALU.mult, ALU.mult).then_inc(s["Qr"][b].sem, 1)
                    dve.wait_ge(s["k"][b].sem, s["k"][b].now(i))
                    dve.wait_ge(s["enR"][b].sem, s["enR"][b].now(i))
                    nc.vector.tensor_tensor(Kr[b][:], PJ[3][:], enR[b][:], ALU.mult).then_inc(s["Kr"][b].sem, 1)

                def states(b):
                    for c in range(NSUB):
                        dve.wait_ge(s["kv"][b].sem, s["kv"][b].part(i, c + 1))
                        dve.wait_ge(s["Sh"][b].sem, s["Sh"][b].part(i, c + 1))
                        nc.vector.tensor_tensor(kvm[b][:], BK[2 + c % 2][:].rearrange("p (c n) -> p c n", c=KC),
                                                heads[:].unsqueeze(1).to_broadcast([P, KC, P]), ALU.mult).then_inc(s["kvm"][b].sem, 1)

                def masked(b, banks):
                    for j in range(HG):
                        dve.wait_ge(s["A"][b].sem, s["A"][b].part(i, j + 1))
                        nc.vector.tensor_tensor(Am[b][:, j], BK[banks[j]][:].rearrange("p (c n) -> p c n", c=KC),
                                                causal[:].unsqueeze(1).to_broadcast([P, KC, P]), ALU.mult).then_inc(s["Am"][b].sem, 1)

                def norm_y(b):
                    dve.wait_ge(s["y"][b].sem, s["y"][b].now(i))
                    n1[b].stats(nc, dve, i, BK[(0, 1)[b]][:])
                    n1[b].newton(nc, dve, i)
                    n1[b].apply(nc, eR[b][:], BK[(0, 1)[b]][:]).then_inc(s["yn"][b].sem, 1)

                def split_y(b):
                    dve.wait_ge(s["yT"][b].sem, s["yT"][b].now(i))
                    nc.vector.tensor_copy(yTh[b][:].rearrange("p c t -> p (c t)"), enR[b][:]).then_inc(s["yTh"][b].sem, 1)
                    dve.wait_ge(s["yTh"][b].sem, s["yTh"][b].now(i))
                    nc.vector.tensor_tensor(yTl[b][:].rearrange("p c t -> p (c t)"), enR[b][:],
                                            yTh[b][:].bitcast(F32).rearrange("p c t -> p (c t)"), ALU.subtract).then_inc(s["yTl"][b].sem, 1)

                def norm_x(b):
                    dve.wait_ge(s["o"][b].sem, s["o"][b].now(i))
                    dve.wait_ge(s["xt_in"][b].sem, s["xt_in"][b].now(i))
                    dve.wait_ge(s["KTp"][b].sem, s["KTp"][b].now(i))
                    nc.vector.tensor_tensor(Qr[b][:], BK[(2, 1)[b]][:], xt[b][:], ALU.add).then_inc(s["r"][b].sem, 1)
                    dve.wait_ge(s["r"][b].sem, s["r"][b].now(i))
                    n2[b].stats(nc, dve, i, Qr[b][:])
                    n2[b].newton(nc, dve, i)
                    n2[b].apply(nc, g[b][:], Qr[b][:]).then_inc(s["x1"][b].sem, 1)

                split_x(0)
                split_x(1)
                gate(0)
                decayed(0)
                gate(1)
                decayed(1)
                states(0)
                masked(0, (0, 1, 0, 1))
                states(1)
                norm_y(0)
                masked(1, (1, 2, 3, 1))
                split_y(0)
                norm_y(1)
                norm_x(0)
                split_y(1)
                norm_x(1)

        @block.tensor
        def _(pe):
            pe.wait_ge(consts.sem, consts.now(1))
            with pe.Fori(1, NT + 1) as i:
                def project(b, name, m, used):
                    pe.wait_ge(s[used][1 - b].sem, s[used][1 - b].now(i) if b else s[used][1 - b].last(i))
                    exact3(pe, PJ[m][:], lambda c: xTh[b][:, c, :], lambda c: xTl[b][:, c, :],
                           lambda c: wh[name][:, c, :], lambda c: wl[name][:, c, :]).then_inc(s[("z", "v", "q", "k")[m]][b].sem, 1)

                def projections(b):
                    pe.wait_ge(s["xl"][b].sem, s["xl"][b].now(i))
                    project(b, "Wg", 0, "g")
                    project(b, "Wv", 1, "V")
                    project(b, "Wq", 2, "Qr")
                    project(b, "Wk", 3, "Kr")

                def log_decays(b):
                    pe.wait_ge(s["g"][b].sem, s["g"][b].now(i))
                    if b == 0:
                        pe.wait_ge(s["yT"][0].sem, s["yT"][0].last(i))
                        pe.wait_ge(s["r"][1].sem, s["r"][1].last(i))
                    else:
                        pe.wait_ge(s["enR"][0].sem, s["enR"][0].now(i))
                        pe.wait_ge(s["decay"][0].sem, s["decay"][0].now(i))
                    pe.matmul(BK[0][:], cum[:], g[b][:], start=True, stop=True)
                    for c in range(KC):
                        last = pe.matmul(BK[1][:, c * (NSUB + 1):(c + 1) * (NSUB + 1)], g[b][:, c * P:(c + 1) * P], sel[:],
                                         start=True, stop=True, skip_group_check=True)
                    last.then_inc(s["R"][b].sem, 1)

                def turn(b):
                    pe.wait_ge(s["Qr"][b].sem, s["Qr"][b].now(i))
                    if b == 0:
                        pe.wait_ge(s["r"][0].sem, s["r"][0].last(i))
                        pe.wait_ge(s["yT"][1].sem, s["yT"][1].last(i))
                    else:
                        pe.wait_ge(s["kvm"][0].sem, s["kvm"][0].part(i, NSUB))
                    for c in range(KC):
                        last = pe.transpose(BK[2][:, c * P:(c + 1) * P], Qr[b][:, c * P:(c + 1) * P], ident[:])
                    last.then_inc(s["QTp"][b].sem, 1)
                    pe.wait_ge(s["Kr"][b].sem, s["Kr"][b].now(i))
                    for c in range(KC):
                        last = pe.transpose(BK[3][:, c * P:(c + 1) * P], Kr[b][:, c * P:(c + 1) * P], ident[:])
                    last.then_inc(s["KTp"][b].sem, 1)

                def key_values(b):
                    pe.wait_ge(s["V"][b].sem, s["V"][b].now(i))
                    pe.wait_ge(s["KT"][b].sem, s["KT"][b].now(i))
                    pe.wait_ge(s["QT"][b].sem, s["QT"][b].now(i))
                    for c in range(NSUB):
                        if c >= 2:
                            pe.wait_ge(s["kvm"][b].sem, s["kvm"][b].part(i, c - 1))
                        for m in range(KC):
                            last = pe.matmul(BK[2 + c % 2][:, m * P:(m + 1) * P],
                                             Kr[b][c * SUB:(c + 1) * SUB, m * P:(m + 1) * P],
                                             V[b][c * SUB:(c + 1) * SUB, m * P:(m + 1) * P], start=True, stop=True,
                                             skip_group_check=True)
                        last.then_inc(s["kv"][b].sem, 1)

                def scores(b, banks, free):
                    pe.wait_ge(s["KT"][b].sem, s["KT"][b].now(i))
                    for j in range(HG):
                        free(j)
                        for m in range(KC):
                            last = pe.matmul(BK[banks[j]][:, m * P:(m + 1) * P], KT[b][j * DH:(j + 1) * DH, m, :],
                                             QT[b][j * DH:(j + 1) * DH, m, :], start=True, stop=True, skip_group_check=True)
                        last.then_inc(s["A"][b].sem, 1)

                def free_0(j):
                    if j == 0:
                        pe.wait_ge(s["enR"][1].sem, s["enR"][1].now(i))
                    if j == 1:
                        pe.wait_ge(s["decay"][1].sem, s["decay"][1].now(i))
                    if j >= 2:
                        pe.wait_ge(s["Am"][0].sem, s["Am"][0].part(i, j - 1))

                def free_1(j):
                    if j == 0:
                        pe.wait_ge(s["Am"][0].sem, s["Am"][0].part(i, 4))
                    if j == 1:
                        pe.wait_ge(s["kvm"][1].sem, s["kvm"][1].part(i, 3))
                    if j == 2:
                        pe.wait_ge(s["kvm"][1].sem, s["kvm"][1].part(i, 4))
                    if j == 3:
                        pe.wait_ge(s["Am"][1].sem, s["Am"][1].part(i, 1))

                def outputs(b):
                    bk = BK[(0, 1)[b]]
                    pe.wait_ge(s["Am"][b].sem, s["Am"][b].part(i, HG))
                    for m in range(KC):
                        for j in range(HG):
                            h = m * HG + j
                            pe.matmul(bk[:, h * DH:(h + 1) * DH], Am[b][:, j, m, :], V[b][:, h * DH:(h + 1) * DH],
                                      start=(h == 0), stop=False, skip_group_check=True)
                    pe.wait_ge(s["Sh"][b].sem, s["Sh"][b].part(i, NSUB))
                    for c in range(NSUB):
                        for m in range(KC):
                            last = pe.matmul(bk[c * SUB:(c + 1) * SUB, m * P:(m + 1) * P],
                                             QT[b][:, m, c * SUB:(c + 1) * SUB], Sh[b][:, c, m, :],
                                             start=False, stop=(m == KC - 1), skip_group_check=True)
                    last.then_inc(s["y"][b].sem, 1)

                def turn_y(b):
                    pe.wait_ge(s["yn"][b].sem, s["yn"][b].now(i))
                    if b == 1:
                        pe.wait_ge(s["Am"][1].sem, s["Am"][1].part(i, 3))
                    for c in range(KC):
                        last = pe.transpose(BK[(0, 3)[b]][:, c * P:(c + 1) * P], eR[b][:, c * P:(c + 1) * P], ident[:])
                    last.then_inc(s["yTp"][b].sem, 1)

                def out_proj(b):
                    pe.wait_ge(s["yTl"][b].sem, s["yTl"][b].now(i))
                    if b == 0:
                        pe.wait_ge(s["Am"][1].sem, s["Am"][1].part(i, 2))
                    exact3(pe, BK[(2, 1)[b]][:], lambda c: yTh[b][:, c, :], lambda c: yTl[b][:, c, :],
                           lambda c: wh["Wo"][:, c, :], lambda c: wl["Wo"][:, c, :]).then_inc(s["o"][b].sem, 1)

                projections(0)
                log_decays(0)
                projections(1)
                turn(0)
                log_decays(1)
                key_values(0)
                scores(0, (0, 1, 0, 1), free_0)
                turn(1)
                outputs(0)
                key_values(1)
                scores(1, (1, 2, 3, 1), free_1)
                turn_y(0)
                out_proj(0)
                outputs(1)
                turn_y(1)
                out_proj(1)
    ph.end()
    top.close()


def by_chunk(t):
    return t.rearrange("p (g j d) -> p g j d", g=KC, j=HG)


def heads_of(t):
    return t.rearrange("p (h d) -> p h d", h=H)


def lora_and_projections(nc, K, bank, a):
    top = ExitStack()
    wide = {"base": D, "Wq3": D, "Wk3": D, "Wv3": D, "AR": EXPERTS * RANK + EXPERTS, "BG": H + DH}
    wh = {n: top.enter_context(nc.sbuf_tensor(f"ffn_{n}_hi", [P, KC, w], F32R)) for n, w in wide.items()}
    wl = {n: top.enter_context(nc.sbuf_tensor(f"ffn_{n}_lo", [P, KC, w], F32R)) for n, w in wide.items()}
    lbh = top.enter_context(nc.sbuf_tensor("ffn_loraB_hi", [P, D], F32R))
    lbl = top.enter_context(nc.sbuf_tensor("ffn_loraB_lo", [P, D], F32R))
    load_split(nc, "ffn_w", [(a[n], wh[n][:].rearrange("p c n -> p (c n)"), wl[n][:].rearrange("p c n -> p (c n)"))
                             for n in wide] + [(a["loraB"], lbh[:], lbl[:])])
    ph = Phase(nc, "ffn")
    bk = [bank[0:4], bank[4:8]]
    ident = ph.sb("ident", [P, P])
    base_b, router_b = ph.sb("base_b", [P, D]), ph.sb("router_b", [P, EXPERTS])
    order = ph.sb("order", [P, EXPERTS])
    wg2 = ph.sb("wg2", [DH, D])
    x1, xb = ph.sb2("x1", [P, D]), ph.sb2("xb", [P, D])
    xh, xl = ph.sb2("xh", [P, KC, P], F32R), ph.sb2("xl", [P, KC, P], F32R)
    lg, top8 = ph.sb2("lg", [P, EXPERTS]), ph.sb2("top8", [P, 8])
    idx, idf = ph.sb2("idx", [P, 8], U32), ph.sb2("idf", [P, 8])
    mask, ex, tot, neg = ph.sb2("mask", [P, EXPERTS]), ph.sb2("ex", [P, EXPERTS]), ph.sb2("tot", [P, 2]), ph.sb2("neg", [P, 1])
    mid, mh, ml = ph.sb2("mid", [P, P]), ph.sb2("mh", [P, P], F32R), ph.sb2("ml", [P, P], F32R)
    x2 = ph.sb2("x2", [P, D])
    q3, kn, sq, sg = ph.sb2("q3", [P, D]), ph.sb2("kn", [P, D]), ph.sb2("sq", [P, D]), ph.sb2("sg", [P, D])
    kw = ph.sb2("kw", [P, 6, H])
    te = ph.sb2("te", [P, HG, KC, DH + 1])
    g1, g1T = ph.sb2("g1", [P, DH]), ph.sb2("g1T", [DH, P])
    qT, kT = ph.sb2("qT", [P, D]), ph.sb2("kT", [P, D])
    s = {}
    for n, per in [("x1_in", 16), ("xb", 1), ("x1T", 1), ("x1h", 1), ("x1l", 1), ("lm", 1), ("lg", 1), ("top", 1),
                   ("idx", 1), ("idf", 1), ("m1", 1), ("mask", 1), ("neg", 1), ("ex", 1), ("em", 1), ("tot", 1), ("inv", 1),
                   ("gate", 1), ("mid", 1), ("midT", 1), ("mh", 1), ("ml", 1), ("ffn", 1), ("r", 1), ("x2", 1),
                   ("x2T", 1), ("x2h", 1), ("x2l", 1), ("bg", 1), ("q", 1), ("k", 1), ("v", 1), ("q3", 1), ("eta", 1),
                   ("sq", 1), ("ss", 1), ("kn1", 1), ("kn2", 1), ("kn3", 1), ("kn4", 1), ("m1b", 1), ("m2b", 1), ("kr", 1), ("kn", 1), ("te", 1),
                   ("eta2", 1), ("qTp", 1), ("kTp", 1), ("qT", 1), ("kT", 1), ("g1", 1), ("g1Tp", 1), ("g1T", 1), ("gt", 1), ("sg", 1),
                   ("stored", 16 * 6)]:
        s[n] = ph.counters_of_two(n, per)
    nx = [Norm(ph, "nx", b, 1e-5) for b in range(2)]
    consts = ph.counter("consts", 16 * 5)

    with nc.Block() as block:
        def rows(name, i, b):
            return a[name][bass.ds((i * 2 + (b - 2)) * P, P), :]

        @block.sync
        def _(sp):
            for t, src in ((ident, K["ident"]), (base_b, a["base_b"]), (router_b, a["router_b"]), (order, K["order"]),
                           (wg2, a["Wg2"])):
                sp.dma_start(t[:], src).then_inc(consts.sem, 16)
            with sp.Fori(1, NT + 1) as i:
                for b in range(2):
                    sp.wait_ge(s["x1T"][b].sem, s["x1T"][b].last(i))
                    sp.wait_ge(s["xb"][b].sem, s["xb"][b].last(i))
                    sp.dma_start(x1[b][:], rows("x1", i, b)).then_inc(s["x1_in"][b].sem, 16)
                for b in range(2):
                    for made, buf, name in (("x2", x2, "x2"), ("q3", q3, "q3"), ("qT", qT, "qT"), ("kT", kT, "kT")):
                        sp.wait_ge(s[made][b].sem, s[made][b].now(i))
                        sp.dma_start(rows(name, i, b), buf[b][:]).then_inc(s["stored"][b].sem, 16)
                    sp.wait_ge(s["te"][b].sem, s["te"][b].now(i))
                    sp.wait_ge(s["eta2"][b].sem, s["eta2"][b].now(i))
                    sp.dma_start(rows("te", i, b), te[b][:].rearrange("p j g d -> p (j g d)")).then_inc(s["stored"][b].sem, 16)
                    sp.wait_ge(s["sg"][b].sem, s["sg"][b].now(i))
                    sp.dma_start(rows("sg", i, b), sg[b][:]).then_inc(s["stored"][b].sem, 16)
            for b in range(2):
                sp.wait_ge(s["stored"][b].sem, s["stored"][b].now(NT))

        @block.gpsimd
        def _(pool):
            ph.credit(pool)
            pool.wait_ge(consts.sem, consts.now(1))
            with pool.Fori(1, NT + 1) as i:
                for b in range(2):
                    pool.wait_ge(s["x1_in"][b].sem, s["x1_in"][b].now(i))
                    pool.wait_ge(s["r"][b].sem, s["r"][b].last(i))
                    nc.gpsimd.tensor_tensor(xb[b][:], x1[b][:], base_b[:], ALU.add).then_inc(s["xb"][b].sem, 1)
                for b in range(2):
                    pool.wait_ge(s["eta"][b].sem, s["eta"][b].now(i))
                    sig = kw[b][:, 5].rearrange("p (g j) -> p g j", g=KC)
                    pool.wait_ge(s["stored"][b].sem, s["stored"][b].last(i))
                    nc.gpsimd.tensor_tensor(te[b][:, :, :, DH].rearrange("p j g -> p g j"), sig, sig,
                                            ALU.add).then_inc(s["eta2"][b].sem, 1)

        @block.scalar
        def _(act):
            act.wait_ge(consts.sem, consts.now(1))
            with act.Fori(1, NT + 1) as i:
                def lead_x1(b):
                    act.wait_ge(s["x1T"][b].sem, s["x1T"][b].now(i))
                    nc.scalar.copy(xh[b][:].rearrange("p c t -> p (c t)"), bk[b][0][:]).then_inc(s["x1h"][b].sem, 1)

                def soft(b):
                    act.wait_ge(s["neg"][b].sem, s["neg"][b].now(i))
                    nc.scalar.activation(ex[b][:], lg[b][:], ACT.Exp, bias=neg[b][:, 0:1]).then_inc(s["ex"][b].sem, 1)

                def lead_mid(b):
                    act.wait_ge(s["midT"][b].sem, s["midT"][b].now(i))
                    nc.scalar.copy(mh[b][:], bk[b][3][:, 0:P]).then_inc(s["mh"][b].sem, 1)

                def lead_x2(b):
                    act.wait_ge(s["x2T"][b].sem, s["x2T"][b].now(i))
                    nc.scalar.copy(xh[b][:].rearrange("p c t -> p (c t)"), bk[b][0][:]).then_inc(s["x2h"][b].sem, 1)

                def squares(b):
                    act.wait_ge(s["bg"][b].sem, s["bg"][b].now(i))
                    nc.scalar.copy(g1[b][:], bk[b][1][:, H:H + DH]).then_inc(s["g1"][b].sem, 1)
                    act.wait_ge(s["k"][b].sem, s["k"][b].now(i))
                    nc.scalar.activation(sq[b][:], bk[b][3][:], ACT.Square).then_inc(s["sq"][b].sem, 1)
                    act.wait_ge(s["kn1"][b].sem, s["kn1"][b].now(i))
                    nc.scalar.activation(kw[b][:, 1], kw[b][:, 0], ACT.Ln).then_inc(s["kn2"][b].sem, 1)
                    act.wait_ge(s["kn2"][b].sem, s["kn2"][b].now(i))
                    nc.scalar.activation(kw[b][:, 2], kw[b][:, 1], ACT.Exp, scale=-0.5).then_inc(s["kn3"][b].sem, 1)

                def silus(b):
                    act.wait_ge(s["q"][b].sem, s["q"][b].now(i))
                    act.wait_ge(s["stored"][b].sem, s["stored"][b].last(i))
                    nc.scalar.activation(q3[b][:], bk[b][2][:], ACT.Silu).then_inc(s["q3"][b].sem, 1)
                    nc.scalar.activation(kw[b][:, 5], bk[b][1][:, 0:H], ACT.Sigmoid).then_inc(s["eta"][b].sem, 1)

                def turned(b):
                    act.wait_ge(s["qTp"][b].sem, s["qTp"][b].now(i))
                    nc.scalar.copy(qT[b][:], bk[b][1][:]).then_inc(s["qT"][b].sem, 1)
                    act.wait_ge(s["kTp"][b].sem, s["kTp"][b].now(i))
                    nc.scalar.copy(kT[b][:], bk[b][2][:]).then_inc(s["kT"][b].sem, 1)
                    act.wait_ge(s["g1Tp"][b].sem, s["g1Tp"][b].now(i))
                    nc.scalar.copy(g1T[b][:], bk[b][3][0:DH, 0:P]).then_inc(s["g1T"][b].sem, 1)
                    act.wait_ge(s["gt"][b].sem, s["gt"][b].now(i))
                    nc.scalar.activation(sg[b][:], bk[b][0][:], ACT.Sigmoid).then_inc(s["sg"][b].sem, 1)

                lead_x1(0)
                lead_x1(1)
                soft(0)
                lead_mid(0)
                soft(1)
                lead_mid(1)
                nx[0].guesses(nc, act, i)
                lead_x2(0)
                nx[1].guesses(nc, act, i)
                lead_x2(1)
                squares(0)
                squares(1)
                silus(0)
                turned(0)
                silus(1)
                turned(1)

        @block.vector
        def _(dve):
            dve.wait_ge(consts.sem, consts.now(1))
            with dve.Fori(1, NT + 1) as i:
                def trail_x1(b):
                    dve.wait_ge(s["x1h"][b].sem, s["x1h"][b].now(i))
                    nc.vector.tensor_tensor(xl[b][:].rearrange("p c t -> p (c t)"), bk[b][0][:],
                                            xh[b][:].bitcast(F32).rearrange("p c t -> p (c t)"), ALU.subtract).then_inc(s["x1l"][b].sem, 1)

                def step(name, b, ins):
                    ins.then_inc(s[name][b].sem, 1)
                    dve.wait_ge(s[name][b].sem, s[name][b].now(i))

                def route(b):
                    dve.wait_ge(s["lm"][b].sem, s["lm"][b].now(i))
                    step("lg", b, nc.vector.tensor_tensor(lg[b][:], bk[b][1][:, P:P + EXPERTS], router_b[:], ALU.add))
                    nc.vector.memset(neg[b][:], 0.0)
                    step("top", b, nc.vector.max(top8[b][:], lg[b][:]))
                    nc.vector.tensor_scalar(neg[b][:], top8[b][:, 0:1], -1.0, None, ALU.mult).then_inc(s["neg"][b].sem, 1)
                    step("idx", b, nc.vector.max_index(idx[b][:], top8[b][:], lg[b][:]))
                    step("idf", b, nc.vector.tensor_copy(idf[b][:], idx[b][:]))
                    step("m1", b, nc.vector.tensor_scalar(mask[b][:], order[:], idf[b][:, 0:1], None, ALU.is_equal))
                    step("mask", b, nc.vector.scalar_tensor_tensor(mask[b][:], order[:], idf[b][:, 1:2], mask[b][:], ALU.is_equal, ALU.add))
                    dve.wait_ge(s["ex"][b].sem, s["ex"][b].now(i))
                    step("em", b, nc.vector.tensor_tensor(ex[b][:], ex[b][:], mask[b][:], ALU.mult))
                    step("tot", b, nc.vector.tensor_reduce(tot[b][:, 0:1], ex[b][:], AX, ALU.add))
                    step("inv", b, nc.vector.reciprocal(tot[b][:, 1:2], tot[b][:, 0:1]))
                    step("gate", b, nc.vector.tensor_scalar(ex[b][:], ex[b][:], tot[b][:, 1:2], 2.0, ALU.mult, ALU.mult))
                    nc.vector.tensor_tensor(mid[b][:].rearrange("p (e r) -> p e r", e=EXPERTS),
                                            bk[b][1][:, 0:P].rearrange("p (e r) -> p e r", e=EXPERTS),
                                            ex[b][:].unsqueeze(2).to_broadcast([P, EXPERTS, RANK]), ALU.mult).then_inc(s["mid"][b].sem, 1)

                def trail_mid(b):
                    dve.wait_ge(s["mh"][b].sem, s["mh"][b].now(i))
                    nc.vector.tensor_tensor(ml[b][:], bk[b][3][:, 0:P], mh[b][:].bitcast(F32), ALU.subtract).then_inc(s["ml"][b].sem, 1)

                def norm_x(b):
                    dve.wait_ge(s["ffn"][b].sem, s["ffn"][b].now(i))
                    dve.wait_ge(s["xb"][b].sem, s["xb"][b].now(i))
                    dve.wait_ge(s["stored"][b].sem, s["stored"][b].last(i))
                    step("r", b, nc.vector.tensor_tensor(x2[b][:], bk[b][2][:], xb[b][:], ALU.add))
                    nx[b].stats(nc, dve, i, x2[b][:])
                    nx[b].newton(nc, dve, i)
                    nx[b].apply(nc, x2[b][:], x2[b][:]).then_inc(s["x2"][b].sem, 1)

                def trail_x2(b):
                    dve.wait_ge(s["x2h"][b].sem, s["x2h"][b].now(i))
                    nc.vector.tensor_tensor(xl[b][:].rearrange("p c t -> p (c t)"), bk[b][0][:],
                                            xh[b][:].bitcast(F32).rearrange("p c t -> p (c t)"), ALU.subtract).then_inc(s["x2l"][b].sem, 1)

                def keys(b):
                    dve.wait_ge(s["sq"][b].sem, s["sq"][b].now(i))
                    step("ss", b, nc.vector.tensor_reduce(kw[b][:, 0], heads_of(sq[b][:]), AX, ALU.add))
                    nc.vector.tensor_scalar(kw[b][:, 0], kw[b][:, 0], 1e-6, None, ALU.add).then_inc(s["kn1"][b].sem, 1)
                    dve.wait_ge(s["kn3"][b].sem, s["kn3"][b].now(i))
                    step("kn4", b, nc.vector.tensor_tensor(kw[b][:, 3], kw[b][:, 2], kw[b][:, 2], ALU.mult))
                    step("m1b", b, nc.vector.tensor_tensor(kw[b][:, 3], kw[b][:, 3], kw[b][:, 0], ALU.mult))
                    step("m2b", b, nc.vector.tensor_scalar(kw[b][:, 3], kw[b][:, 3], -0.5, 1.5, ALU.mult, ALU.add))
                    step("kr", b, nc.vector.tensor_tensor(kw[b][:, 4], kw[b][:, 3], kw[b][:, 2], ALU.mult))
                    step("kn", b, nc.vector.tensor_tensor(heads_of(kn[b][:]), heads_of(bk[b][3][:]),
                                                          kw[b][:, 4].unsqueeze(2).to_broadcast([P, H, DH]), ALU.mult))
                    dve.wait_ge(s["v"][b].sem, s["v"][b].now(i))
                    nc.vector.tensor_tensor(te[b][:, :, :, 0:DH].rearrange("p j g d -> p g j d"), by_chunk(bk[b][0][:]),
                                            by_chunk(kn[b][:]), ALU.subtract).then_inc(s["te"][b].sem, 1)

                trail_x1(0)
                trail_x1(1)
                route(0)
                trail_mid(0)
                route(1)
                trail_mid(1)
                norm_x(0)
                trail_x2(0)
                norm_x(1)
                trail_x2(1)
                keys(0)
                keys(1)

        @block.tensor
        def _(pe):
            pe.wait_ge(consts.sem, consts.now(1))
            with pe.Fori(1, NT + 1) as i:
                def turn(b, src, dst, got, made):
                    pe.wait_ge(s[got][b].sem, s[got][b].now(i))
                    for c in range(KC):
                        last = pe.transpose(dst[:, c * P:(c + 1) * P], src[:, c * P:(c + 1) * P], ident[:])
                    last.then_inc(s[made][b].sem, 1)

                def times(out, b, name, stop=True):
                    return exact3(pe, out, lambda c: xh[b][:, c, :], lambda c: xl[b][:, c, :],
                                  lambda c: wh[name][:, c, :], lambda c: wl[name][:, c, :], stop=stop)

                def ffn(b):
                    pe.wait_ge(s["x1l"][b].sem, s["x1l"][b].now(i))
                    pe.wait_ge(s["qT"][b].sem, s["qT"][b].last(i))
                    times(bk[b][1][:, 0:P + EXPERTS], b, "AR").then_inc(s["lm"][b].sem, 1)
                    pe.wait_ge(s["kT"][b].sem, s["kT"][b].last(i))
                    times(bk[b][2][:], b, "base", stop=False)

                def lora(b):
                    pe.wait_ge(s["mid"][b].sem, s["mid"][b].now(i))
                    pe.wait_ge(s["g1T"][b].sem, s["g1T"][b].last(i))
                    pe.transpose(bk[b][3][:, 0:P], mid[b][:], ident[:]).then_inc(s["midT"][b].sem, 1)
                    pe.wait_ge(s["ml"][b].sem, s["ml"][b].now(i))
                    exact3(pe, bk[b][2][:], lambda c: mh[b][:], lambda c: ml[b][:], lambda c: lbh[:], lambda c: lbl[:],
                           start=False, n=1).then_inc(s["ffn"][b].sem, 1)

                def projections(b):
                    pe.wait_ge(s["x2l"][b].sem, s["x2l"][b].now(i))
                    pe.wait_ge(s["mid"][b].sem, s["mid"][b].now(i))
                    times(bk[b][1][:, 0:H + DH], b, "BG").then_inc(s["bg"][b].sem, 1)
                    times(bk[b][3][:], b, "Wk3").then_inc(s["k"][b].sem, 1)
                    times(bk[b][2][:], b, "Wq3").then_inc(s["q"][b].sem, 1)
                    times(bk[b][0][:], b, "Wv3").then_inc(s["v"][b].sem, 1)

                def turns(b):
                    pe.wait_ge(s["g1"][b].sem, s["g1"][b].now(i))
                    pe.wait_ge(s["eta"][b].sem, s["eta"][b].now(i))
                    turn(b, q3[b], bk[b][1], "q3", "qTp")
                    turn(b, kn[b], bk[b][2], "kn", "kTp")
                    pe.transpose(bk[b][3][0:DH, 0:P], g1[b][:], ident[:]).then_inc(s["g1Tp"][b].sem, 1)
                    pe.wait_ge(s["g1T"][b].sem, s["g1T"][b].now(i))
                    pe.wait_ge(s["te"][b].sem, s["te"][b].now(i))
                    pe.matmul(bk[b][0][:], g1T[b][:], wg2[:], start=True, stop=True).then_inc(s["gt"][b].sem, 1)

                for b in range(2):
                    pe.wait_ge(s["sg"][b].sem, s["sg"][b].last(i))
                    turn(b, x1[b], bk[b][0], "x1_in", "x1T")
                ffn(0)
                ffn(1)
                lora(0)
                lora(1)
                turn(0, x2[0], bk[0][0], "x2", "x2T")
                projections(0)
                turn(1, x2[1], bk[1][0], "x2", "x2T")
                projections(1)
                turns(0)
                turns(1)
    ph.end()
    top.close()


def ttt_recurrence(nc, K, bank, a):
    ST, NI = NCH, NT
    HALF = ST // 2
    ph = Phase(nc, "ttt")
    bS, bH, bQ, bA, bK, bC = bank[0:6]
    G = KC
    R64 = HG * TTT
    ident = ph.sb("ident", [P, P])
    tri = ph.sb("tri", [P, R64])
    w_row, b_row, w2 = ph.sb("w_row", [P, G, DH]), ph.sb("b_row", [P, G, DH]), ph.sb("w2", [P, G, DH])
    seq, own = ph.sb("seq", [P, 2]), ph.sb("own", [P, HG])
    zero = ph.sb("zero", [P, 2 * P])
    cK, cQ = ph.sb("cK", [P, B, G, ST * TTT]), ph.sb("cQ", [P, B, G, ST * TTT])
    te = ph.sb("te", [P, ST, G, DH + 1])
    bw = ph.sb("bw", [P, ST, G, DH])
    neta = ph.sb("neta", [P, ST, G])
    KB = [ph.sb(f"KB{r}", [P, G, B, HG, TTT]) for r in range(ST)]
    QB = [ph.sb(f"QB{r}", [P, G, B, HG, TTT]) for r in range(ST)]
    S = ph.sb("S", [P, G, B, DH])
    kb = ph.sb("kb", [P, G, P])
    am = ph.sb("am", [P, G, R64])
    u = ph.sb("u", [P, G, DH])
    ub = ph.sb("ub", [P, G, B, DH])
    cross = ph.sb("cross", [P, G, P])
    qh = ph.sb("qh", [R64, ST, B, G, DH])
    c1, c2, c3, c4, c5, c6 = (ph.sb(f"c{k}", [P, G, DH]) for k in range(6))
    eps = ph.sb("eps", [P, 1])
    m = ph.sb("m", [P, 8, G])
    re = ph.sb("re", [P, G])
    s = {n: ph.counter(n, per) for n, per in
         [("cK", 16 * 4), ("te", 16 * 8), ("bw1", 2), ("bw", 2), ("neta", 2), ("blocks", ST), ("S", ST), ("KH", ST), ("QS", ST),
          ("A", ST), ("KT", ST), ("kb", ST), ("am", ST), ("s1", ST), ("xc", ST), ("sq", ST), ("s2", ST), ("sd", ST), ("rs", ST),
          ("re", ST), ("xw", ST), ("hat", ST), ("t", ST), ("gw", ST), ("r1", ST), ("p", ST), ("r2", ST), ("v1", ST), ("q", ST),
          ("v2", ST), ("u", ST), ("ub", ST), ("KK", ST), ("cross", ST), ("KS", ST), ("SU", ST), ("AU", ST), ("qh", ST), ("stored0", 16 * 8), ("stored1", 16 * 8)]}
    consts = ph.counter("consts", 16 * 6)
    zeroed = ph.counter("zeroed", 2)
    w2_made = ph.counter("w2", 1)
    s0_made = ph.counter("s0", 1)

    with nc.Block() as block:
        @block.sync
        def _(sp):
            for t, src in ((ident, K["ident"]), (tri, K["tri"]), (w_row, a["ln_w"]), (b_row, a["ln_b"]), (seq, K["seq"]),
                           (own, K["own"])):
                sp.dma_start(t[:] if len(t.shape) < 3 else t[:].rearrange("p g d -> p (g d)"), src).then_inc(consts.sem, 16)

            def load(i):
                sp.wait_ge(s["blocks"].sem, s["blocks"].last(i))
                for b in range(B):
                    for dst, name in ((cK, "kT"), (cQ, "qT")):
                        sp.dma_start(dst[:, b].rearrange("p g t -> p (g t)"), a[name][bass.ds((i * 2 + (b - 2)) * P, P), :]).then_inc(s["cK"].sem, 16)
                sp.wait_ge(s["bw"].sem, s["bw"].last(i))
                sp.wait_ge(s["neta"].sem, s["neta"].last(i))
                for b in range(B):
                    for j in range(HG):
                        rows = a["te"][bass.ds((i * 2 + (b - 2)) * P, P), :]
                        src = rows.rearrange("(c t) (j e) -> j t c e", t=TTT, j=HG)[j]
                        r = b * R64 + j * TTT
                        sp.dma_start(te[r:r + TTT].rearrange("t c g e -> t c (g e)"), src).then_inc(s["te"].sem, 16)

            def store(i):
                for f in range(2):
                    sp.wait_ge(s["qh"].sem, s["qh"].part(i, (f + 1) * HALF))
                    for b in range(B):
                        for j in range(HG):
                            rows = a["qh"][bass.ds((i * 2 + (b - 2)) * P + f * HALF * TTT, HALF * TTT), :]
                            sp.dma_start(rows.rearrange("(c t) (j e) -> j t c e", t=TTT, j=HG)[j],
                                         qh[j * TTT:(j + 1) * TTT, f * HALF:(f + 1) * HALF, b].rearrange("t c g e -> t c (g e)")).then_inc(s[f"stored{f}"].sem, 16)

            load(1)
            with sp.Fori(2, NI + 1) as i:
                load(i)
                store(i - 1)
            store(NI)
            for f in range(2):
                sp.wait_ge(s[f"stored{f}"].sem, s[f"stored{f}"].now(NI))

        @block.gpsimd
        def _(pool):
            ph.credit(pool)
            nc.gpsimd.memset(zero[:], 0.0).then_inc(zeroed.sem, 1)
            nc.gpsimd.memset(cross[:], 0.0).then_inc(zeroed.sem, 1)
            pool.wait_ge(zeroed.sem, zeroed.now(1))
            pool.wait_ge(consts.sem, consts.now(1))

            def spread(n):
                for b in range(B):
                    for src, dst in ((cK, KB[n]), (cQ, QB[n])):
                        shape = [P, G, HG, TTT]
                        last = nc.gpsimd.tensor_tensor(
                            dst[:, :, b], src[:, b, :, n * TTT:(n + 1) * TTT].unsqueeze(2).to_broadcast(shape),
                            own[:].unsqueeze(1).unsqueeze(3).to_broadcast(shape), ALU.mult)
                last.then_inc(s["blocks"].sem, 1)

            with pool.Fori(1, NI + 1) as i:
                pool.wait_ge(s["te"].sem, s["te"].now(i))
                pool.wait_ge(s["cK"].sem, s["cK"].now(i))
                for f in range(2):
                    pool.wait_ge(s["re"].sem, s["re"].part(i, (f + 1) * HALF - ST))
                    pool.wait_ge(s["gw"].sem, s["gw"].part(i, (f + 1) * HALF - ST))
                    c = slice(f * HALF, (f + 1) * HALF)
                    nc.gpsimd.tensor_tensor(bw[:, c], b_row[:].unsqueeze(1).to_broadcast([P, HALF, G, DH]), te[:, c, :, 0:DH],
                                            ALU.subtract).then_inc(s["bw1"].sem, 1)
                    nc.gpsimd.tensor_tensor(neta[:, c], zero[:, 0:HALF * G].rearrange("p (c g) -> p c g", g=G), te[:, c, :, DH],
                                            ALU.subtract).then_inc(s["neta"].sem, 1)
                    pool.wait_ge(s["bw1"].sem, s["bw1"].part(i, f + 1))
                    nc.gpsimd.tensor_tensor(bw[:, c], bw[:, c], w_row[:].unsqueeze(1).to_broadcast([P, HALF, G, DH]),
                                            ALU.mult).then_inc(s["bw"].sem, 1)
                    for n in range(f * HALF, (f + 1) * HALF):
                        pool.wait_ge(s["QS"].sem, s["QS"].part(i, n + 1 - ST))
                        spread(n)
            for n in range(2):
                pool.wait_ge(s["QS"].sem, s["QS"].part(NI + 1, n + 1 - ST))
                spread(n)

        @block.scalar
        def _(act):
            act.wait_ge(consts.sem, consts.now(1))
            act.wait_ge(s0_made.sem, s0_made.now(1))
            act.wait_ge(w2_made.sem, 3)
            act.wait_ge(zeroed.sem, zeroed.now(1))
            nc.scalar.preload_act_table_set("sqrt_and_others")
            nc.scalar.copy(S[:].rearrange("p g b e -> p (g b e)"), bS[:, 0:2 * P]).then_inc(s["S"].sem, 1)
            act.wait_ge(s["s2"].sem, s["s2"].part(1, 1))
            nc.scalar.activation(m[:, 2], m[:, 1], ACT.Sqrt, scale=1.0 / DH, bias=eps[:, 0:1]).then_inc(s["sd"].sem, 1)
            with act.Fori(1, NI + 1) as i:
                for n in range(ST):
                    act.wait_ge(s["KT"].sem, s["KT"].part(i, n + 1))
                    nc.scalar.copy(kb[:].rearrange("p g n -> p (g n)"), bK[:]).then_inc(s["kb"].sem, 1)
                    act.wait_ge(s["KK"].sem, s["KK"].part(i, n + 1))
                    act.wait_ge(s["KH"].sem, s["KH"].part(i, n + 1))
                    for b in range(B):
                        r = slice(b * R64, (b + 1) * R64)
                        last = nc.scalar.copy(cross[r, :, r], bC[r, :].rearrange("p (g n) -> p g n", g=G)[:, :, r])
                    last.then_inc(s["cross"].sem, 1)
                    act.wait_ge(s["SU"].sem, s["SU"].part(i, n + 1))
                    act.wait_ge(s["QS"].sem, s["QS"].part(i, n + 1))
                    act.wait_ge(s["KS"].sem, s["KS"].part(i, n + 1))
                    nc.scalar.copy(S[:].rearrange("p g b e -> p (g b e)"), bS[:, 0:2 * P]).then_inc(s["S"].sem, 1)
                    act.wait_ge(s["s2"].sem, s["s2"].part(i, n + 2))
                    nc.scalar.activation(m[:, 2], m[:, 1], ACT.Sqrt, scale=1.0 / DH, bias=eps[:, 0:1]).then_inc(s["sd"].sem, 1)
                    act.wait_ge(s["AU"].sem, s["AU"].part(i, n + 1))
                    if n % HALF == 0:
                        act.wait_ge(s[f"stored{n // HALF}"].sem, s[f"stored{n // HALF}"].last(i))
                    nc.scalar.copy(qh[:, n].rearrange("p b g e -> p (b g e)"), bQ[0:R64, 0:2 * P]).then_inc(s["qh"].sem, 1)

        @block.vector
        def _(dve):
            dve.wait_ge(consts.sem, consts.now(1))
            nc.vector.memset(eps[:], 1e-6).then_inc(w2_made.sem, 1)
            nc.vector.tensor_tensor(w2[:], w_row[:], w_row[:], ALU.mult).then_inc(w2_made.sem, 1)
            dve.wait_ge(w2_made.sem, 3)
            with dve.Fori(1, NI + 1) as i:
                for n in range(ST):
                    def step(name, ins):
                        ins.then_inc(s[name].sem, 1)
                        dve.wait_ge(s[name].sem, s[name].part(i, n + 1))

                    def over_e(t):
                        return t.unsqueeze(2).to_broadcast([P, G, DH])
                    kh = bH[:, 0:P].rearrange("p (g e) -> p g e", g=G)
                    dve.wait_ge(s["KH"].sem, s["KH"].part(i, n + 1))
                    step("s1", nc.vector.tensor_reduce(m[:, 0], kh, AX, ALU.add))
                    step("xc", nc.vector.scalar_tensor_tensor(c1[:], over_e(m[:, 0]), -1.0 / DH, kh, ALU.mult, ALU.add))
                    step("sq", nc.vector.tensor_tensor(c2[:], c1[:], c1[:], ALU.mult))
                    step("s2", nc.vector.tensor_reduce(m[:, 1], c2[:], AX, ALU.add))
                    nc.vector.tensor_tensor(c3[:], c1[:], w2[:], ALU.mult).then_inc(s["xw"].sem, 1)
                    dve.wait_ge(s["sd"].sem, s["sd"].part(i, n + 1))
                    step("rs", nc.vector.reciprocal(m[:, 3], m[:, 2]))
                    if n % HALF == 0:
                        dve.wait_ge(s["neta"].sem, s["neta"].part(i, n // HALF + 1))
                        dve.wait_ge(s["bw"].sem, s["bw"].part(i, n // HALF + 1))
                    nc.vector.tensor_tensor(re[:], m[:, 3], neta[:, n], ALU.mult).then_inc(s["re"].sem, 1)
                    nc.vector.tensor_tensor(c1[:], c1[:], over_e(m[:, 3]), ALU.mult).then_inc(s["hat"].sem, 1)
                    dve.wait_ge(s["xw"].sem, s["xw"].part(i, n + 1))
                    step("t", nc.vector.tensor_tensor(c3[:], c3[:], over_e(m[:, 3]), ALU.mult))
                    step("gw", nc.vector.tensor_tensor(c3[:], c3[:], bw[:, n], ALU.add))
                    dve.wait_ge(s["hat"].sem, s["hat"].part(i, n + 1))
                    nc.vector.tensor_tensor(c2[:], c3[:], c1[:], ALU.mult).then_inc(s["p"].sem, 1)
                    nc.vector.tensor_reduce(m[:, 4], c3[:], AX, ALU.add).then_inc(s["r1"].sem, 1)
                    dve.wait_ge(s["p"].sem, s["p"].part(i, n + 1))
                    step("r2", nc.vector.tensor_reduce(m[:, 5], c2[:], AX, ALU.add))
                    dve.wait_ge(s["r1"].sem, s["r1"].part(i, n + 1))
                    nc.vector.scalar_tensor_tensor(c4[:], over_e(m[:, 4]), -1.0 / DH, c3[:], ALU.mult, ALU.add).then_inc(s["v1"].sem, 1)
                    step("q", nc.vector.tensor_tensor(c5[:], c1[:], over_e(m[:, 5]), ALU.mult))
                    dve.wait_ge(s["v1"].sem, s["v1"].part(i, n + 1))
                    step("v2", nc.vector.scalar_tensor_tensor(c6[:], c5[:], -1.0 / DH, c4[:], ALU.mult, ALU.add))
                    dve.wait_ge(s["re"].sem, s["re"].part(i, n + 1))
                    dve.wait_ge(s["SU"].sem, s["SU"].part(i, n))
                    dve.wait_ge(s["AU"].sem, s["AU"].part(i, n))
                    step("u", nc.vector.tensor_tensor(u[:], c6[:], over_e(re[:]), ALU.mult))
                    nc.vector.tensor_tensor(ub[:], u[:].unsqueeze(2).to_broadcast([P, G, B, DH]),
                                            seq[:].unsqueeze(1).unsqueeze(3).to_broadcast([P, G, B, DH]), ALU.mult).then_inc(s["ub"].sem, 1)
                    dve.wait_ge(s["A"].sem, s["A"].part(i, n + 1))
                    nc.vector.tensor_tensor(am[:], bA[:, 0:2 * P].rearrange("p (g n) -> p g n", g=G),
                                            tri[:].unsqueeze(1).to_broadcast([P, G, R64]), ALU.mult).then_inc(s["am"].sem, 1)
            nc.vector.memset(m[:, 1], 1.0).then_inc(s["s2"].sem, 1)

        @block.tensor
        def _(pe):
            pe.wait_ge(consts.sem, consts.now(1))
            pe.wait_ge(zeroed.sem, zeroed.now(1))
            pe.matmul(bS[:, 0:2 * P], zero[:, 0:P], zero[:], start=True, stop=False, skip_group_check=True).then_inc(s0_made.sem, 1)

            def keys_times_state(n):
                for g in range(G):
                    for b in range(B):
                        last = pe.matmul(bH[b * R64:(b + 1) * R64, g * DH:(g + 1) * DH], KB[n][:, g, b].rearrange("p j t -> p (j t)"),
                                         S[:, g, b, :], start=(g == 0), stop=False, skip_group_check=True)
                return last

            def scores(n, g, b):
                return pe.matmul(bA[b * R64:(b + 1) * R64, g * R64:(g + 1) * R64], KB[n][:, g, b].rearrange("p j t -> p (j t)"),
                                 QB[n][:, g, b].rearrange("p j t -> p (j t)"), start=True, stop=True, skip_group_check=True)

            def keys_times_next(n, g):
                return pe.matmul(bC[:, g * P:(g + 1) * P], KB[n][:].rearrange(both)[:, g],
                                 KB[(n + 1) % ST][:].rearrange(both)[:, g], start=True, stop=True, skip_group_check=True)

            both = "p g b j t -> p g (b j t)"

            pe.wait_ge(s["blocks"].sem, s["blocks"].part(1, 2))
            pe.wait_ge(s["S"].sem, s["S"].part(1, 1))
            keys_times_state(0)
            pe.matmul(bH[:, 0:P], zero[:, 0:P], zero[:, 0:P], start=False, stop=True, skip_group_check=True).then_inc(s["KH"].sem, 1)
            for g in range(G):
                for b in range(B):
                    last = scores(0, g, b)
            last.then_inc(s["A"].sem, 1)
            for g in range(G):
                last = pe.transpose(bK[:, g * P:(g + 1) * P], KB[0][:].rearrange(both)[:, g], ident[:])
            last.then_inc(s["KT"].sem, 1)
            for g in range(G):
                last = keys_times_next(0, g)
            last.then_inc(s["KK"].sem, 1)
            with pe.Fori(1, NI + 1) as i:
                for n in range(ST):
                    QBf = QB[n][:].rearrange("p g b j t -> p g b (j t)")
                    pe.wait_ge(s["S"].sem, s["S"].part(i, n + 1))
                    pe.wait_ge(s["xc"].sem, s["xc"].part(i, n + 1))
                    pe.wait_ge(s["blocks"].sem, s["blocks"].part(i, n + 2))
                    keys_times_state((n + 1) % ST).then_inc(s["KS"].sem, 1)
                    pe.wait_ge(s["qh"].sem, s["qh"].part(i, n))
                    for g in range(G):
                        for b in range(B):
                            last = pe.matmul(bQ[0:R64, (b * G + g) * DH:(b * G + g + 1) * DH], QBf[:, g, b, :], S[:, g, b, :],
                                             start=(g == 0 and b == 0), stop=False, skip_group_check=True)
                    last.then_inc(s["QS"].sem, 1)
                    pe.wait_ge(s["u"].sem, s["u"].part(i, n + 1))
                    pe.wait_ge(s["cross"].sem, s["cross"].part(i, n + 1))
                    for g in range(G):
                        last = pe.matmul(bH[:, g * DH:(g + 1) * DH], cross[:, g, :], u[:, g, :], start=False, stop=True, skip_group_check=True)
                    last.then_inc(s["KH"].sem, 1)
                    pe.wait_ge(s["ub"].sem, s["ub"].part(i, n + 1))
                    pe.wait_ge(s["kb"].sem, s["kb"].part(i, n + 1))
                    for g in range(G):
                        last = pe.matmul(bS[:, g * B * DH:(g + 1) * B * DH], kb[:, g, :], ub[:, g].rearrange("p b e -> p (b e)"),
                                         start=False, stop=False, skip_group_check=True)
                    last.then_inc(s["SU"].sem, 1)
                    pe.wait_ge(s["am"].sem, s["am"].part(i, n + 1))
                    for g in range(G):
                        last = pe.matmul(bQ[0:R64, 0:2 * P].rearrange("p (b g e) -> p g b e", b=B, g=G)[:, g], am[:, g, :],
                                         ub[:, g].rearrange("p b e -> p (b e)"),
                                         start=False, stop=(g == G - 1), skip_group_check=True)
                    last.then_inc(s["AU"].sem, 1)
                    for g in range(G):
                        for b in range(B):
                            last = scores((n + 1) % ST, g, b)
                    last.then_inc(s["A"].sem, 1)
                    for g in range(G):
                        last = pe.transpose(bK[:, g * P:(g + 1) * P], KB[(n + 1) % ST][:].rearrange(both)[:, g], ident[:])
                    last.then_inc(s["KT"].sem, 1)
                    pe.wait_ge(s["blocks"].sem, s["blocks"].part(i, n + 3))
                    for g in range(G):
                        last = keys_times_next((n + 1) % ST, g)
                    last.then_inc(s["KK"].sem, 1)
    ph.end()


def attention_output(nc, K, bank, a):
    top = ExitStack()
    wh = top.enter_context(nc.sbuf_tensor("out_w_hi", [P, KC, D], F32R))
    wl = top.enter_context(nc.sbuf_tensor("out_w_lo", [P, KC, D], F32R))
    load_split(nc, "out_w", [(a["Wo3"], wh[:].rearrange("p c n -> p (c n)"), wl[:].rearrange("p c n -> p (c n)"))])
    ph = Phase(nc, "out")
    bk = [bank[0:4], bank[4:8]]
    ident = ph.sb("ident", [P, P])
    w_all, b_all, norm_w = ph.sb("w_all", [P, D]), ph.sb("b_all", [P, D]), ph.sb("norm_w", [P, KC])
    eps6, eps5 = ph.sb("eps6", [P, 1]), ph.sb("eps5", [P, 1])
    names = ["qh", "q3", "sg", "x2"]
    t = {n: ph.sb2(n, [P, D]) for n in names}
    xc, sq, og, oT, r, x3T = (ph.sb2(n, [P, D]) for n in ("xc", "sq", "og", "oT", "r", "x3T"))
    oh, ol = ph.sb2("oh", [P, KC, P], F32R), ph.sb2("ol", [P, KC, P], F32R)
    w = ph.sb2("w", [P, 8, H])
    st, mv = ph.sb2("st", [P, 6]), ph.sb2("mv", [P, 4])
    s = {}
    for n, per in [("in", 16 * 4), ("s1", 1), ("xc", 1), ("sq", 1), ("s2", 1), ("sd", 1), ("rs", 1), ("hat", 1), ("ow", 1), ("ob", 1),
                   ("oq", 1), ("og", 1), ("sq2", 1), ("s3", 1), ("sd2", 1), ("rs2", 1), ("o5", 1), ("oTp", 1), ("oT", 1), ("oh", 1), ("ol", 1),
                   ("o", 1), ("r", 1), ("st", 1), ("mv", 1), ("sd3", 1), ("rs3", 1), ("x3", 1), ("x3Tp", 1), ("x3T", 1), ("stored", 32)]:
        s[n] = ph.counters_of_two(n, per)
    consts = ph.counter("consts", 16 * 4)
    epsed = ph.counter("eps", 2)

    def rows(name, i, b):
        return a[name][bass.ds((i * 2 + (b - 2)) * P, P), :]

    def by_place(v):
        return v.rearrange("p (g j e) -> p j g e", g=KC, j=HG)

    def placed(v):
        return v.rearrange("p (j g e) -> p j g e", g=KC, j=HG)

    def each_head(v):
        return v.unsqueeze(2).to_broadcast([P, H, DH])

    with nc.Block() as block:
        @block.sync
        def _(sp):
            for dst, src in ((ident, K["ident"]), (w_all, a["w_all"]), (b_all, a["b_all"]), (norm_w, a["norm_w"])):
                sp.dma_start(dst[:], src).then_inc(consts.sem, 16)
            with sp.Fori(1, NT + 1) as i:
                for b in range(2):
                    sp.wait_ge(s["og"][b].sem, s["og"][b].last(i))
                    sp.wait_ge(s["r"][b].sem, s["r"][b].last(i))
                    for n in names:
                        sp.dma_start(t[n][b][:], rows(n, i, b)).then_inc(s["in"][b].sem, 16)
                for b in range(2):
                    sp.wait_ge(s["x3"][b].sem, s["x3"][b].now(i))
                    sp.dma_start(rows("x3", i, b), r[b][:]).then_inc(s["stored"][b].sem, 16)
                    sp.wait_ge(s["x3T"][b].sem, s["x3T"][b].now(i))
                    sp.dma_start(rows("x3T", i, b), x3T[b][:]).then_inc(s["stored"][b].sem, 16)
            for b in range(2):
                sp.wait_ge(s["stored"][b].sem, s["stored"][b].now(NT))

        @block.gpsimd
        def _(pool):
            ph.credit(pool)
            nc.gpsimd.memset(eps6[:], 1e-6).then_inc(epsed.sem, 1)
            nc.gpsimd.memset(eps5[:], 1e-5).then_inc(epsed.sem, 1)
            pool.wait_ge(consts.sem, consts.now(1))
            with pool.Fori(1, NT + 1) as i:
                for b in range(2):
                    def step(name, ins):
                        ins.then_inc(s[name][b].sem, 1)
                        pool.wait_ge(s[name][b].sem, s[name][b].now(i))
                    pool.wait_ge(s["hat"][b].sem, s["hat"][b].now(i))
                    step("ow", nc.gpsimd.tensor_tensor(xc[b][:], xc[b][:], w_all[:], ALU.mult))
                    step("ob", nc.gpsimd.tensor_tensor(xc[b][:], xc[b][:], b_all[:], ALU.add))
                    step("oq", nc.gpsimd.tensor_tensor(placed(xc[b][:]), placed(xc[b][:]), by_place(t["q3"][b][:]), ALU.add))
                    pool.wait_ge(s["oTp"][b].sem, s["oTp"][b].last(i))
                    nc.gpsimd.tensor_tensor(by_place(og[b][:]), placed(xc[b][:]), by_place(t["sg"][b][:]), ALU.mult).then_inc(s["og"][b].sem, 1)

        @block.scalar
        def _(act):
            act.wait_ge(consts.sem, consts.now(1))
            act.wait_ge(epsed.sem, epsed.now(1))
            with act.Fori(1, NT + 1) as i:
                def square(b, src, got, made):
                    act.wait_ge(s[got][b].sem, s[got][b].now(i))
                    nc.scalar.activation(sq[b][:], src[b][:], ACT.Square).then_inc(s[made][b].sem, 1)

                def root(b, col, got, made):
                    act.wait_ge(s[got][b].sem, s[got][b].now(i))
                    nc.scalar.activation(w[b][:, col + 1], w[b][:, col], ACT.Sqrt, scale=1.0 / DH, bias=eps6[:, 0:1]).then_inc(s[made][b].sem, 1)

                def scaled(b):
                    act.wait_ge(s["oTp"][b].sem, s["oTp"][b].now(i))
                    for c in range(KC):
                        last = nc.scalar.activation(oT[b][:, c * P:(c + 1) * P], bk[b][0][:, c * P:(c + 1) * P], ACT.Identity,
                                                    scale=norm_w[:, c:c + 1])
                    last.then_inc(s["oT"][b].sem, 1)

                def root_x(b):
                    act.wait_ge(s["mv"][b].sem, s["mv"][b].now(i))
                    nc.scalar.activation(mv[b][:, 2:3], mv[b][:, 1:2], ACT.Sqrt, bias=eps5[:, 0:1]).then_inc(s["sd3"][b].sem, 1)

                def turned(b):
                    act.wait_ge(s["x3Tp"][b].sem, s["x3Tp"][b].now(i))
                    act.wait_ge(s["stored"][b].sem, s["stored"][b].last(i))
                    nc.scalar.copy(x3T[b][:], bk[b][2][:]).then_inc(s["x3T"][b].sem, 1)

                for b in range(2):
                    square(b, xc, "xc", "sq")
                    root(b, 1, "s2", "sd")
                for b in range(2):
                    square(b, og, "og", "sq2")
                    root(b, 4, "s3", "sd2")
                scaled(0)
                scaled(1)
                root_x(0)
                root_x(1)
                turned(0)
                turned(1)

        @block.vector
        def _(dve):
            dve.wait_ge(consts.sem, consts.now(1))
            with dve.Fori(1, NT + 1) as i:
                def step(name, b, ins):
                    ins.then_inc(s[name][b].sem, 1)
                    dve.wait_ge(s[name][b].sem, s[name][b].now(i))

                def centre(b):
                    dve.wait_ge(s["in"][b].sem, s["in"][b].now(i))
                    dve.wait_ge(s["og"][b].sem, s["og"][b].last(i))
                    step("s1", b, nc.vector.tensor_reduce(w[b][:, 0], heads_of(t["qh"][b][:]), AX, ALU.add))
                    step("xc", b, nc.vector.scalar_tensor_tensor(heads_of(xc[b][:]), each_head(w[b][:, 0]), -1.0 / DH,
                                                                 heads_of(t["qh"][b][:]), ALU.mult, ALU.add))

                def unit(b):
                    dve.wait_ge(s["sq"][b].sem, s["sq"][b].now(i))
                    step("s2", b, nc.vector.tensor_reduce(w[b][:, 1], heads_of(sq[b][:]), AX, ALU.add))
                    dve.wait_ge(s["sd"][b].sem, s["sd"][b].now(i))
                    step("rs", b, nc.vector.reciprocal(w[b][:, 3], w[b][:, 2]))
                    nc.vector.tensor_tensor(heads_of(xc[b][:]), heads_of(xc[b][:]), each_head(w[b][:, 3]), ALU.mult).then_inc(s["hat"][b].sem, 1)

                def rms(b):
                    dve.wait_ge(s["sq2"][b].sem, s["sq2"][b].now(i))
                    step("s3", b, nc.vector.tensor_reduce(w[b][:, 4], heads_of(sq[b][:]), AX, ALU.add))
                    dve.wait_ge(s["sd2"][b].sem, s["sd2"][b].now(i))
                    step("rs2", b, nc.vector.reciprocal(w[b][:, 6], w[b][:, 5]))
                    nc.vector.tensor_tensor(heads_of(og[b][:]), heads_of(og[b][:]), each_head(w[b][:, 6]), ALU.mult).then_inc(s["o5"][b].sem, 1)

                def split(b):
                    dve.wait_ge(s["oT"][b].sem, s["oT"][b].now(i))
                    step("oh", b, nc.vector.tensor_copy(oh[b][:].rearrange("p c t -> p (c t)"), oT[b][:]))
                    nc.vector.tensor_tensor(ol[b][:].rearrange("p c t -> p (c t)"), oT[b][:],
                                            oh[b][:].bitcast(F32).rearrange("p c t -> p (c t)"), ALU.subtract).then_inc(s["ol"][b].sem, 1)

                def norm(b):
                    dve.wait_ge(s["o"][b].sem, s["o"][b].now(i))
                    dve.wait_ge(s["stored"][b].sem, s["stored"][b].last(i))
                    step("r", b, nc.vector.tensor_tensor(r[b][:], bk[b][1][:], t["x2"][b][:], ALU.add))
                    step("st", b, nc.vector.bn_stats(st[b][:], r[b][:]))
                    nc.vector.memset(mv[b][:, 3:4], 0.0)
                    nc.vector.bn_aggr(mv[b][:, 0:2], st[b][:]).then_inc(s["mv"][b].sem, 1)
                    dve.wait_ge(s["sd3"][b].sem, s["sd3"][b].now(i))
                    step("rs3", b, nc.vector.reciprocal(mv[b][:, 3:4], mv[b][:, 2:3]))
                    nc.vector.tensor_scalar(r[b][:], r[b][:], mv[b][:, 0:1], mv[b][:, 3:4], ALU.subtract, ALU.mult).then_inc(s["x3"][b].sem, 1)

                for stage in (centre, unit, rms, split, norm):
                    stage(0)
                    stage(1)

        @block.tensor
        def _(pe):
            pe.wait_ge(consts.sem, consts.now(1))
            with pe.Fori(1, NT + 1) as i:
                for b in range(2):
                    pe.wait_ge(s["o5"][b].sem, s["o5"][b].now(i))
                    for c in range(KC):
                        last = pe.transpose(bk[b][0][:, c * P:(c + 1) * P], og[b][:, c * P:(c + 1) * P], ident[:])
                    last.then_inc(s["oTp"][b].sem, 1)
                for b in range(2):
                    pe.wait_ge(s["ol"][b].sem, s["ol"][b].now(i))
                    exact3(pe, bk[b][1][:], lambda c: oh[b][:, c, :], lambda c: ol[b][:, c, :],
                           lambda c: wh[:, c, :], lambda c: wl[:, c, :]).then_inc(s["o"][b].sem, 1)
                for b in range(2):
                    pe.wait_ge(s["x3"][b].sem, s["x3"][b].now(i))
                    for c in range(KC):
                        last = pe.transpose(bk[b][2][:, c * P:(c + 1) * P], r[b][:, c * P:(c + 1) * P], ident[:])
                    last.then_inc(s["x3Tp"][b].sem, 1)
    ph.end()
    top.close()


def route(nc, K, bank, a, w6, slot6, expert_row, xh, xl):
    N = B * NT
    ph = Phase(nc, "route")
    gh, gl, gf = ph.sb("gh", [P, KC, MOE_E], F32R), ph.sb("gl", [P, KC, MOE_E], F32R), ph.sb("gf", [P, KC * MOE_E])
    bias = ph.sb("bias", [P, MOE_E])
    low4, low16 = ph.sb("low4", [P, 16]), ph.sb("low16", [P, MOE_E * MOE_E])
    before, ones = ph.sb("before", [P, P]), ph.sb("ones", [P, P])
    order, token, filled, tiles = (ph.sb("order", [P, EXPERTS]), ph.sb("token", [P, 1]), ph.sb("filled", [P, N * P // SLOTS]),
                                   ph.sb("tiles", [P, TILES]))
    sc, sfc = ph.sb("sc", [P, N, MOE_E]), ph.sb("sfc", [P, N, MOE_E])
    pairs, gs = ph.sb("pairs", [P, N * MOE_G, 6]), ph.sb("gs", [P, N, MOE_G])
    c1, c2 = ph.sb("c1", [P, N, MOE_E, MOE_E]), ph.sb("c2", [P, N, MOE_E, MOE_E])
    rank, sel, tot, inv = ph.sb("rank", [P, N, MOE_E]), ph.sb("sel", [P, N, MOE_E]), ph.sb("tot", [P, N]), ph.sb("inv", [P, N])
    each, slot = ph.sb("each", [P, N, MOE_E]), ph.sb("slot", [P, N, MOE_E])
    load, taken, base = ph.sb("load", [P, MOE_E]), ph.sb("taken", [P, MOE_E]), ph.sb("base", [P, MOE_E])
    slot_f, of_tile, row = ph.sb("slot_f", [P, N, TOP]), ph.sb("of_tile", [P, TILES]), ph.sb("row", [P, TILES])
    landed, lead, trail, logits, scored, chain, chosen, counted = (nc.alloc_semaphore(name=f"route_{n}") for n in
                                                                   ("landed", "lead", "trail", "logits", "scored", "chain", "chosen", "counted"))
    with nc.Block() as block:
        @block.sync
        def _(sp):
            for dst, src in ((gf, a["gate_w"]), (bias, a["gate_b"]), (low4, K["low4"]), (low16, K["low16"]), (before, K["before"]),
                             (ones, K["ones"]), (order, K["order"]), (token, K["token"]), (filled, K["filled"]), (tiles, K["tiles"])):
                sp.dma_start(dst[:], src).then_inc(landed, 16)

        @block.scalar
        def _(act):
            act.wait_ge(logits, 1)
            nc.scalar.activation(sc[:].rearrange("p n e -> p (n e)"), bank[0][:, 0:N * MOE_E], ACT.Sigmoid).then_inc(scored, 1)

        @block.tensor
        def _(pe):
            pe.wait_ge(trail, 1)
            for n in range(N):
                last = exact3(pe, bank[0][:, n * MOE_E:(n + 1) * MOE_E], lambda c: xh[:, c, n * P:(n + 1) * P],
                              lambda c: xl[:, c, n * P:(n + 1) * P], lambda c: gh[:, c, :], lambda c: gl[:, c, :])
            last.then_inc(logits, 1)
            pe.wait_ge(chosen, 1)
            for k, m in ((1, before), (2, ones)):
                pe.matmul(bank[k][:, 0:N * MOE_E], m[:], sel[:].rearrange("p n e -> p (n e)"), start=True, stop=True).then_inc(counted, 1)

        @block.vector
        def _(dve):
            count = [0]

            def link(ins):
                count[0] += 1
                ins.then_inc(chain, 1)
                dve.wait_ge(chain, count[0])
            dve.wait_ge(landed, 16 * 10)
            flat = "p c e -> p (c e)"
            nc.vector.tensor_copy(gh[:].rearrange(flat), gf[:]).then_inc(lead, 1)
            dve.wait_ge(lead, 1)
            nc.vector.tensor_tensor(gl[:].rearrange(flat), gf[:], gh[:].bitcast(F32).rearrange(flat), ALU.subtract).then_inc(trail, 1)
            dve.wait_ge(scored, 1)
            link(nc.vector.tensor_tensor(sfc[:], sc[:], bias[:].unsqueeze(1).to_broadcast([P, N, MOE_E]), ALU.add))
            v = sfc[:].rearrange("p n (g k) -> p (n g) k", g=MOE_G)
            nc.vector.tensor_tensor(pairs[:, :, 0:3], v[:, :, 0:3], v[:, :, 1:4], ALU.add)
            nc.vector.tensor_tensor(pairs[:, :, 3:5], v[:, :, 0:2], v[:, :, 2:4], ALU.add)
            link(nc.vector.tensor_tensor(pairs[:, :, 5:6], v[:, :, 0:1], v[:, :, 3:4], ALU.add))
            link(nc.vector.tensor_reduce(gs[:].rearrange("p n g -> p (n g)"), pairs[:], AX, ALU.max))

            def ranked(vals, m, lower):
                shape = [P, N, m, m]
                others, own = vals.unsqueeze(2).to_broadcast(shape), vals.unsqueeze(3).to_broadcast(shape)
                a1 = c1[:].rearrange("p n e f -> p (n e f)")[:, 0:N * m * m].rearrange("p (n e f) -> p n e f", n=N, e=m)
                a2 = c2[:].rearrange("p n e f -> p (n e f)")[:, 0:N * m * m].rearrange("p (n e f) -> p n e f", n=N, e=m)
                link(nc.vector.tensor_tensor(a1, others, own, ALU.is_equal))
                link(nc.vector.tensor_tensor(a1.rearrange("p n e f -> p n (e f)"), a1.rearrange("p n e f -> p n (e f)"),
                                             lower[:].unsqueeze(1).to_broadcast([P, N, m * m]), ALU.mult))
                link(nc.vector.tensor_tensor(a2, others, own, ALU.is_gt))
                link(nc.vector.tensor_tensor(a1, a1, a2, ALU.add))
                link(nc.vector.tensor_reduce(rank[:].rearrange("p n e -> p (n e)")[:, 0:N * m].rearrange("p (n e) -> p n e", n=N), a1, AX, ALU.add))

            ranked(gs[:], MOE_G, low4)
            g_rank = rank[:].rearrange("p n e -> p (n e)")[:, 0:N * MOE_G]
            link(nc.vector.tensor_scalar(gs[:].rearrange("p n g -> p (n g)"), g_rank, 1.5, None, ALU.is_lt))
            g_sel = gs[:].rearrange("p n g -> p (n g)").unsqueeze(2).to_broadcast([P, N * MOE_G, MOE_E // MOE_G])
            link(nc.vector.tensor_tensor(v, v, g_sel, ALU.mult))
            ranked(sfc[:], MOE_E, low16)
            nc.vector.tensor_scalar(sel[:], rank[:], TOP - 0.5, None, ALU.is_lt).then_inc(chosen, 1)
            dve.wait_ge(chosen, 1)
            link(nc.vector.tensor_tensor(sc[:], sel[:], sc[:], ALU.mult))
            link(nc.vector.tensor_reduce(tot[:], sc[:], AX, ALU.add))
            link(nc.vector.tensor_scalar(tot[:], tot[:], 1e-20, None, ALU.add))
            link(nc.vector.reciprocal(inv[:], tot[:]))
            link(nc.vector.tensor_scalar(inv[:], inv[:], 2.5, None, ALU.mult))
            link(nc.vector.tensor_tensor(sc[:], sc[:], inv[:].unsqueeze(2).to_broadcast([P, N, MOE_E]), ALU.mult))
            dve.wait_ge(counted, 2)
            link(nc.vector.tensor_copy(each[:].rearrange("p n e -> p (n e)"), bank[2][:, 0:N * MOE_E]))
            shape = [P, N, MOE_E, N]
            others, low = each[:].rearrange("p n e -> p e n"), low16[:].rearrange("p (n m) -> p n m", n=N)
            link(nc.vector.tensor_tensor(c1[:], others.unsqueeze(1).to_broadcast(shape), low.unsqueeze(2).to_broadcast(shape), ALU.mult))
            link(nc.vector.tensor_reduce(slot[:], c1[:], AX, ALU.add))
            link(nc.vector.tensor_tensor(slot[:].rearrange("p n e -> p (n e)"), slot[:].rearrange("p n e -> p (n e)"),
                                         bank[1][:, 0:N * MOE_E], ALU.add))
            link(nc.vector.tensor_reduce(load[:], others, AX, ALU.add))
            NK = N * P // SLOTS
            a1 = c1[:].rearrange("p n e f -> p (n e f)")[:, 0:MOE_E * NK].rearrange("p (e k) -> p e k", k=NK)
            link(nc.vector.tensor_tensor(a1, load[:].unsqueeze(2).to_broadcast([P, MOE_E, NK]),
                                         filled[:].unsqueeze(1).to_broadcast([P, MOE_E, NK]), ALU.is_gt))
            link(nc.vector.tensor_reduce(taken[:], a1, AX, ALU.add))
            link(nc.vector.tensor_tensor(c1[:, 0], taken[:].unsqueeze(1).to_broadcast([P, MOE_E, MOE_E]),
                                         low16[:].rearrange("p (e f) -> p e f", e=MOE_E), ALU.mult))
            link(nc.vector.tensor_reduce(base[:], c1[:, 0], AX, ALU.add))
            link(nc.vector.tensor_tensor(taken[:], taken[:], base[:], ALU.add))
            link(nc.vector.scalar_tensor_tensor(slot[:], base[:].unsqueeze(1).to_broadcast([P, N, MOE_E]), float(SLOTS), slot[:],
                                                ALU.mult, ALU.add))
            shape = [P, N, TOP, MOE_E]
            a1 = c1[:].rearrange("p n e f -> p (n e f)")[:, 0:N * TOP * MOE_E].rearrange("p (n j e) -> p n j e", n=N, j=TOP)
            a2 = c2[:].rearrange("p n e f -> p (n e f)")[:, 0:N * TOP * MOE_E].rearrange("p (n j e) -> p n j e", n=N, j=TOP)
            link(nc.vector.tensor_tensor(a1, rank[:].unsqueeze(2).to_broadcast(shape),
                                         order[:, 0:TOP].unsqueeze(1).unsqueeze(3).to_broadcast(shape), ALU.is_equal))
            link(nc.vector.tensor_tensor(a2, a1, slot[:].unsqueeze(2).to_broadcast(shape), ALU.mult))
            link(nc.vector.tensor_reduce(slot_f[:], a2, AX, ALU.add))
            link(nc.vector.tensor_tensor(a2, a1, sc[:].unsqueeze(2).to_broadcast(shape), ALU.mult))
            link(nc.vector.tensor_reduce(w6[:], a2, AX, ALU.add))
            link(nc.vector.tensor_copy(slot6[:], slot_f[:]))
            a1 = c1[:].rearrange("p n e f -> p (n e f)")[:, 0:TILES * MOE_E].rearrange("p (t e) -> p t e", e=MOE_E)
            link(nc.vector.tensor_tensor(a1, taken[:].unsqueeze(1).to_broadcast([P, TILES, MOE_E]),
                                         tiles[:].unsqueeze(2).to_broadcast([P, TILES, MOE_E]), ALU.is_le))
            link(nc.vector.tensor_reduce(of_tile[:], a1, AX, ALU.add))
            link(nc.vector.tensor_scalar(of_tile[:], of_tile[:], MOE_E - 1.0, None, ALU.min))
            link(nc.vector.memset(row[:, 0:2], 0.0))
            link(nc.vector.tensor_tensor(row[:, 2:], of_tile[:, 2:], of_tile[:, 0:TILES - 2], ALU.is_equal))
            link(nc.vector.tensor_scalar(row[:], row[:], float(NOWHERE), token[:, 0:1], ALU.mult, ALU.add))
            link(nc.vector.scalar_tensor_tensor(row[:], of_tile[:], float(P), row[:], ALU.mult, ALU.add))
            link(nc.vector.tensor_copy(expert_row[:], row[:]))
    nc.clear_and_free_semaphores([landed, lead, trail, logits, scored, chain, chosen, counted])
    nc.all_engine_barrier()
    ph.stack.close()


def shared_experts(nc, K, bank, a, acc, slot6, x_row, y_row, xh, xl):
    N, NB = B * NT, 4
    TB = N * P // NB
    ph = Phase(nc, "moe")
    GU, DN = 2 * KC * MOE_I, 3 * D
    guf, guh, gul = ph.sb("guf", [P, GU]), ph.sb("guh", [P, 2, KC, MOE_I], F32R), ph.sb("gul", [P, 2, KC, MOE_I], F32R)
    dnf, dnh, dnl = ph.sb("dnf", [P, DN]), ph.sb("dnh", [P, 3, D], F32R), ph.sb("dnl", [P, 3, D], F32R)
    ih, il = ph.sb("ih", [P, 3, TB], F32R), ph.sb("il", [P, 3, TB], F32R)
    sil = ph.sb2("sil", [P, TB])
    ident, pair, table = ph.sb("ident", [P, P]), ph.sb("pair", [P, N, TOP, 2]), ph.sb("table", [TILES, SLOTS, 2])
    NH = 3 * NB
    s = {n: ph.counter(n, per) for n, per in
         [("acc_in", 16), ("gu_in", 16), ("dn_in", 16), ("guh", 1), ("gul", 1), ("dnh", 1), ("dnl", 1), ("gu", NH), ("sil", NH), ("prod", NH),
          ("ih", NH), ("il", NH), ("dn", N), ("acc", N)]}
    consts, freed, given, listed, turned, rows_made = (nc.alloc_semaphore(name=f"slots_{n}") for n in
                                                      ("consts", "freed", "given", "listed", "turned", "rows_made"))
    with nc.Block() as block:
        @block.sync
        def _(sp):
            sp.dma_start(a["slots"], K["free"]).then_inc(freed, 16)
            sp.dma_start(ident[:], K["ident"]).then_inc(consts, 16)
            sp.dma_start(pair[:].rearrange("p n j k -> p (n j k)"), K["pair"]).then_inc(consts, 16)
            sp.dma_start(acc[:], a["x3"].rearrange("(n p) d -> p n d", p=P)).then_inc(s["acc_in"].sem, 16)
            with sp.Fori(1, NS + 1) as i:
                sp.wait_ge(s["gul"].sem, s["gul"].last(i))
                sp.wait_ge(s["guh"].sem, s["guh"].last(i))
                sp.dma_start(guf[:], a["GU"][bass.ds((i + (MOE_E - 1)) * P, P), :]).then_inc(s["gu_in"].sem, 16)
                sp.wait_ge(s["dnl"].sem, s["dnl"].last(i))
                sp.wait_ge(s["dnh"].sem, s["dnh"].last(i))
                sp.dma_start(dnf[:], a["DN"][bass.ds((i + (MOE_E - 1)) * P, P), :]).then_inc(s["dn_in"].sem, 16)
            sp.wait_ge(given, 16 * N * TOP)
            sp.dma_start(table[:].rearrange("t s k -> t (s k)"), a["slots"].rearrange("(t s) k -> t (s k)", s=SLOTS)).then_inc(listed, 16)

        @block.gpsimd
        def _(pool):
            ph.credit(pool)
            pool.wait_ge(freed, 16)
            pool.wait_ge(consts, 32)
            for n in range(N):
                for j in range(TOP):
                    nc.gpsimd.indirect_dma_start(a["slots"], bass.IndirectOffsetOnAxis(ap=slot6[:, n, j:j + 1], axis=0), pair[:, n, j], None).then_inc(given, 16)
            pool.wait_ge(given, 16 * N * TOP)

        def hidden():
            k = 0
            for blk in range(NB):
                for c, (at_, m) in enumerate(ICH):
                    yield k, blk, c, at_, m
                    k += 1

        @block.scalar
        def _(act):
            nc.scalar.preload_act_table_set("silu_and_others")
            with act.Fori(1, NS + 1) as i:
                act.wait_ge(s["gu_in"].sem, s["gu_in"].now(i))
                act.wait_ge(s["gu"].sem, s["gu"].part(i, 0))
                nc.scalar.copy(guh[:].rearrange("p a c n -> p (a c n)"), guf[:]).then_inc(s["guh"].sem, 1)
                for k, blk, c, o, m in hidden():
                    act.wait_ge(s["gu"].sem, s["gu"].part(i, k + 1))
                    act.wait_ge(s["il"].sem, s["il"].part(i, k - 1))
                    nc.scalar.activation(sil[k % 2][0:m], bank[2 * (k % 3)][0:m, :], ACT.Silu).then_inc(s["sil"].sem, 1)
                    act.wait_ge(s["prod"].sem, s["prod"].part(i, k + 1))
                    act.wait_ge(s["dn"].sem, s["dn"].part(i, blk * TB // P))
                    nc.scalar.copy(ih[0:m, c], sil[k % 2][0:m]).then_inc(s["ih"].sem, 1)
                    if k == 1:
                        act.wait_ge(s["dn_in"].sem, s["dn_in"].now(i))
                        nc.scalar.copy(dnh[:].rearrange("p c n -> p (c n)"), dnf[:]).then_inc(s["dnh"].sem, 1)

        @block.vector
        def _(dve):
            dve.wait_ge(s["acc_in"].sem, s["acc_in"].now(1))
            with dve.Fori(1, NS + 1) as i:
                dve.wait_ge(s["guh"].sem, s["guh"].now(i))
                nc.vector.tensor_tensor(gul[:].rearrange("p a c n -> p (a c n)"), guf[:],
                                        guh[:].bitcast(F32).rearrange("p a c n -> p (a c n)"), ALU.subtract).then_inc(s["gul"].sem, 1)
                for k, blk, c, o, m in hidden():
                    dve.wait_ge(s["sil"].sem, s["sil"].part(i, k + 1))
                    nc.vector.tensor_tensor(sil[k % 2][0:m], sil[k % 2][0:m], bank[2 * (k % 3) + 1][0:m, :], ALU.mult).then_inc(s["prod"].sem, 1)
                    dve.wait_ge(s["ih"].sem, s["ih"].part(i, k + 1))
                    nc.vector.tensor_tensor(il[0:m, c], sil[k % 2][0:m], ih[0:m, c].bitcast(F32), ALU.subtract).then_inc(s["il"].sem, 1)
                    if k == 1:
                        dve.wait_ge(s["dnh"].sem, s["dnh"].now(i))
                        nc.vector.tensor_tensor(dnl[:].rearrange("p c n -> p (c n)"), dnf[:],
                                                dnh[:].bitcast(F32).rearrange("p c n -> p (c n)"), ALU.subtract).then_inc(s["dnl"].sem, 1)
                    if c == 2:
                        for n in range(blk * TB // P, (blk + 1) * TB // P):
                            dve.wait_ge(s["dn"].sem, s["dn"].part(i, n + 1))
                            dve.wait_ge(s["acc"].sem, s["acc"].part(i, n + 1 - N))
                            nc.vector.tensor_tensor(acc[:, n], bank[6 + n % 2][:], acc[:, n], ALU.add).then_inc(s["acc"].sem, 1)
            nc.vector.memset(y_row[:, :, 0:1], NOWHERE).then_inc(rows_made, 1)
            dve.wait_ge(turned, 2)
            nc.vector.tensor_copy(x_row[:], bank[0][:, 0:2 * TILES].rearrange("p (h t) -> p h t", h=2)).then_inc(rows_made, 1)
            nc.vector.tensor_copy(y_row[:, :, 1:], bank[1][:, 0:2 * TILES].rearrange("p (h t) -> p h t", h=2)).then_inc(rows_made, 1)
            dve.wait_ge(rows_made, 3)

        @block.tensor
        def _(pe):
            with pe.Fori(1, NS + 1) as i:
                pe.wait_ge(s["gul"].sem, s["gul"].now(i))
                for k, blk, c, o, m in hidden():
                    pe.wait_ge(s["prod"].sem, s["prod"].part(i, k - 2))
                    for u in range(2):
                        last = exact3(pe, bank[2 * (k % 3) + u][0:m, :], lambda q: guh[:, u, q, o:o + m], lambda q: gul[:, u, q, o:o + m],
                                      lambda q: xh[:, q, blk * TB:(blk + 1) * TB], lambda q: xl[:, q, blk * TB:(blk + 1) * TB])
                    last.then_inc(s["gu"].sem, 1)
                    if c < 2:
                        continue
                    pe.wait_ge(s["dnl"].sem, s["dnl"].now(i))
                    pe.wait_ge(s["il"].sem, s["il"].part(i, k + 1))
                    for n in range(blk * TB // P, (blk + 1) * TB // P):
                        pe.wait_ge(s["acc"].sem, s["acc"].part(i, n - 1))
                        t = slice(n * P - blk * TB, (n + 1) * P - blk * TB)
                        for c, (o, m) in enumerate(ICH):
                            last = exact3(pe, bank[6 + n % 2][:], lambda q: ih[0:m, c, t], lambda q: il[0:m, c, t],
                                          lambda q: dnh[0:m, c, :], lambda q: dnl[0:m, c, :], start=(c == 0), stop=(c == 2), n=1)
                        last.then_inc(s["dn"].sem, 1)
            pe.wait_ge(listed, 16)
            pe.wait_ge(consts, 32)
            for k in range(2):
                for h in range(2):
                    last = pe.transpose(bank[k][:, h * TILES:(h + 1) * TILES], table[:, h * P:(h + 1) * P, k], ident[0:TILES, 0:TILES])
                last.then_inc(turned, 1)
    nc.clear_and_free_semaphores([consts, freed, given, listed, turned, rows_made])
    ph.end()


def routed_experts(nc, K, bank, a, x_row, y_row, expert_row):
    ph = Phase(nc, "routed")
    GU, DN, NR = 2 * KC * MOE_I, 3 * D, (MOE_E + NS) * P
    guf, dnf = ph.sb2("guf", [P, GU]), ph.sb2("dnf", [P, DN])
    guh, gul = ph.sb2("guh", [P, 2, KC, MOE_I], F32R), ph.sb2("gul", [P, 2, KC, MOE_I], F32R)
    dnh, dnl = ph.sb2("dnh", [P, 3, D], F32R), ph.sb2("dnl", [P, 3, D], F32R)
    x, xh, xl = ph.sb2("x", [P, 2, D]), ph.sb2("xh", [P, KC, SLOTS], F32R), ph.sb2("xl", [P, KC, SLOTS], F32R)
    ih, il = ph.sb2("ih", [P, 3, SLOTS], F32R), ph.sb2("il", [P, 3, SLOTS], F32R)
    sil = ph.sb2("sil", [P, SLOTS])
    y = ph.sb2("y", [P, 2, D])
    zero, ident = ph.sb("zero", [P, DN]), ph.sb("ident", [P, P])
    xi, yi, wi = ph.sb2("xi", [P, 2], U32), ph.sb2("yi", [P, 2], U32), ph.sb2("wi", [P, 1], U32)
    gu_bank, y_bank, t_bank = bank[0:3], bank[3:5], bank[5:7]
    s = {n: ph.counter(n, per) for n, per in
         [("rows", 2), ("turned", 2), ("xh", 2), ("xl", 2), ("guh", 2), ("gul", 2), ("dnh", 2), ("dnl", 2), ("gu", 6), ("sil", 6), ("prod", 6),
          ("ih", 6), ("il", 6), ("dn", 4), ("y", 4)]}
    x_in, gu_in, dn_in, y_out = ([nc.alloc_semaphore(name=f"routed_{n}{q}") for q in range(2)] for n in ("x_in", "gu_in", "dn_in", "y_out"))
    asked, consts, zeroed = (nc.alloc_semaphore(name=f"routed_{n}") for n in ("asked", "consts", "zeroed"))

    with nc.Block() as block:
        @block.sync
        def _(sp):
            sp.dma_start(ident[:], K["ident"]).then_inc(consts, 16)

        @block.gpsimd
        def _(pool):
            ph.credit(pool)

            def tokens(q):
                for h in range(2):
                    nc.gpsimd.indirect_dma_start(x[q][:, h], None, a["x3"], bass.IndirectOffsetOnAxis(ap=xi[q][:, h:h + 1], axis=0)).then_inc(x_in[q], 16)

            def weights(dst, src, q, landed):
                nc.gpsimd.indirect_dma_start(dst[q][:], None, a[src], bass.IndirectOffsetOnAxis(ap=wi[q][:], axis=0),
                                             bounds_check=NR - 1, oob_is_err=False).then_inc(landed[q], 16)

            def products(q):
                for h in range(2):
                    nc.gpsimd.indirect_dma_start(a["y"], bass.IndirectOffsetOnAxis(ap=yi[q][:, h:h + 1], axis=0), y[q][:, h], None,
                                                 bounds_check=B * L * TOP - 1, oob_is_err=False).then_inc(y_out[q], 16)

            pool.wait_ge(zeroed, 13)
            for q in range(2):
                tokens(q)
                weights(guf, "GU", q, gu_in)
                weights(dnf, "DN", q, dn_in)
            for q in range(2):
                products(q)
            with pool.Fori(1, PAIRS + 1) as i:
                for r in range(2):
                    pool.wait_ge(s["rows"].sem, s["rows"].part(i, r + 1))
                    pool.sem_inc(asked, 1)
                    tokens(r)
                    pool.wait_ge(s["gul"].sem, s["gul"].part(i, r + 1))
                    pool.sem_inc(asked, 1)
                    weights(guf, "GU", r, gu_in)
                    pool.wait_ge(s["dnl"].sem, s["dnl"].part(i, r + 1))
                    pool.sem_inc(asked, 1)
                    weights(dnf, "DN", r, dn_in)
                    pool.wait_ge(s["y"].sem, s["y"].part(i, 2 * r + 2))
                    pool.sem_inc(asked, 1)
                    products(r)
            for q in range(2):
                pool.wait_ge(y_out[q], 32 * (PAIRS + 1))
                pool.wait_ge(x_in[q], 32 * (PAIRS + 1))
                pool.wait_ge(gu_in[q], 16 * (PAIRS + 1))
                pool.wait_ge(dn_in[q], 16 * (PAIRS + 1))

        @block.scalar
        def _(act):
            nc.scalar.preload_act_table_set("silu_and_others")

            def turned_lead(q, done):
                for k in range(2):
                    last = nc.scalar.copy(xh[q][:, 2 * k:2 * k + 2].rearrange("p c t -> p (c t)"), t_bank[k][:])
                last.then_inc(done, 1)

            act.wait_ge(gu_in[0], 16)
            nc.scalar.copy(guh[0][:].rearrange("p a c n -> p (a c n)"), guf[0][:]).then_inc(s["guh"].sem, 1)
            act.wait_ge(s["turned"].sem, s["turned"].part(1, 1))
            turned_lead(0, s["xh"].sem)
            with act.Fori(1, PAIRS + 1) as i:
                for r in range(2):
                    q = 1 - r
                    act.wait_ge(gu_in[q], 16 * (i + r))
                    act.wait_ge(s["gu"].sem, s["gu"].part(i, 3 * r))
                    nc.scalar.copy(guh[q][:].rearrange("p a c n -> p (a c n)"), guf[q][:]).then_inc(s["guh"].sem, 1)
                    for c, (o, m) in enumerate(ICH):
                        act.wait_ge(s["gu"].sem, s["gu"].part(i, 3 * r + c + 1))
                        act.wait_ge(s["il"].sem, s["il"].part(i, 3 * r + c - 1))
                        nc.scalar.activation(sil[(3 * r + c) % 2][0:m], gu_bank[c][0:m, 0:SLOTS], ACT.Silu).then_inc(s["sil"].sem, 1)
                        if c == 0:
                            act.wait_ge(dn_in[r], 16 * i)
                            act.wait_ge(s["dn"].sem, s["dn"].part(i, 2 * r))
                            nc.scalar.copy(dnh[r][:].rearrange("p c n -> p (c n)"), dnf[r][:]).then_inc(s["dnh"].sem, 1)
                        act.wait_ge(s["prod"].sem, s["prod"].part(i, 3 * r + c + 1))
                        nc.scalar.copy(ih[r][0:m, c], sil[(3 * r + c) % 2][0:m]).then_inc(s["ih"].sem, 1)
                    act.wait_ge(s["turned"].sem, s["turned"].part(i, r + 2))
                    turned_lead(q, s["xh"].sem)
                    act.wait_ge(y_out[r], 32 * i)
                    for h in range(2):
                        act.wait_ge(s["dn"].sem, s["dn"].part(i, 2 * r + h + 1))
                        nc.scalar.copy(y[r][:, h], y_bank[h][:]).then_inc(s["y"].sem, 1)

        @block.vector
        def _(dve):
            def turned_trail(q, done):
                for k in range(2):
                    c = slice(2 * k, 2 * k + 2)
                    last = nc.vector.tensor_tensor(xl[q][:, c].rearrange("p c t -> p (c t)"), t_bank[k][:],
                                                   xh[q][:, c].bitcast(F32).rearrange("p c t -> p (c t)"), ALU.subtract)
                last.then_inc(done, 1)

            for q in range(2):
                nc.vector.tensor_copy(xi[q][:], x_row[:, :, q]).then_inc(zeroed, 1)
                nc.vector.tensor_copy(wi[q][:], expert_row[:, q:q + 1]).then_inc(zeroed, 1)
                nc.vector.tensor_copy(yi[q][:], y_row[:, :, 0]).then_inc(zeroed, 1)
            nc.vector.memset(zero[:], 0.0).then_inc(zeroed, 1)
            dve.wait_ge(zeroed, 7)
            for dst in (dnh[1], dnl[1], ih[1], il[1]):
                nc.vector.tensor_copy(dst[:].rearrange("p c n -> p (c n)"), zero[:, 0:3 * dst.shape[2]]).then_inc(zeroed, 1)
            for q in range(2):
                nc.vector.tensor_copy(y[q][:].rearrange("p h d -> p (h d)"), zero[:, 0:2 * D]).then_inc(zeroed, 1)
            dve.wait_ge(s["guh"].sem, s["guh"].part(1, 1))
            nc.vector.tensor_tensor(gul[0][:].rearrange("p a c n -> p (a c n)"), guf[0][:],
                                    guh[0][:].bitcast(F32).rearrange("p a c n -> p (a c n)"), ALU.subtract).then_inc(s["gul"].sem, 1)
            dve.wait_ge(s["xh"].sem, s["xh"].part(1, 1))
            turned_trail(0, s["xl"].sem)
            with dve.Fori(1, PAIRS + 1) as i:
                for r in range(2):
                    q = 1 - r
                    dve.wait_ge(s["turned"].sem, s["turned"].part(i, r + 1))
                    dve.wait_ge(s["guh"].sem, s["guh"].part(i, r + 1))
                    dve.wait_ge(dn_in[r], 16 * i)
                    dve.wait_ge(y_out[r], 32 * i)
                    nc.vector.tensor_copy(xi[r][:], x_row[:, :, bass.ds(i * 2 + r, 1)].rearrange("p h o -> p (h o)"))
                    nc.vector.tensor_copy(yi[r][:], y_row[:, :, bass.ds(i * 2 + (r - 2), 1)].rearrange("p h o -> p (h o)"))
                    nc.vector.tensor_copy(wi[r][:], expert_row[:, bass.ds(i * 2 + r, 1)]).then_inc(s["rows"].sem, 1)
                    dve.wait_ge(s["guh"].sem, s["guh"].part(i, r + 2))
                    nc.vector.tensor_tensor(gul[q][:].rearrange("p a c n -> p (a c n)"), guf[q][:],
                                            guh[q][:].bitcast(F32).rearrange("p a c n -> p (a c n)"), ALU.subtract).then_inc(s["gul"].sem, 1)
                    for c, (o, m) in enumerate(ICH):
                        k = (3 * r + c) % 2
                        dve.wait_ge(s["sil"].sem, s["sil"].part(i, 3 * r + c + 1))
                        nc.vector.tensor_tensor(sil[k][0:m], sil[k][0:m], gu_bank[c][0:m, SLOTS:], ALU.mult).then_inc(s["prod"].sem, 1)
                        if c == 0:
                            dve.wait_ge(s["dnh"].sem, s["dnh"].part(i, r + 1))
                            nc.vector.tensor_tensor(dnl[r][:].rearrange("p c n -> p (c n)"), dnf[r][:],
                                                    dnh[r][:].bitcast(F32).rearrange("p c n -> p (c n)"), ALU.subtract).then_inc(s["dnl"].sem, 1)
                        dve.wait_ge(s["ih"].sem, s["ih"].part(i, 3 * r + c + 1))
                        nc.vector.tensor_tensor(il[r][0:m, c], sil[k][0:m], ih[r][0:m, c].bitcast(F32), ALU.subtract).then_inc(s["il"].sem, 1)
                    dve.wait_ge(s["xh"].sem, s["xh"].part(i, r + 2))
                    turned_trail(q, s["xl"].sem)

        @block.tensor
        def _(pe):
            def turn(q):
                for c in range(KC):
                    for h in range(2):
                        o = (c % 2) * SLOTS + h * P
                        last = pe.transpose(t_bank[c // 2][:, o:o + P], x[q][:, h, c * P:(c + 1) * P], ident[:])
                last.then_inc(s["turned"].sem, 1)

            pe.wait_ge(consts, 16)
            pe.wait_ge(zeroed, 13)
            pe.wait_ge(x_in[0], 32)
            turn(0)
            with pe.Fori(1, PAIRS + 1) as i:
                for r in range(2):
                    q = 1 - r
                    pe.wait_ge(s["gul"].sem, s["gul"].part(i, r + 1))
                    pe.wait_ge(s["xl"].sem, s["xl"].part(i, r + 1))
                    for c, (o, m) in enumerate(ICH):
                        pe.wait_ge(s["prod"].sem, s["prod"].part(i, 3 * r + c - 2))
                        for u in range(2):
                            last = exact3(pe, gu_bank[c][0:m, u * SLOTS:(u + 1) * SLOTS], lambda k: guh[r][:, u, k, o:o + m],
                                          lambda k: gul[r][:, u, k, o:o + m], lambda k: xh[r][:, k, :], lambda k: xl[r][:, k, :])
                        last.then_inc(s["gu"].sem, 1)
                    pe.wait_ge(x_in[q], 32 * (i + r))
                    turn(q)
                    pe.wait_ge(s["dnl"].sem, s["dnl"].part(i, r))
                    pe.wait_ge(s["il"].sem, s["il"].part(i, 3 * r))
                    for h in range(2):
                        pe.wait_ge(s["y"].sem, s["y"].part(i, 2 * r + h - 1))
                        t = slice(h * P, (h + 1) * P)
                        for c, (o, m) in enumerate(ICH):
                            last = exact3(pe, y_bank[h][:], lambda k: ih[q][0:m, c, t], lambda k: il[q][0:m, c, t],
                                          lambda k: dnh[q][0:m, c, :], lambda k: dnl[q][0:m, c, :], start=(c == 0), stop=(c == 2), n=1)
                        last.then_inc(s["dn"].sem, 1)
    nc.clear_and_free_semaphores([*x_in, *gu_in, *dn_in, *y_out, asked, consts, zeroed])
    ph.end()


def experts(nc, K, bank, a):
    N = B * NT
    top = ExitStack()
    acc = top.enter_context(nc.sbuf_tensor("moe_acc", [P, N, D], F32))
    w6 = top.enter_context(nc.sbuf_tensor("moe_w6", [P, N, TOP], F32))
    slot6 = top.enter_context(nc.sbuf_tensor("moe_slot6", [P, N, TOP], U32))
    x_row = top.enter_context(nc.sbuf_tensor("moe_x_row", [P, 2, TILES], U32))
    y_row = top.enter_context(nc.sbuf_tensor("moe_y_row", [P, 2, TILES + 1], U32))
    expert_row = top.enter_context(nc.sbuf_tensor("moe_expert_row", [P, TILES], U32))
    columns = ExitStack()
    xh = columns.enter_context(nc.sbuf_tensor("moe_xh", [P, KC, N * P], F32R))
    xl = columns.enter_context(nc.sbuf_tensor("moe_xl", [P, KC, N * P], F32R))
    load_split(nc, "moe_x", [(a["x3T"][n * P:(n + 1) * P, :], xh[:, :, n * P:(n + 1) * P], xl[:, :, n * P:(n + 1) * P])
                             for n in range(N)], stage_cols=D)
    route(nc, K, bank, a, w6, slot6, expert_row, xh, xl)
    shared_experts(nc, K, bank, a, acc, slot6, x_row, y_row, xh, xl)
    columns.close()
    routed_experts(nc, K, bank, a, x_row, y_row, expert_row)

    ph = Phase(nc, "last")
    y = [ph.sb(f"y{k}", [P, TOP, D]) for k in range(4)]
    st, mv, rs, eps = ph.sb("st", [P, N, 6]), ph.sb("mv", [P, N, 2]), ph.sb("rs", [P, 2, N]), ph.sb("eps", [P, 1])
    added, stats, root, inv, done, stored = (nc.alloc_semaphore(name=f"last_{n}") for n in ("added", "stats", "root", "inv", "done", "stored"))
    y_in = [nc.alloc_semaphore(name=f"last_y_in{k}") for k in range(4)]
    with nc.Block() as block:
        @block.sync
        def _(sp):
            rows = a["y"].rearrange("(n p j) d -> n p (j d)", p=P, j=TOP)
            for n in range(N):
                if n >= 4:
                    sp.wait_ge(added, (n - 3) * TOP)
                sp.dma_start(y[n % 4][:].rearrange("p j d -> p (j d)"), rows[n]).then_inc(y_in[n % 4], 16)

        @block.vector
        def _(dve):
            nc.vector.memset(eps[:], 1e-5)
            for n in range(N):
                dve.wait_ge(y_in[n % 4], 16 * (n // 4 + 1))
                for j in range(TOP):
                    if j:
                        dve.wait_ge(added, n * TOP + j)
                    nc.vector.scalar_tensor_tensor(acc[:, n], y[n % 4][:, j], w6[:, n, j:j + 1], acc[:, n], ALU.mult, ALU.add).then_inc(added, 1)
                dve.wait_ge(added, n * TOP + TOP)
                nc.vector.bn_stats(st[:, n], acc[:, n]).then_inc(stats, 1)
                dve.wait_ge(stats, 2 * n + 1)
                nc.vector.bn_aggr(mv[:, n], st[:, n]).then_inc(stats, 1)
                if n:
                    dve.wait_ge(root, n)
                    nc.vector.reciprocal(rs[:, 1, n - 1:n], rs[:, 0, n - 1:n]).then_inc(inv, 1)
            dve.wait_ge(root, N)
            nc.vector.reciprocal(rs[:, 1, N - 1:N], rs[:, 0, N - 1:N]).then_inc(inv, 1)

        @block.scalar
        def _(act):
            nc.scalar.preload_act_table_set("sqrt_and_others")
            for n in range(N):
                act.wait_ge(stats, 2 * n + 2)
                nc.scalar.activation(rs[:, 0, n:n + 1], mv[:, n, 1:2], ACT.Sqrt, bias=eps[:, 0:1]).then_inc(root, 1)

        @block.gpsimd
        def _(pool):
            for n in range(N):
                pool.wait_ge(inv, n + 1)
                i, b = n // B, n % B
                nc.gpsimd.tensor_scalar(acc[:, n], acc[:, n], mv[:, n, 0:1], rs[:, 1, n:n + 1], ALU.subtract, ALU.mult).then_inc(done, 1)
                pool.wait_ge(done, n + 1)
                pool.dma_start(a["out"][b, i * P:(i + 1) * P, :], acc[:, n]).then_inc(stored, 16)
            pool.wait_ge(stored, 16 * N)
    ph.stack.close()
    top.close()


def shape_constants():
    N = B * NT
    tok = np.arange(P)
    sub, mid = tok // SUB, (tok // SUB) * SUB + SUB // 2 - 1
    src, dst = tok[:, None], tok[None, :]
    same = sub[:, None] == sub[None, :]
    m = mid[None, :]
    cum = same * (((src > m) & (src <= dst)) * 1.0 - ((src > dst) & (src <= m)) * 1.0)
    edges = [-1, *(np.arange(NSUB) * SUB + SUB // 2 - 1), P - 1]
    sel = np.stack([(tok > lo) & (tok <= hi) for lo, hi in zip(edges[:-1], edges[1:])], 1)
    return {
        "ident": np.eye(P),
        "cum": cum,
        "sel": sel,
        "causal": same & (src <= dst),
        "tri": ((tok[:, None] // TTT) % HG == tok[None, :HG * TTT] // TTT) & (tok[:, None] % TTT <= tok[None, :HG * TTT] % TTT),
        "seq": tok[:, None] // (HG * TTT) == np.arange(2)[None, :],
        "low4": np.broadcast_to(np.tri(MOE_G, k=-1).reshape(1, -1), (P, MOE_G ** 2)),
        "low16": np.broadcast_to(np.tri(MOE_E, k=-1).reshape(1, -1), (P, MOE_E ** 2)),
        "own": tok[:, None] // DH == np.arange(HG)[None, :],
        "order": np.broadcast_to(np.arange(EXPERTS), (P, EXPERTS)),
        "before": src < dst,
        "ones": np.ones((P, P)),
        "token": tok[:, None],
        "filled": np.broadcast_to(np.arange(B * L // SLOTS) * SLOTS, (P, B * L // SLOTS)),
        "tiles": np.broadcast_to(np.arange(TILES), (P, TILES)),
        "pair": np.stack(np.broadcast_arrays((np.arange(N)[None, :] * P + tok[:, None])[:, :, None],
                                             ((np.arange(N)[None, :] * P + tok[:, None]) * TOP)[:, :, None] + np.arange(TOP)), 3).reshape(P, -1),
        "free": np.stack(np.broadcast_arrays(0, NOWHERE + np.arange(TILES * SLOTS)), 1),
        "heads": (tok[:, None] // DH) == (tok[None, :] // DH),
    }


def by_feature(w):
    n = w.shape[0] // P
    return np.ascontiguousarray(w.reshape(n, P, -1).transpose(1, 0, 2).reshape(P, -1))


def layout(x):
    x = {k: np.asarray(v) for k, v in x.items()}
    tok = x["L0_attn_x"].reshape(B, NT, P, D).transpose(1, 0, 2, 3)
    a = {"x": tok.reshape(-1, D)}
    a["xT"] = tok.reshape(NT, B, P, KC, P).transpose(0, 1, 4, 3, 2).reshape(-1, D)
    for n in ("Wq", "Wk", "Wv", "Wg", "Wo"):
        a[n] = by_feature(x[f"L0_attn_{n}"].T)
    for n in ("gamma", "beta"):
        a[n] = x[f"L0_attn_{n}"].reshape(KC, P).T
    def on_all(v):
        return np.broadcast_to(v, (P, v.size))
    a["base"] = by_feature(x["L0_ffn_base_w"].T)
    a["base_b"], a["router_b"] = on_all(x["L0_ffn_base_b"]), on_all(x["L0_ffn_router_b"])
    a["AR"] = by_feature(np.concatenate([x["L0_ffn_lora_A"].transpose(1, 0, 2).reshape(D, -1), x["L0_ffn_router_w"].T], 1))
    a["loraB"] = x["L0_ffn_lora_B"].reshape(EXPERTS * RANK, D)
    for n in ("Wq", "Wk", "Wv"):
        a[n + "3"] = by_feature(x[f"L1_attn_{n}"])
    a["Wo3"] = by_feature(x["L1_attn_Wo"])
    a["BG"] = by_feature(np.concatenate([x["L1_attn_Wbeta"], x["L1_attn_Wg1"]], 1))
    a["Wg2"] = x["L1_attn_Wg2"]
    for n in ("ln_w", "ln_b"):
        v = x[f"L1_attn_{n}"].reshape(KC, HG, DH).transpose(1, 0, 2).reshape(1, HG, 1, KC * DH)
        a[n] = np.broadcast_to(v, (B, HG, TTT, KC * DH)).reshape(P, KC * DH)
    for n in ("w", "b"):
        a[n + "_all"] = on_all(x["L1_attn_ln_" + n].reshape(KC, HG, DH).transpose(1, 0, 2).reshape(-1))
    a["gate_w"], a["gate_b"] = by_feature(x["L1_ffn_gate_weight"].T), on_all(x["L1_ffn_e_score_correction_bias"])
    f = "L1_ffn_"
    gu = [np.concatenate([x[f + n], x[f + "shared_" + m].reshape(2, MOE_I, D)]) for n, m in (("gate_proj", "gate_w"), ("up_proj", "up_w"))]
    gu = np.stack(gu, 1).reshape(-1, 2, MOE_I, KC, P)
    a["GU"] = gu.transpose(0, 4, 1, 3, 2).reshape(-1, 2 * KC * MOE_I)
    dn = np.concatenate([x[f + "down_proj"], x[f + "shared_down_w"].reshape(D, 2, MOE_I).transpose(1, 0, 2)]).transpose(0, 2, 1)
    dn = np.pad(dn, ((0, 0), (0, 3 * P - MOE_I), (0, 0))).reshape(-1, 3, P, D)
    a["DN"] = dn.transpose(0, 2, 1, 3).reshape(-1, 3 * D)
    a["norm_w"] = x["L1_attn_norm_w"].reshape(KC, P).T
    a = {k: np.ascontiguousarray(v) for k, v in a.items()}
    a.update({k: np.ascontiguousarray(v.astype(np.float32)) for k, v in shape_constants().items()})
    return a


def build(nc, a, out):
    N = B * L
    for name, cols in (("x1", D), ("x2", D), ("q3", D), ("qT", D), ("kT", D), ("te", H * (DH + 1)), ("sg", D), ("qh", D),
                       ("x3", D), ("x3T", D)):
        a[name] = nc.dram_tensor(f"mid_{name}", (N, cols), F32).ap()
    a["slots"] = nc.dram_tensor("mid_slots", (TILES * SLOTS, 2), F32).ap()
    a["y"] = nc.dram_tensor("mid_y", (N * TOP, D), F32).ap()
    a["out"] = out
    with ExitStack() as ctx:
        bank = [ctx.enter_context(nc.psum_tensor(f"bank{k}", [P, D], F32)) for k in range(8)]
        gated_recurrence(nc, a, bank, a)
        lora_and_projections(nc, a, bank, a)
        ttt_recurrence(nc, a, bank, a)
        attention_output(nc, a, bank, a)
        experts(nc, a, bank, a)


def kernel(**inputs):
    import concourse.bacc as bacc
    from concourse.bass_utils import run_bass_kernel_spmd

    nc = bacc.Bacc("TRN2", target_bir_lowering=False, num_devices=1)
    arrays = layout(inputs)
    a = {n: nc.dram_tensor(f"in_{n}", v.shape, F32, kind="ExternalInput").ap() for n, v in arrays.items()}
    out = nc.dram_tensor("out", (B, L, D), F32, kind="ExternalOutput").ap()
    build(nc, a, out)
    r = run_bass_kernel_spmd(nc, [{f"in_{n}": v for n, v in arrays.items()}], core_ids=[0])
    return r.results[0]["out"]
```

```python
from contextlib import ExitStack

import numpy as np
import concourse.bass as bass
from concourse import mybir

ALU = mybir.AluOpType
ACT = mybir.ActivationFunctionType
F32 = mybir.dt.float32
F32R = mybir.dt.float32r
U32 = mybir.dt.uint32
AX = mybir.AxisListType.X

P = 128
B, L, D, H = 2, 1024, 512, 16
DH = D // H
KC = D // P
NT = L // P
HG = P // DH
SUB = 32
NSUB = P // SUB
EXPERTS, RANK = 8, 16
FULL_RATE = 256
TTT = 16
NCH = P // TTT
MOE_E, MOE_I, MOE_G, TOP = 16, 352, 4, 6
NS = 2
SLOTS = 2 * P
FULL = (B * L * TOP + MOE_E * (SLOTS - 1)) // SLOTS
PAIRS = (FULL + 2) // 2
TILES = 2 * PAIRS + 2
NOWHERE = 1 << 16
ICH = [(0, 128), (128, 128), (256, 96)]


class Counter:

    def __init__(self, nc, name, per):
        self.sem, self.per = nc.alloc_semaphore(name=name), per

    def now(self, i):
        return i * self.per + self.per

    def last(self, i):
        return i * self.per

    def part(self, i, k):
        return i * self.per + k


class Phase:

    def __init__(self, nc, name):
        self.nc, self.name, self.counters, self.stack = nc, name, [], ExitStack()

    def counter(self, name, per=1):
        s = Counter(self.nc, f"{self.name}_{name}", per)
        self.counters.append(s)
        return s

    def counters_of_two(self, name, per=1):
        return [self.counter(f"{name}{b}", per) for b in range(2)]

    def sb(self, name, shape, dt=F32):
        return self.stack.enter_context(self.nc.sbuf_tensor(f"{self.name}_{name}", shape, dt))

    def sb2(self, name, shape, dt=F32):
        return [self.sb(f"{name}{b}", shape, dt) for b in range(2)]

    def credit(self, eng):
        for s in self.counters:
            eng.sem_inc(s.sem, s.per)

    def end(self):
        self.nc.clear_and_free_semaphores([s.sem for s in self.counters])
        self.nc.all_engine_barrier()
        self.stack.close()


def exact3(pe, out, hi, lo, whi, wlo, start=True, stop=True, n=KC):
    for c in range(n):
        pe.matmul(out, hi(c), whi(c), start=start and c == 0, stop=False, skip_group_check=True)
        pe.matmul(out, lo(c), whi(c), start=False, stop=False, skip_group_check=True)
        last = pe.matmul(out, hi(c), wlo(c), start=False, stop=stop and c == n - 1, skip_group_check=True)
    return last


def load_split(nc, name, parts, stage_cols=D * KC):
    stack = ExitStack()
    NSTAGE = 4 if stage_cols > D else 8
    stage = [stack.enter_context(nc.sbuf_tensor(f"{name}_stage{k}", [P, stage_cols], F32)) for k in range(NSTAGE)]
    landed = [nc.alloc_semaphore(name=f"{name}_landed{k}") for k in range(NSTAGE)]
    leading = nc.alloc_semaphore(name=f"{name}_leading")
    trailing = nc.alloc_semaphore(name=f"{name}_trailing")

    def view(n, src, like):
        v = stage[n % NSTAGE][0:src.shape[0], 0:src.shape[1]]
        return v.rearrange("p (c t) -> p c t", c=like.shape[1]) if len(like.shape) == 3 else v

    with nc.Block() as block:
        @block.sync
        def _(sp):
            for n, (src, hi, lo) in enumerate(parts):
                if n >= NSTAGE:
                    sp.wait_ge(trailing, n - NSTAGE + 1)
                sp.dma_start(stage[n % NSTAGE][0:src.shape[0], 0:src.shape[1]], src).then_inc(landed[n % NSTAGE], 16)

        @block.scalar
        def _(act):
            for n, (src, hi, lo) in enumerate(parts):
                act.wait_ge(landed[n % NSTAGE], 16 * (n // NSTAGE + 1))
                nc.scalar.copy(hi, view(n, src, hi)).then_inc(leading, 1)

        @block.vector
        def _(dve):
            for n, (src, hi, lo) in enumerate(parts):
                dve.wait_ge(leading, n + 1)
                dve.wait_ge(landed[n % NSTAGE], 16 * (n // NSTAGE + 1))
                nc.vector.tensor_tensor(lo, view(n, src, hi), hi.bitcast(F32),
                                        ALU.subtract).then_inc(trailing, 1)
            dve.wait_ge(trailing, len(parts))
    nc.clear_and_free_semaphores([*landed, leading, trailing])
    nc.all_engine_barrier()
    stack.close()


class Norm:

    def __init__(self, ph, name, b, eps):
        self.eps = eps
        self.st = ph.sb(f"{name}_st{b}", [P, 6])
        self.mv = ph.sb(f"{name}_mv{b}", [P, 2])
        self.w = ph.sb(f"{name}_w{b}", [P, 5])
        self.stat, self.mean, self.var, self.log, self.guess, self.n1, self.n2, self.rstd = (
            ph.counter(f"{name}_{n}{b}") for n in ("stat", "mean", "var", "log", "guess", "n1", "n2", "rstd"))

    def stats(self, nc, dve, i, src):
        nc.vector.bn_stats(self.st[:], src).then_inc(self.stat.sem, 1)
        dve.wait_ge(self.stat.sem, self.stat.now(i))
        nc.vector.memset(self.w[:, 0:1], 0.0)
        nc.vector.bn_aggr(self.mv[:], self.st[:]).then_inc(self.mean.sem, 1)
        dve.wait_ge(self.mean.sem, self.mean.now(i))
        nc.vector.tensor_scalar(self.w[:, 0:1], self.mv[:, 1:2], self.eps, None, ALU.add).then_inc(self.var.sem, 1)

    def guesses(self, nc, act, i):
        act.wait_ge(self.var.sem, self.var.now(i))
        nc.scalar.activation(self.w[:, 1:2], self.w[:, 0:1], ACT.Ln).then_inc(self.log.sem, 1)
        act.wait_ge(self.log.sem, self.log.now(i))
        nc.scalar.activation(self.w[:, 2:3], self.w[:, 1:2], ACT.Exp, scale=-0.5).then_inc(self.guess.sem, 1)

    def newton(self, nc, dve, i):
        dve.wait_ge(self.guess.sem, self.guess.now(i))
        nc.vector.scalar_tensor_tensor(self.w[:, 3:4], self.w[:, 2:3], self.w[:, 0:1], self.w[:, 2:3],
                                       ALU.mult, ALU.mult).then_inc(self.n1.sem, 1)
        dve.wait_ge(self.n1.sem, self.n1.now(i))
        nc.vector.tensor_scalar(self.w[:, 3:4], self.w[:, 3:4], -0.5, 1.5, ALU.mult, ALU.add).then_inc(self.n2.sem, 1)
        dve.wait_ge(self.n2.sem, self.n2.now(i))
        nc.vector.tensor_tensor(self.w[:, 4:5], self.w[:, 3:4], self.w[:, 2:3], ALU.mult).then_inc(self.rstd.sem, 1)
        dve.wait_ge(self.rstd.sem, self.rstd.now(i))

    def apply(self, nc, out, src):
        return nc.vector.tensor_scalar(out, src, self.mv[:, 0:1], self.w[:, 4:5], ALU.subtract, ALU.mult)


def gated_recurrence(nc, K, bank, a):
    top = ExitStack()
    names = ["Wg", "Wv", "Wq", "Wk", "Wo"]
    wh = {n: top.enter_context(nc.sbuf_tensor(f"gla_{n}_hi", [P, KC, D], F32R)) for n in names}
    wl = {n: top.enter_context(nc.sbuf_tensor(f"gla_{n}_lo", [P, KC, D], F32R)) for n in names}
    load_split(nc, "gla_w", [(a[n], wh[n][:].rearrange("p c n -> p (c n)"), wl[n][:].rearrange("p c n -> p (c n)"))
                             for n in names])
    ph = Phase(nc, "gla")
    PJ, BK = bank[0:4], bank[4:8]
    ident = ph.sb("ident", [P, P])
    cum = ph.sb("cum", [P, P])
    sel = ph.sb("sel", [P, NSUB + 1])
    causal = ph.sb("causal", [P, P])
    heads = ph.sb("heads", [P, P])
    gamma = ph.sb("gamma", [P, KC])
    beta = ph.sb("beta", [P, KC])
    xT, xTh, xTl = ph.sb2("xT", [P, KC, P]), ph.sb2("xTh", [P, KC, P], F32R), ph.sb2("xTl", [P, KC, P], F32R)
    xt, az, g = ph.sb2("xt", [P, D]), ph.sb2("az", [P, D]), ph.sb2("g", [P, D])
    eR, enR = ph.sb2("eR", [P, D]), ph.sb2("enR", [P, D])
    x1 = ph.sb2("x1", [P, D])
    Qr, Kr, V = ph.sb2("Qr", [P, D]), ph.sb2("Kr", [P, D]), ph.sb2("V", [P, D])
    QT, KT = ph.sb2("QT", [P, KC, P]), ph.sb2("KT", [P, KC, P])
    Am = ph.sb2("Am", [P, HG, KC, P])
    kvm = ph.sb2("kvm", [P, KC, P])
    Sh = ph.sb2("Sh", [P, NSUB, KC, P])
    carry = ph.sb2("carry", [P, KC, P])
    decay = ph.sb2("decay", [P, KC, NSUB + 1])
    yTh, yTl = ph.sb2("yTh", [P, KC, P], F32R), ph.sb2("yTl", [P, KC, P], F32R)

    s = {}
    for n, per in [("xT_in", 16), ("xt_in", 16), ("xh", 1), ("xl", 1), ("z", 1), ("v", 1), ("q", 1), ("k", 1),
                   ("az", 1), ("ez", 1), ("lz", 1), ("g", 1), ("R", 1), ("eR", 1), ("enR", 1), ("decay", 1),
                   ("V", 1), ("Qr", 1), ("Kr", 1), ("QTp", 1), ("KTp", 1), ("QT", 1), ("KT", 1),
                   ("kv", NSUB), ("kvm", NSUB), ("sum", NSUB), ("Sh", NSUB + 1), ("A", HG), ("Am", HG),
                   ("y", 1), ("yn", 1), ("yTp", 1), ("yT", 1), ("yTh", 1), ("yTl", 1), ("o", 1), ("r", 1),
                   ("x1", 1), ("x1_out", 16)]:
        s[n] = ph.counters_of_two(n, per)
    n1 = [Norm(ph, "ny", b, 1e-5) for b in range(2)]
    n2 = [Norm(ph, "nx", b, 1e-5) for b in range(2)]
    consts = ph.counter("consts", 16 * 7)
    zeroed = ph.counter("zeroed", 2)

    def x1_rows(i, b):
        return a["x1"][bass.ds((i * 2 + (b - 2)) * P, P), :]

    with nc.Block() as block:
        @block.sync
        def _(sp):
            for t, src in ((ident, K["ident"]), (cum, K["cum"]), (sel, K["sel"]), (causal, K["causal"]),
                           (heads, K["heads"]), (gamma, a["gamma"]), (beta, a["beta"])):
                sp.dma_start(t[:], src).then_inc(consts.sem, 16)

            def load_columns(i):
                for b in range(2):
                    sp.wait_ge(s["xh"][b].sem, s["xh"][b].last(i))
                    sp.wait_ge(s["xl"][b].sem, s["xl"][b].last(i))
                    sp.dma_start(xT[b][:].rearrange("p c t -> p (c t)"), a["xT"][bass.ds((i * 2 + (b - 2)) * P, P), :]).then_inc(s["xT_in"][b].sem, 16)

            def load_rows(i):
                for b in range(2):
                    sp.wait_ge(s["r"][b].sem, s["r"][b].last(i))
                    sp.dma_start(xt[b][:], a["x"][bass.ds((i * 2 + (b - 2)) * P, P), :]).then_inc(s["xt_in"][b].sem, 16)

            load_columns(1)
            load_rows(1)
            with sp.Fori(2, NT + 1) as i:
                load_columns(i)
                load_rows(i)
                for b in range(2):
                    sp.wait_ge(s["x1"][b].sem, s["x1"][b].last(i))
                    sp.dma_start(x1_rows(i - 1, b), x1[b][:]).then_inc(s["x1_out"][b].sem, 16)
            for b in range(2):
                sp.wait_ge(s["x1"][b].sem, s["x1"][b].now(NT))
                sp.dma_start(x1_rows(NT, b), x1[b][:]).then_inc(s["x1_out"][b].sem, 16)
            for b in range(2):
                sp.wait_ge(s["x1_out"][b].sem, s["x1_out"][b].now(NT))

        @block.gpsimd
        def _(pool):
            ph.credit(pool)
            for b in range(2):
                nc.gpsimd.memset(carry[b][:], 0.0).then_inc(zeroed.sem, 1)
            pool.wait_ge(zeroed.sem, 4)
            with pool.Fori(1, NT + 1) as i:
                for b in range(2):
                    def scale(out, in_, c, k):
                        nc.gpsimd.tensor_tensor(out, in_, decay[b][:, :, c:c + 1].to_broadcast([P, KC, P]),
                                                ALU.mult).then_inc(s["Sh"][b].sem, 1)
                    pool.wait_ge(s["decay"][b].sem, s["decay"][b].now(i))
                    pool.wait_ge(s["y"][b].sem, s["y"][b].last(i))
                    pool.wait_ge(s["Sh"][b].sem, s["Sh"][b].last(i))
                    scale(Sh[b][:, 0], carry[b][:], 0, 0)
                    for c in range(NSUB):
                        pool.wait_ge(s["Sh"][b].sem, s["Sh"][b].part(i, c + 1))
                        pool.wait_ge(s["kvm"][b].sem, s["kvm"][b].part(i, c + 1))
                        nc.gpsimd.tensor_tensor(kvm[b][:], kvm[b][:], Sh[b][:, c], ALU.add).then_inc(s["sum"][b].sem, 1)
                        pool.wait_ge(s["sum"][b].sem, s["sum"][b].part(i, c + 1))
                        scale(Sh[b][:, c + 1] if c < NSUB - 1 else carry[b][:], kvm[b][:], c + 1, c + 1)

        @block.scalar
        def _(act):
            act.wait_ge(consts.sem, consts.now(1))
            nc.scalar.preload_act_table_set("natural_log_exp_and_others")
            with act.Fori(1, NT + 1) as i:
                def gates(b):
                    act.wait_ge(s["z"][b].sem, s["z"][b].now(i))
                    nc.scalar.activation(az[b][:], PJ[0][:], ACT.Abs).then_inc(s["az"][b].sem, 1)
                    act.wait_ge(s["az"][b].sem, s["az"][b].now(i))
                    nc.scalar.activation(az[b][:], az[b][:], ACT.Exp, scale=-1.0).then_inc(s["ez"][b].sem, 1)
                    act.wait_ge(s["ez"][b].sem, s["ez"][b].now(i))
                    nc.scalar.activation(az[b][:], az[b][:], ACT.Ln, bias=1.0).then_inc(s["lz"][b].sem, 1)
                    act.wait_ge(s["v"][b].sem, s["v"][b].now(i))
                    act.wait_ge(s["y"][b].sem, s["y"][b].last(i))
                    nc.scalar.copy(V[b][:], PJ[1][:]).then_inc(s["V"][b].sem, 1)

                def decays(b):
                    act.wait_ge(s["R"][b].sem, s["R"][b].now(i))
                    act.wait_ge(s["yTp"][b].sem, s["yTp"][b].last(i))
                    nc.scalar.activation(eR[b][:], BK[0][:], ACT.Exp).then_inc(s["eR"][b].sem, 1)
                    act.wait_ge(s["yTl"][b].sem, s["yTl"][b].last(i))
                    nc.scalar.activation(enR[b][:], BK[0][:], ACT.Exp, scale=-1.0).then_inc(s["enR"][b].sem, 1)
                    act.wait_ge(s["Sh"][b].sem, s["Sh"][b].part(i, 0))
                    nc.scalar.activation(decay[b][:].rearrange("p c n -> p (c n)"), BK[1][:, 0:KC * (NSUB + 1)],
                                         ACT.Exp).then_inc(s["decay"][b].sem, 1)

                def turned(b):
                    act.wait_ge(s["QTp"][b].sem, s["QTp"][b].now(i))
                    act.wait_ge(s["y"][b].sem, s["y"][b].last(i))
                    nc.scalar.copy(QT[b][:].rearrange("p c t -> p (c t)"), BK[2][:]).then_inc(s["QT"][b].sem, 1)
                    act.wait_ge(s["KTp"][b].sem, s["KTp"][b].now(i))
                    nc.scalar.copy(KT[b][:].rearrange("p c t -> p (c t)"), BK[3][:]).then_inc(s["KT"][b].sem, 1)

                def scaled(b):
                    act.wait_ge(s["yTp"][b].sem, s["yTp"][b].now(i))
                    for c in range(KC):
                        last = nc.scalar.activation(enR[b][:, c * P:(c + 1) * P], BK[(0, 3)[b]][:, c * P:(c + 1) * P],
                                                    ACT.Identity, scale=gamma[:, c:c + 1], bias=beta[:, c:c + 1])
                    last.then_inc(s["yT"][b].sem, 1)

                gates(0)
                decays(0)
                gates(1)
                turned(0)
                decays(1)
                turned(1)
                n1[0].guesses(nc, act, i)
                scaled(0)
                n1[1].guesses(nc, act, i)
                scaled(1)
                n2[0].guesses(nc, act, i)
                n2[1].guesses(nc, act, i)

        @block.vector
        def _(dve):
            dve.wait_ge(consts.sem, consts.now(1))
            def split_x(b, i):
                dve.wait_ge(s["xT_in"][b].sem, s["xT_in"][b].now(i))
                dve.wait_ge(s["k"][b].sem, s["k"][b].last(i))
                nc.vector.tensor_copy(xTh[b][:], xT[b][:]).then_inc(s["xh"][b].sem, 1)
                dve.wait_ge(s["xh"][b].sem, s["xh"][b].now(i))
                nc.vector.tensor_tensor(xTl[b][:], xT[b][:], xTh[b][:].bitcast(F32), ALU.subtract).then_inc(s["xl"][b].sem, 1)

            def gate(b, i):
                dve.wait_ge(s["lz"][b].sem, s["lz"][b].now(i))
                nc.vector.scalar_tensor_tensor(g[b][:], PJ[0][:], 0.0, az[b][:], ALU.min, ALU.subtract).then_inc(s["g"][b].sem, 1)

            def decayed(b, i):
                dve.wait_ge(s["q"][b].sem, s["q"][b].now(i))
                dve.wait_ge(s["eR"][b].sem, s["eR"][b].now(i))
                nc.vector.scalar_tensor_tensor(Qr[b][:], PJ[2][:], float(DH) ** -0.5, eR[b][:], ALU.mult, ALU.mult).then_inc(s["Qr"][b].sem, 1)
                dve.wait_ge(s["k"][b].sem, s["k"][b].now(i))
                dve.wait_ge(s["enR"][b].sem, s["enR"][b].now(i))
                nc.vector.tensor_tensor(Kr[b][:], PJ[3][:], enR[b][:], ALU.mult).then_inc(s["Kr"][b].sem, 1)

            def states(b, i):
                for c in range(NSUB):
                    dve.wait_ge(s["kv"][b].sem, s["kv"][b].part(i, c + 1))
                    dve.wait_ge(s["Sh"][b].sem, s["Sh"][b].part(i, c + 1))
                    nc.vector.tensor_tensor(kvm[b][:], BK[2 + c % 2][:].rearrange("p (c n) -> p c n", c=KC),
                                            heads[:].unsqueeze(1).to_broadcast([P, KC, P]), ALU.mult).then_inc(s["kvm"][b].sem, 1)

            def masked(b, i, banks, first):
                for j in range(first, first + len(banks)):
                    dve.wait_ge(s["A"][b].sem, s["A"][b].part(i, j + 1))
                    nc.vector.tensor_tensor(Am[b][:, j], BK[banks[j - first]][:].rearrange("p (c n) -> p c n", c=KC),
                                            causal[:].unsqueeze(1).to_broadcast([P, KC, P]), ALU.mult).then_inc(s["Am"][b].sem, 1)

            def y_stats(b, i):
                dve.wait_ge(s["y"][b].sem, s["y"][b].now(i))
                n1[b].stats(nc, dve, i, BK[(0, 1)[b]][:])

            def y_normed(b, i):
                n1[b].newton(nc, dve, i)
                n1[b].apply(nc, eR[b][:], BK[(0, 1)[b]][:]).then_inc(s["yn"][b].sem, 1)

            def split_y(b, i):
                dve.wait_ge(s["yT"][b].sem, s["yT"][b].now(i))
                nc.vector.tensor_copy(yTh[b][:].rearrange("p c t -> p (c t)"), enR[b][:]).then_inc(s["yTh"][b].sem, 1)
                dve.wait_ge(s["yTh"][b].sem, s["yTh"][b].now(i))
                nc.vector.tensor_tensor(yTl[b][:].rearrange("p c t -> p (c t)"), enR[b][:],
                                        yTh[b][:].bitcast(F32).rearrange("p c t -> p (c t)"), ALU.subtract).then_inc(s["yTl"][b].sem, 1)

            def x_stats(b, i):
                dve.wait_ge(s["o"][b].sem, s["o"][b].now(i))
                dve.wait_ge(s["xt_in"][b].sem, s["xt_in"][b].now(i))
                dve.wait_ge(s["KTp"][b].sem, s["KTp"][b].now(i))
                nc.vector.tensor_tensor(Qr[b][:], BK[(2, 1)[b]][:], xt[b][:], ALU.add).then_inc(s["r"][b].sem, 1)
                dve.wait_ge(s["r"][b].sem, s["r"][b].now(i))
                n2[b].stats(nc, dve, i, Qr[b][:])

            def x_normed(b, i):
                n2[b].newton(nc, dve, i)
                dve.wait_ge(s["x1_out"][b].sem, s["x1_out"][b].last(i))
                n2[b].apply(nc, x1[b][:], Qr[b][:]).then_inc(s["x1"][b].sem, 1)

            def tiles(i, more):
                gate(0, i)
                decayed(0, i)
                gate(1, i)
                decayed(1, i)
                states(0, i)
                masked(0, i, (0, 1, 0, 1), 0)
                states(1, i)
                if more:
                    split_x(0, i + 1)
                y_stats(0, i)
                masked(1, i, (1, 2), 0)
                y_normed(0, i)
                masked(1, i, (3, 1), 2)
                split_y(0, i)
                y_stats(1, i)
                if more:
                    split_x(1, i + 1)
                y_normed(1, i)
                x_stats(0, i)
                split_y(1, i)
                x_normed(0, i)
                x_stats(1, i)
                x_normed(1, i)

            split_x(0, 1)
            split_x(1, 1)
            with dve.Fori(1, NT) as i:
                tiles(i, True)
            tiles(NT, False)

        @block.tensor
        def _(pe):
            pe.wait_ge(consts.sem, consts.now(1))
            def project(b, i, m):
                name, used = (("Wg", "g"), ("Wv", "V"), ("Wq", "Qr"), ("Wk", "Kr"))[m]
                pe.wait_ge(s[used][1 - b].sem, s[used][1 - b].now(i) if b else s[used][1 - b].last(i))
                pe.wait_ge(s["xl"][b].sem, s["xl"][b].now(i))
                exact3(pe, PJ[m][:], lambda c: xTh[b][:, c, :], lambda c: xTl[b][:, c, :],
                       lambda c: wh[name][:, c, :], lambda c: wl[name][:, c, :]).then_inc(s[("z", "v", "q", "k")[m]][b].sem, 1)

            def log_decays(b, i):
                pe.wait_ge(s["g"][b].sem, s["g"][b].now(i))
                if b == 0:
                    pe.wait_ge(s["yT"][0].sem, s["yT"][0].last(i))
                    pe.wait_ge(s["r"][1].sem, s["r"][1].last(i))
                else:
                    pe.wait_ge(s["enR"][0].sem, s["enR"][0].now(i))
                    pe.wait_ge(s["decay"][0].sem, s["decay"][0].now(i))
                pe.matmul(BK[0][:], cum[:], g[b][:], start=True, stop=True)
                for c in range(KC):
                    last = pe.matmul(BK[1][:, c * (NSUB + 1):(c + 1) * (NSUB + 1)], g[b][:, c * P:(c + 1) * P], sel[:],
                                     start=True, stop=True, skip_group_check=True)
                last.then_inc(s["R"][b].sem, 1)

            def turn(b, i):
                pe.wait_ge(s["Qr"][b].sem, s["Qr"][b].now(i))
                if b == 0:
                    pe.wait_ge(s["r"][0].sem, s["r"][0].last(i))
                    pe.wait_ge(s["yT"][1].sem, s["yT"][1].last(i))
                else:
                    pe.wait_ge(s["kvm"][0].sem, s["kvm"][0].part(i, NSUB))
                for c in range(KC):
                    last = pe.transpose(BK[2][:, c * P:(c + 1) * P], Qr[b][:, c * P:(c + 1) * P], ident[:])
                last.then_inc(s["QTp"][b].sem, 1)
                pe.wait_ge(s["Kr"][b].sem, s["Kr"][b].now(i))
                for c in range(KC):
                    last = pe.transpose(BK[3][:, c * P:(c + 1) * P], Kr[b][:, c * P:(c + 1) * P], ident[:])
                last.then_inc(s["KTp"][b].sem, 1)

            def key_values(b, i):
                pe.wait_ge(s["V"][b].sem, s["V"][b].now(i))
                pe.wait_ge(s["KT"][b].sem, s["KT"][b].now(i))
                pe.wait_ge(s["QT"][b].sem, s["QT"][b].now(i))
                for c in range(NSUB):
                    if c >= 2:
                        pe.wait_ge(s["kvm"][b].sem, s["kvm"][b].part(i, c - 1))
                    for m in range(KC):
                        last = pe.matmul(BK[2 + c % 2][:, m * P:(m + 1) * P],
                                         Kr[b][c * SUB:(c + 1) * SUB, m * P:(m + 1) * P],
                                         V[b][c * SUB:(c + 1) * SUB, m * P:(m + 1) * P], start=True, stop=True,
                                         skip_group_check=True)
                    last.then_inc(s["kv"][b].sem, 1)

            def scores(b, i, banks, free):
                pe.wait_ge(s["KT"][b].sem, s["KT"][b].now(i))
                for j in range(HG):
                    free(j, i)
                    for m in range(KC):
                        last = pe.matmul(BK[banks[j]][:, m * P:(m + 1) * P], KT[b][j * DH:(j + 1) * DH, m, :],
                                         QT[b][j * DH:(j + 1) * DH, m, :], start=True, stop=True, skip_group_check=True)
                    last.then_inc(s["A"][b].sem, 1)

            def free_0(j, i):
                if j == 0:
                    pe.wait_ge(s["enR"][1].sem, s["enR"][1].now(i))
                if j == 1:
                    pe.wait_ge(s["decay"][1].sem, s["decay"][1].now(i))
                if j >= 2:
                    pe.wait_ge(s["Am"][0].sem, s["Am"][0].part(i, j - 1))

            def free_1(j, i):
                if j == 0:
                    pe.wait_ge(s["Am"][0].sem, s["Am"][0].part(i, 4))
                if j == 1:
                    pe.wait_ge(s["kvm"][1].sem, s["kvm"][1].part(i, 3))
                if j == 2:
                    pe.wait_ge(s["kvm"][1].sem, s["kvm"][1].part(i, 4))
                if j == 3:
                    pe.wait_ge(s["Am"][1].sem, s["Am"][1].part(i, 1))

            def outputs(b, i):
                bk = BK[(0, 1)[b]]
                pe.wait_ge(s["Am"][b].sem, s["Am"][b].part(i, HG))
                for m in range(KC):
                    for j in range(HG):
                        h = m * HG + j
                        pe.matmul(bk[:, h * DH:(h + 1) * DH], Am[b][:, j, m, :], V[b][:, h * DH:(h + 1) * DH],
                                  start=(h == 0), stop=False, skip_group_check=True)
                pe.wait_ge(s["Sh"][b].sem, s["Sh"][b].part(i, NSUB))
                for c in range(NSUB):
                    for m in range(KC):
                        last = pe.matmul(bk[c * SUB:(c + 1) * SUB, m * P:(m + 1) * P],
                                         QT[b][:, m, c * SUB:(c + 1) * SUB], Sh[b][:, c, m, :],
                                         start=False, stop=(m == KC - 1), skip_group_check=True)
                last.then_inc(s["y"][b].sem, 1)

            def turn_y(b, i):
                pe.wait_ge(s["yn"][b].sem, s["yn"][b].now(i))
                if b == 1:
                    pe.wait_ge(s["Am"][1].sem, s["Am"][1].part(i, 3))
                for c in range(KC):
                    last = pe.transpose(BK[(0, 3)[b]][:, c * P:(c + 1) * P], eR[b][:, c * P:(c + 1) * P], ident[:])
                last.then_inc(s["yTp"][b].sem, 1)

            def out_proj(b, i):
                pe.wait_ge(s["yTl"][b].sem, s["yTl"][b].now(i))
                if b == 0:
                    pe.wait_ge(s["Am"][1].sem, s["Am"][1].part(i, 2))
                exact3(pe, BK[(2, 1)[b]][:], lambda c: yTh[b][:, c, :], lambda c: yTl[b][:, c, :],
                       lambda c: wh["Wo"][:, c, :], lambda c: wl["Wo"][:, c, :]).then_inc(s["o"][b].sem, 1)

            def tiles(i, more):
                log_decays(0, i)
                for m in range(4):
                    project(1, i, m)
                turn(0, i)
                log_decays(1, i)
                key_values(0, i)
                scores(0, i, (0, 1, 0, 1), free_0)
                turn(1, i)
                outputs(0, i)
                key_values(1, i)
                scores(1, i, (1, 2, 3, 1), free_1)
                if more:
                    project(0, i + 1, 0)
                turn_y(0, i)
                if more:
                    project(0, i + 1, 1)
                out_proj(0, i)
                outputs(1, i)
                if more:
                    project(0, i + 1, 2)
                turn_y(1, i)
                if more:
                    project(0, i + 1, 3)
                out_proj(1, i)

            for m in range(4):
                project(0, 1, m)
            with pe.Fori(1, NT) as i:
                tiles(i, True)
            tiles(NT, False)
    ph.end()
    top.close()


def by_chunk(t):
    return t.rearrange("p (g j d) -> p g j d", g=KC, j=HG)


def heads_of(t):
    return t.rearrange("p (h d) -> p h d", h=H)


def lora_and_projections(nc, K, bank, a):
    top = ExitStack()
    wide = {"base": D, "Wq3": D, "Wk3": D, "Wv3": D, "AR": FULL_RATE, "BG": H + DH}
    wh = {n: top.enter_context(nc.sbuf_tensor(f"ffn_{n}_hi", [P, KC, w], F32R)) for n, w in wide.items()}
    wl = {n: top.enter_context(nc.sbuf_tensor(f"ffn_{n}_lo", [P, KC, w], F32R)) for n, w in wide.items()}
    lbh = top.enter_context(nc.sbuf_tensor("ffn_loraB_hi", [P, D], F32R))
    lbl = top.enter_context(nc.sbuf_tensor("ffn_loraB_lo", [P, D], F32R))
    load_split(nc, "ffn_w", [(a[n], wh[n][:].rearrange("p c n -> p (c n)"), wl[n][:].rearrange("p c n -> p (c n)"))
                             for n in wide] + [(a["loraB"], lbh[:], lbl[:])])
    ph = Phase(nc, "ffn")
    bk = [bank[0:4], bank[4:8]]
    ident = ph.sb("ident", [P, P])
    base_b, router_b = ph.sb("base_b", [P, D]), ph.sb("router_b", [P, EXPERTS])
    order = ph.sb("order", [P, EXPERTS])
    wg2 = ph.sb("wg2", [DH, D])
    x1, xb = ph.sb2("x1", [P, D]), ph.sb2("xb", [P, D])
    xh, xl = ph.sb2("xh", [P, KC, P], F32R), ph.sb2("xl", [P, KC, P], F32R)
    lg, top8 = ph.sb2("lg", [P, EXPERTS]), ph.sb2("top8", [P, 8])
    idx, idf = ph.sb2("idx", [P, 8], U32), ph.sb2("idf", [P, 8])
    mask, ex, tot, neg = ph.sb2("mask", [P, EXPERTS]), ph.sb2("ex", [P, EXPERTS]), ph.sb2("tot", [P, 2]), ph.sb2("neg", [P, 1])
    mid, mh, ml = ph.sb2("mid", [P, P]), ph.sb2("mh", [P, P], F32R), ph.sb2("ml", [P, P], F32R)
    x2 = ph.sb2("x2", [P, D])
    q3, kn, sq, sg = ph.sb2("q3", [P, D]), ph.sb2("kn", [P, D]), ph.sb2("sq", [P, D]), ph.sb2("sg", [P, D])
    qe, one = ph.sb2("qe", [P, D]), ph.sb("one", [P, 1])
    kw = ph.sb2("kw", [P, 6, H])
    te = ph.sb2("te", [P, HG, KC, DH + 1])
    g1, g1T = ph.sb2("g1", [P, DH]), ph.sb2("g1T", [DH, P])
    qT, kT = ph.sb2("qT", [P, D]), ph.sb2("kT", [P, D])
    s = {}
    for n, per in [("x1_in", 16), ("xb", 1), ("x1T", 1), ("x1h", 1), ("x1l", 1), ("lm", 1), ("lg", 1), ("top", 1),
                   ("idx", 1), ("idf", 1), ("m1", 1), ("mask", 1), ("neg", 1), ("ex", 1), ("em", 1), ("tot", 1), ("inv", 1),
                   ("gate", 1), ("mid", 1), ("midT", 1), ("mh", 1), ("ml", 1), ("ffn", 1), ("r", 1), ("x2", 1),
                   ("x2T", 1), ("x2h", 1), ("x2l", 1), ("bg", 1), ("q", 1), ("k", 1), ("v", 1), ("q3", 1), ("eta", 1),
                   ("sq", 1), ("ss", 1), ("kn1", 1), ("kn2", 1), ("kn3", 1), ("kn4", 1), ("m1b", 1), ("m2b", 1), ("kr", 1), ("kn", 1), ("te", 1),
                   ("eta2", 1), ("qTp", 1), ("kTp", 1), ("qT", 1), ("kT", 1), ("g1", 1), ("g1Tp", 1), ("g1T", 1), ("gt", 1), ("sg", 1),
                   ("eta_e", 1), ("eta_1", 1), ("qe", 1), ("q_e", 1), ("q_l", 1), ("sg_e", 1), ("sg_l", 1),
                   ("stored", 16 * 6)]:
        s[n] = ph.counters_of_two(n, per)
    nx = [Norm(ph, "nx", b, 1e-5) for b in range(2)]
    consts = ph.counter("consts", 16 * 5)
    ones_made = ph.counter("ones", 1)

    with nc.Block() as block:
        def rows(name, i, b):
            return a[name][bass.ds((i * 2 + (b - 2)) * P, P), :]

        @block.sync
        def _(sp):
            for t, src in ((ident, K["ident"]), (base_b, a["base_b"]), (router_b, a["router_b"]), (order, K["order"]),
                           (wg2, a["Wg2"])):
                sp.dma_start(t[:], src).then_inc(consts.sem, 16)

            def load(b, i):
                sp.wait_ge(s["x1T"][b].sem, s["x1T"][b].last(i))
                sp.wait_ge(s["xb"][b].sem, s["xb"][b].last(i))
                sp.dma_start(x1[b][:], rows("x1", i, b)).then_inc(s["x1_in"][b].sem, 16)

            def store(b, i):
                for made, buf, name in (("x2", x2, "x2"), ("q3", q3, "q3"), ("qT", qT, "qT"), ("kT", kT, "kT")):
                    sp.wait_ge(s[made][b].sem, s[made][b].now(i))
                    sp.dma_start(rows(name, i, b), buf[b][:]).then_inc(s["stored"][b].sem, 16)
                sp.wait_ge(s["te"][b].sem, s["te"][b].now(i))
                sp.wait_ge(s["eta2"][b].sem, s["eta2"][b].now(i))
                sp.dma_start(rows("te", i, b), te[b][:].rearrange("p j g d -> p (j g d)")).then_inc(s["stored"][b].sem, 16)
                sp.wait_ge(s["sg"][b].sem, s["sg"][b].now(i))
                sp.dma_start(rows("sg", i, b), sg[b][:]).then_inc(s["stored"][b].sem, 16)

            load(1, 1)
            load(0, 1)
            with sp.Fori(1, NT) as i:
                load(1, i + 1)
                store(1, i)
                load(0, i + 1)
                store(0, i)
            store(1, NT)
            store(0, NT)
            for b in range(2):
                sp.wait_ge(s["stored"][b].sem, s["stored"][b].now(NT))

        @block.gpsimd
        def _(pool):
            ph.credit(pool)
            nc.gpsimd.memset(one[:], 1.0).then_inc(ones_made.sem, 1)
            pool.wait_ge(ones_made.sem, ones_made.now(1))
            pool.wait_ge(consts.sem, consts.now(1))

            def with_bias(b, i):
                pool.wait_ge(s["x1_in"][b].sem, s["x1_in"][b].now(i))
                pool.wait_ge(s["r"][b].sem, s["r"][b].last(i))
                nc.gpsimd.tensor_tensor(xb[b][:], x1[b][:], base_b[:], ALU.add).then_inc(s["xb"][b].sem, 1)

            def rates(b, i):
                pool.wait_ge(s["eta"][b].sem, s["eta"][b].now(i))
                sig = kw[b][:, 5].rearrange("p (g j) -> p g j", g=KC)
                pool.wait_ge(s["stored"][b].sem, s["stored"][b].last(i))
                nc.gpsimd.tensor_tensor(te[b][:, :, :, DH].rearrange("p j g -> p g j"), sig, sig,
                                        ALU.add).then_inc(s["eta2"][b].sem, 1)

            with_bias(1, 1)
            with pool.Fori(1, NT) as i:
                with_bias(0, i)
                rates(1, i)
                with_bias(1, i + 1)
                rates(0, i)
            with_bias(0, NT)
            rates(1, NT)
            rates(0, NT)

        @block.scalar
        def _(act):
            act.wait_ge(consts.sem, consts.now(1))
            act.wait_ge(ones_made.sem, ones_made.now(1))
            nc.scalar.preload_act_table_set("natural_log_exp_and_others")
            def lead_x1(b, i):
                act.wait_ge(s["x1T"][b].sem, s["x1T"][b].now(i))
                act.wait_ge(s["q"][b].sem, s["q"][b].last(i))
                nc.scalar.copy(xh[b][:].rearrange("p c t -> p (c t)"), bk[b][3][:]).then_inc(s["x1h"][b].sem, 1)

            def soft(b, i):
                act.wait_ge(s["neg"][b].sem, s["neg"][b].now(i))
                nc.scalar.activation(ex[b][:], lg[b][:], ACT.Exp, bias=neg[b][:, 0:1]).then_inc(s["ex"][b].sem, 1)

            def lead_mid(b, i):
                act.wait_ge(s["midT"][b].sem, s["midT"][b].now(i))
                nc.scalar.copy(mh[b][:], bk[b][3][:, 0:P]).then_inc(s["mh"][b].sem, 1)

            def lead_x2(b, i):
                act.wait_ge(s["x2T"][b].sem, s["x2T"][b].now(i))
                nc.scalar.copy(xh[b][:].rearrange("p c t -> p (c t)"), bk[b][0][:]).then_inc(s["x2h"][b].sem, 1)

            def keys_squared(b, i):
                act.wait_ge(s["bg"][b].sem, s["bg"][b].now(i))
                nc.scalar.copy(g1[b][:], bk[b][1][:, H:H + DH]).then_inc(s["g1"][b].sem, 1)
                act.wait_ge(s["k"][b].sem, s["k"][b].now(i))
                nc.scalar.activation(sq[b][:], bk[b][3][:], ACT.Square).then_inc(s["sq"][b].sem, 1)

            def keys_root(b, i):
                act.wait_ge(s["kn1"][b].sem, s["kn1"][b].now(i))
                nc.scalar.activation(kw[b][:, 1], kw[b][:, 0], ACT.Ln).then_inc(s["kn2"][b].sem, 1)
                act.wait_ge(s["kn2"][b].sem, s["kn2"][b].now(i))
                nc.scalar.activation(kw[b][:, 2], kw[b][:, 1], ACT.Exp, scale=-0.5).then_inc(s["kn3"][b].sem, 1)

            def sigmoid(b, i, dst, src, e, log, made):
                nc.scalar.activation(dst[:], src, ACT.Exp, scale=-1.0).then_inc(s[e][b].sem, 1)
                act.wait_ge(s[e][b].sem, s[e][b].now(i))
                nc.scalar.activation(dst[:], dst[:], ACT.Ln, bias=one[:, 0:1]).then_inc(s[log][b].sem, 1)
                act.wait_ge(s[log][b].sem, s[log][b].now(i))
                nc.scalar.activation(dst[:], dst[:], ACT.Exp, scale=-1.0).then_inc(s[made][b].sem, 1)

            def gate_inputs(b, i):
                nc.scalar.activation(kw[b][:, 5], bk[b][1][:, 0:H], ACT.Exp, scale=-1.0).then_inc(s["eta_e"][b].sem, 1)
                act.wait_ge(s["q"][b].sem, s["q"][b].now(i))
                act.wait_ge(s["q3"][b].sem, s["q3"][b].last(i))
                sigmoid(b, i, qe[b], bk[b][2][:], "q_e", "q_l", "qe")

            def turned(b, i, more):
                act.wait_ge(s["g1Tp"][b].sem, s["g1Tp"][b].now(i))
                nc.scalar.copy(g1T[b][:], bk[b][3][0:DH, 0:P]).then_inc(s["g1T"][b].sem, 1)
                act.wait_ge(s["stored"][b].sem, s["stored"][b].last(i))
                act.wait_ge(s["kTp"][b].sem, s["kTp"][b].now(i))
                nc.scalar.copy(kT[b][:], bk[b][1][:]).then_inc(s["kT"][b].sem, 1)
                if more:
                    lead_x1(b, i + 1)
                act.wait_ge(s["gt"][b].sem, s["gt"][b].now(i))
                act.wait_ge(s["stored"][b].sem, s["stored"][b].last(i))
                sigmoid(b, i, sg[b], bk[b][0][:], "sg_e", "sg_l", "sg")
                act.wait_ge(s["qTp"][b].sem, s["qTp"][b].now(i))
                nc.scalar.copy(qT[b][:], bk[b][2][:]).then_inc(s["qT"][b].sem, 1)

            def half(front, back, more=True):
                if back:
                    lead_x2(*back)
                if front:
                    soft(*front)
                if back:
                    keys_squared(*back)
                if front:
                    lead_mid(*front)
                if back:
                    keys_root(*back)
                    gate_inputs(*back)
                if front:
                    nx[front[0]].guesses(nc, act, front[1])
                if back:
                    turned(*back, more)

            lead_x1(1, 1)
            lead_x1(0, 1)
            half((1, 1), None)
            with act.Fori(1, NT) as i:
                half((0, i), (1, i))
                half((1, i + 1), (0, i))
            half((0, NT), (1, NT), more=False)
            half(None, (0, NT), more=False)

        @block.vector
        def _(dve):
            dve.wait_ge(consts.sem, consts.now(1))
            def trail_x1(b, i):
                dve.wait_ge(s["x1h"][b].sem, s["x1h"][b].now(i))
                nc.vector.tensor_tensor(xl[b][:].rearrange("p c t -> p (c t)"), bk[b][3][:],
                                        xh[b][:].bitcast(F32).rearrange("p c t -> p (c t)"), ALU.subtract).then_inc(s["x1l"][b].sem, 1)

            def step(name, b, i, ins):
                ins.then_inc(s[name][b].sem, 1)
                dve.wait_ge(s[name][b].sem, s[name][b].now(i))

            def route(b, i):
                dve.wait_ge(s["lm"][b].sem, s["lm"][b].now(i))
                step("lg", b, i, nc.vector.tensor_tensor(lg[b][:], bk[b][1][:, P:P + EXPERTS], router_b[:], ALU.add))
                nc.vector.memset(neg[b][:], 0.0)
                step("top", b, i, nc.vector.max(top8[b][:], lg[b][:]))
                nc.vector.tensor_scalar(neg[b][:], top8[b][:, 0:1], -1.0, None, ALU.mult).then_inc(s["neg"][b].sem, 1)
                step("idx", b, i, nc.vector.max_index(idx[b][:], top8[b][:], lg[b][:]))
                step("idf", b, i, nc.vector.tensor_copy(idf[b][:], idx[b][:]))
                step("m1", b, i, nc.vector.tensor_scalar(mask[b][:], order[:], idf[b][:, 0:1], None, ALU.is_equal))
                step("mask", b, i, nc.vector.scalar_tensor_tensor(mask[b][:], order[:], idf[b][:, 1:2], mask[b][:], ALU.is_equal, ALU.add))
                dve.wait_ge(s["ex"][b].sem, s["ex"][b].now(i))
                step("em", b, i, nc.vector.tensor_tensor(ex[b][:], ex[b][:], mask[b][:], ALU.mult))
                step("tot", b, i, nc.vector.tensor_reduce(tot[b][:, 0:1], ex[b][:], AX, ALU.add))
                step("inv", b, i, nc.vector.reciprocal(tot[b][:, 1:2], tot[b][:, 0:1]))
                step("gate", b, i, nc.vector.tensor_scalar(ex[b][:], ex[b][:], tot[b][:, 1:2], 2.0, ALU.mult, ALU.mult))
                nc.vector.tensor_tensor(mid[b][:].rearrange("p (e r) -> p e r", e=EXPERTS),
                                        bk[b][1][:, 0:P].rearrange("p (e r) -> p e r", e=EXPERTS),
                                        ex[b][:].unsqueeze(2).to_broadcast([P, EXPERTS, RANK]), ALU.mult).then_inc(s["mid"][b].sem, 1)

            def trail_mid(b, i):
                dve.wait_ge(s["mh"][b].sem, s["mh"][b].now(i))
                nc.vector.tensor_tensor(ml[b][:], bk[b][3][:, 0:P], mh[b][:].bitcast(F32), ALU.subtract).then_inc(s["ml"][b].sem, 1)

            def norm_stats(b, i):
                dve.wait_ge(s["ffn"][b].sem, s["ffn"][b].now(i))
                dve.wait_ge(s["xb"][b].sem, s["xb"][b].now(i))
                dve.wait_ge(s["stored"][b].sem, s["stored"][b].last(i))
                step("r", b, i, nc.vector.tensor_tensor(x2[b][:], bk[b][2][:], xb[b][:], ALU.add))
                nx[b].stats(nc, dve, i, x2[b][:])

            def norm_apply(b, i):
                nx[b].newton(nc, dve, i)
                nx[b].apply(nc, x2[b][:], x2[b][:]).then_inc(s["x2"][b].sem, 1)

            def trail_x2(b, i):
                dve.wait_ge(s["x2h"][b].sem, s["x2h"][b].now(i))
                nc.vector.tensor_tensor(xl[b][:].rearrange("p c t -> p (c t)"), bk[b][0][:],
                                        xh[b][:].bitcast(F32).rearrange("p c t -> p (c t)"), ALU.subtract).then_inc(s["x2l"][b].sem, 1)

            def keys(b, i):
                dve.wait_ge(s["sq"][b].sem, s["sq"][b].now(i))
                step("ss", b, i, nc.vector.tensor_reduce(kw[b][:, 0], heads_of(sq[b][:]), AX, ALU.add))
                nc.vector.tensor_scalar(kw[b][:, 0], kw[b][:, 0], 1e-6, None, ALU.add).then_inc(s["kn1"][b].sem, 1)
                dve.wait_ge(s["kn3"][b].sem, s["kn3"][b].now(i))
                step("kn4", b, i, nc.vector.tensor_tensor(kw[b][:, 3], kw[b][:, 2], kw[b][:, 2], ALU.mult))
                step("m1b", b, i, nc.vector.tensor_tensor(kw[b][:, 3], kw[b][:, 3], kw[b][:, 0], ALU.mult))
                step("m2b", b, i, nc.vector.tensor_scalar(kw[b][:, 3], kw[b][:, 3], -0.5, 1.5, ALU.mult, ALU.add))
                step("kr", b, i, nc.vector.tensor_tensor(kw[b][:, 4], kw[b][:, 3], kw[b][:, 2], ALU.mult))
                step("kn", b, i, nc.vector.tensor_tensor(heads_of(kn[b][:]), heads_of(bk[b][3][:]),
                                                      kw[b][:, 4].unsqueeze(2).to_broadcast([P, H, DH]), ALU.mult))

            def gates(b, i):
                dve.wait_ge(s["eta_e"][b].sem, s["eta_e"][b].now(i))
                step("eta_1", b, i, nc.vector.tensor_scalar(kw[b][:, 5], kw[b][:, 5], 1.0, None, ALU.add))
                nc.vector.reciprocal(kw[b][:, 5], kw[b][:, 5]).then_inc(s["eta"][b].sem, 1)
                dve.wait_ge(s["qe"][b].sem, s["qe"][b].now(i))
                dve.wait_ge(s["stored"][b].sem, s["stored"][b].last(i))
                nc.vector.tensor_tensor(q3[b][:], bk[b][2][:], qe[b][:], ALU.mult).then_inc(s["q3"][b].sem, 1)

            def targets(b, i):
                dve.wait_ge(s["kn"][b].sem, s["kn"][b].now(i))
                dve.wait_ge(s["v"][b].sem, s["v"][b].now(i))
                nc.vector.tensor_tensor(te[b][:, :, :, 0:DH].rearrange("p j g d -> p g j d"), by_chunk(bk[b][0][:]),
                                        by_chunk(kn[b][:]), ALU.subtract).then_inc(s["te"][b].sem, 1)

            def half(front, back, more=True):
                if back:
                    trail_x2(*back)
                if front:
                    route(*front)
                    trail_mid(*front)
                if back:
                    keys(*back)
                if back:
                    targets(*back)
                if front:
                    norm_stats(*front)
                if back:
                    gates(*back)
                if front:
                    norm_apply(*front)
                if back and more:
                    trail_x1(back[0], back[1] + 1)

            trail_x1(1, 1)
            trail_x1(0, 1)
            half((1, 1), None)
            with dve.Fori(1, NT) as i:
                half((0, i), (1, i))
                half((1, i + 1), (0, i))
            half((0, NT), (1, NT), more=False)
            half(None, (0, NT), more=False)


        @block.tensor
        def _(pe):
            pe.wait_ge(consts.sem, consts.now(1))
            def turn(b, i, src, dst, got, made):
                pe.wait_ge(s[got][b].sem, s[got][b].now(i))
                for c in range(KC):
                    last = pe.transpose(dst[:, c * P:(c + 1) * P], src[:, c * P:(c + 1) * P], ident[:])
                last.then_inc(s[made][b].sem, 1)

            def times(out, b, name, stop=True):
                return exact3(pe, out, lambda c: xh[b][:, c, :], lambda c: xl[b][:, c, :],
                              lambda c: wh[name][:, c, :], lambda c: wl[name][:, c, :], stop=stop)

            def ffn(b, i):
                pe.wait_ge(s["x1l"][b].sem, s["x1l"][b].now(i))
                pe.wait_ge(s["kT"][b].sem, s["kT"][b].last(i))
                times(bk[b][1][:, 0:FULL_RATE], b, "AR").then_inc(s["lm"][b].sem, 1)
                pe.wait_ge(s["qT"][b].sem, s["qT"][b].last(i))
                times(bk[b][2][:], b, "base", stop=False)

            def lora_lead(b, i):
                pe.wait_ge(s["mid"][b].sem, s["mid"][b].now(i))
                pe.wait_ge(s["g1T"][b].sem, s["g1T"][b].last(i))
                pe.transpose(bk[b][3][:, 0:P], mid[b][:], ident[:]).then_inc(s["midT"][b].sem, 1)

            def lora(b, i):
                pe.wait_ge(s["ml"][b].sem, s["ml"][b].now(i))
                exact3(pe, bk[b][2][:], lambda c: mh[b][:], lambda c: ml[b][:], lambda c: lbh[:], lambda c: lbl[:],
                       start=False, n=1).then_inc(s["ffn"][b].sem, 1)

            def projections(b, i):
                pe.wait_ge(s["x2l"][b].sem, s["x2l"][b].now(i))
                pe.wait_ge(s["mid"][b].sem, s["mid"][b].now(i))
                times(bk[b][1][:, 0:H + DH], b, "BG").then_inc(s["bg"][b].sem, 1)
                times(bk[b][3][:], b, "Wk3").then_inc(s["k"][b].sem, 1)

            def turns(b, i, more):
                pe.wait_ge(s["g1"][b].sem, s["g1"][b].now(i))
                pe.wait_ge(s["kn"][b].sem, s["kn"][b].now(i))
                pe.transpose(bk[b][3][0:DH, 0:P], g1[b][:], ident[:]).then_inc(s["g1Tp"][b].sem, 1)
                pe.wait_ge(s["eta_e"][b].sem, s["eta_e"][b].now(i))
                turn(b, i, kn[b], bk[b][1], "kn", "kTp")
                if more:
                    turn_x1(b, i + 1)
                pe.wait_ge(s["g1T"][b].sem, s["g1T"][b].now(i))
                pe.wait_ge(s["te"][b].sem, s["te"][b].now(i))
                pe.matmul(bk[b][0][:], g1T[b][:], wg2[:], start=True, stop=True).then_inc(s["gt"][b].sem, 1)
                turn(b, i, q3[b], bk[b][2], "q3", "qTp")

            def turn_x1(b, i):
                pe.wait_ge(s["g1T"][b].sem, s["g1T"][b].last(i))
                turn(b, i, x1[b], bk[b][3], "x1_in", "x1T")

            def half(front, back, more=True):
                if back:
                    b, i = back
                    pe.wait_ge(s["sg_e"][b].sem, s["sg_e"][b].last(i))
                    turn(b, i, x2[b], bk[b][0], "x2", "x2T")
                if front:
                    ffn(*front)
                if back:
                    projections(*back)
                if front:
                    lora_lead(*front)
                if back:
                    times(bk[back[0]][0][:], back[0], "Wv3").then_inc(s["v"][back[0]].sem, 1)
                if front:
                    lora(*front)
                if back:
                    times(bk[back[0]][2][:], back[0], "Wq3").then_inc(s["q"][back[0]].sem, 1)
                    turns(*back, more)

            turn_x1(1, 1)
            turn_x1(0, 1)
            half((1, 1), None)
            with pe.Fori(1, NT) as i:
                half((0, i), (1, i))
                half((1, i + 1), (0, i))
            half((0, NT), (1, NT), more=False)
            half(None, (0, NT), more=False)
    ph.end()
    top.close()


def ttt_recurrence(nc, K, bank, a):
    ST, NI = NCH, NT
    HALF = ST // 2
    ph = Phase(nc, "ttt")
    bS, bH, bQ, bA, bK, bC = bank[0:6]
    G = KC
    R64 = HG * TTT
    ident = ph.sb("ident", [P, P])
    tri = ph.sb("tri", [P, R64])
    w_row, b_row, w2 = ph.sb("w_row", [P, G, DH]), ph.sb("b_row", [P, G, DH]), ph.sb("w2", [P, G, DH])
    seq, own = ph.sb("seq", [P, 2]), ph.sb("own", [P, HG])
    zero = ph.sb("zero", [P, 2 * P])
    cK, cQ = ph.sb("cK", [P, B, G, ST * TTT]), ph.sb("cQ", [P, B, G, ST * TTT])
    te = ph.sb("te", [P, ST, G, DH + 1])
    bw = ph.sb("bw", [P, ST, G, DH])
    neta = ph.sb("neta", [P, ST, G])
    KB = [ph.sb(f"KB{r}", [P, G, B, HG, TTT]) for r in range(ST)]
    QB = [ph.sb(f"QB{r}", [P, G, B, HG, TTT]) for r in range(ST)]
    S = ph.sb("S", [P, G, B, DH])
    kb = ph.sb("kb", [P, G, P])
    am = ph.sb("am", [P, G, R64])
    u = ph.sb("u", [P, G, DH])
    ub = ph.sb("ub", [P, G, B, DH])
    cross = ph.sb("cross", [P, G, P])
    qh = ph.sb("qh", [R64, ST, B, G, DH])
    c1, c2, c3, c4, c5, c6 = (ph.sb(f"c{k}", [P, G, DH]) for k in range(6))
    eps = ph.sb("eps", [P, 1])
    m = ph.sb("m", [P, 8, G])
    re = ph.sb("re", [P, G])
    s = {n: ph.counter(n, per) for n, per in
         [("cK", 16 * 4), ("te", 16 * 8), ("bw1", 2), ("bw", 2), ("neta", 2), ("blocks", ST), ("S", ST), ("KH", ST), ("QS", ST),
          ("A", ST), ("KT", ST), ("kb", ST), ("am", ST), ("s1", ST), ("xc", ST), ("sq", ST), ("s2", ST), ("sd", ST), ("rs", ST),
          ("re", ST), ("xw", ST), ("hat", ST), ("t", ST), ("gw", ST), ("r1", ST), ("p", ST), ("r2", ST), ("v1", ST), ("q", ST),
          ("v2", ST), ("u", ST), ("ub", ST), ("KK", ST), ("cross", ST), ("KS", ST), ("SU", ST), ("AU", ST), ("qh", ST), ("stored0", 16 * 8), ("stored1", 16 * 8)]}
    consts = ph.counter("consts", 16 * 6)
    zeroed = ph.counter("zeroed", 2)
    w2_made = ph.counter("w2", 1)
    s0_made = ph.counter("s0", 1)

    with nc.Block() as block:
        @block.sync
        def _(sp):
            for t, src in ((ident, K["ident"]), (tri, K["tri"]), (w_row, a["ln_w"]), (b_row, a["ln_b"]), (seq, K["seq"]),
                           (own, K["own"])):
                sp.dma_start(t[:] if len(t.shape) < 3 else t[:].rearrange("p g d -> p (g d)"), src).then_inc(consts.sem, 16)

            def load(i):
                sp.wait_ge(s["blocks"].sem, s["blocks"].last(i))
                for b in range(B):
                    for dst, name in ((cK, "kT"), (cQ, "qT")):
                        sp.dma_start(dst[:, b].rearrange("p g t -> p (g t)"), a[name][bass.ds((i * 2 + (b - 2)) * P, P), :]).then_inc(s["cK"].sem, 16)
                sp.wait_ge(s["bw"].sem, s["bw"].last(i))
                sp.wait_ge(s["neta"].sem, s["neta"].last(i))
                for b in range(B):
                    for j in range(HG):
                        rows = a["te"][bass.ds((i * 2 + (b - 2)) * P, P), :]
                        src = rows.rearrange("(c t) (j e) -> j t c e", t=TTT, j=HG)[j]
                        r = b * R64 + j * TTT
                        sp.dma_start(te[r:r + TTT].rearrange("t c g e -> t c (g e)"), src).then_inc(s["te"].sem, 16)

            def store(i):
                for f in range(2):
                    sp.wait_ge(s["qh"].sem, s["qh"].part(i, (f + 1) * HALF))
                    for b in range(B):
                        for j in range(HG):
                            rows = a["qh"][bass.ds((i * 2 + (b - 2)) * P + f * HALF * TTT, HALF * TTT), :]
                            sp.dma_start(rows.rearrange("(c t) (j e) -> j t c e", t=TTT, j=HG)[j],
                                         qh[j * TTT:(j + 1) * TTT, f * HALF:(f + 1) * HALF, b].rearrange("t c g e -> t c (g e)")).then_inc(s[f"stored{f}"].sem, 16)

            load(1)
            with sp.Fori(2, NI + 1) as i:
                load(i)
                store(i - 1)
            store(NI)
            for f in range(2):
                sp.wait_ge(s[f"stored{f}"].sem, s[f"stored{f}"].now(NI))

        @block.gpsimd
        def _(pool):
            ph.credit(pool)
            nc.gpsimd.memset(zero[:], 0.0).then_inc(zeroed.sem, 1)
            nc.gpsimd.memset(cross[:], 0.0).then_inc(zeroed.sem, 1)
            pool.wait_ge(zeroed.sem, zeroed.now(1))
            pool.wait_ge(consts.sem, consts.now(1))

            def spread(n):
                for b in range(B):
                    for src, dst in ((cK, KB[n]), (cQ, QB[n])):
                        shape = [P, G, HG, TTT]
                        last = nc.gpsimd.tensor_tensor(
                            dst[:, :, b], src[:, b, :, n * TTT:(n + 1) * TTT].unsqueeze(2).to_broadcast(shape),
                            own[:].unsqueeze(1).unsqueeze(3).to_broadcast(shape), ALU.mult)
                last.then_inc(s["blocks"].sem, 1)

            with pool.Fori(1, NI + 1) as i:
                pool.wait_ge(s["te"].sem, s["te"].now(i))
                pool.wait_ge(s["cK"].sem, s["cK"].now(i))
                for f in range(2):
                    pool.wait_ge(s["re"].sem, s["re"].part(i, (f + 1) * HALF - ST))
                    pool.wait_ge(s["gw"].sem, s["gw"].part(i, (f + 1) * HALF - ST))
                    c = slice(f * HALF, (f + 1) * HALF)
                    nc.gpsimd.tensor_tensor(bw[:, c], b_row[:].unsqueeze(1).to_broadcast([P, HALF, G, DH]), te[:, c, :, 0:DH],
                                            ALU.subtract).then_inc(s["bw1"].sem, 1)
                    nc.gpsimd.tensor_tensor(neta[:, c], zero[:, 0:HALF * G].rearrange("p (c g) -> p c g", g=G), te[:, c, :, DH],
                                            ALU.subtract).then_inc(s["neta"].sem, 1)
                    pool.wait_ge(s["bw1"].sem, s["bw1"].part(i, f + 1))
                    nc.gpsimd.tensor_tensor(bw[:, c], bw[:, c], w_row[:].unsqueeze(1).to_broadcast([P, HALF, G, DH]),
                                            ALU.mult).then_inc(s["bw"].sem, 1)
                    for n in range(f * HALF, (f + 1) * HALF):
                        pool.wait_ge(s["QS"].sem, s["QS"].part(i, n + 1 - ST))
                        spread(n)
            for n in range(2):
                pool.wait_ge(s["QS"].sem, s["QS"].part(NI + 1, n + 1 - ST))
                spread(n)

        @block.scalar
        def _(act):
            act.wait_ge(consts.sem, consts.now(1))
            act.wait_ge(s0_made.sem, s0_made.now(1))
            act.wait_ge(w2_made.sem, 3)
            act.wait_ge(zeroed.sem, zeroed.now(1))
            nc.scalar.preload_act_table_set("sqrt_and_others")
            nc.scalar.copy(S[:].rearrange("p g b e -> p (g b e)"), bS[:, 0:2 * P]).then_inc(s["S"].sem, 1)
            act.wait_ge(s["s2"].sem, s["s2"].part(1, 1))
            nc.scalar.activation(m[:, 2], m[:, 1], ACT.Sqrt, scale=1.0 / DH, bias=eps[:, 0:1]).then_inc(s["sd"].sem, 1)
            with act.Fori(1, NI + 1) as i:
                for n in range(ST):
                    act.wait_ge(s["KT"].sem, s["KT"].part(i, n + 1))
                    nc.scalar.copy(kb[:].rearrange("p g n -> p (g n)"), bK[:]).then_inc(s["kb"].sem, 1)
                    act.wait_ge(s["KK"].sem, s["KK"].part(i, n + 1))
                    act.wait_ge(s["KH"].sem, s["KH"].part(i, n + 1))
                    for b in range(B):
                        r = slice(b * R64, (b + 1) * R64)
                        last = nc.scalar.copy(cross[r, :, r], bC[r, :].rearrange("p (g n) -> p g n", g=G)[:, :, r])
                    last.then_inc(s["cross"].sem, 1)
                    act.wait_ge(s["SU"].sem, s["SU"].part(i, n + 1))
                    act.wait_ge(s["QS"].sem, s["QS"].part(i, n + 1))
                    act.wait_ge(s["KS"].sem, s["KS"].part(i, n + 1))
                    nc.scalar.copy(S[:].rearrange("p g b e -> p (g b e)"), bS[:, 0:2 * P]).then_inc(s["S"].sem, 1)
                    act.wait_ge(s["s2"].sem, s["s2"].part(i, n + 2))
                    nc.scalar.activation(m[:, 2], m[:, 1], ACT.Sqrt, scale=1.0 / DH, bias=eps[:, 0:1]).then_inc(s["sd"].sem, 1)
                    act.wait_ge(s["AU"].sem, s["AU"].part(i, n + 1))
                    if n % HALF == 0:
                        act.wait_ge(s[f"stored{n // HALF}"].sem, s[f"stored{n // HALF}"].last(i))
                    nc.scalar.copy(qh[:, n].rearrange("p b g e -> p (b g e)"), bQ[0:R64, 0:2 * P]).then_inc(s["qh"].sem, 1)

        @block.vector
        def _(dve):
            dve.wait_ge(consts.sem, consts.now(1))
            nc.vector.memset(eps[:], 1e-6).then_inc(w2_made.sem, 1)
            nc.vector.tensor_tensor(w2[:], w_row[:], w_row[:], ALU.mult).then_inc(w2_made.sem, 1)
            dve.wait_ge(w2_made.sem, 3)
            with dve.Fori(1, NI + 1) as i:
                for n in range(ST):
                    def step(name, ins):
                        ins.then_inc(s[name].sem, 1)
                        dve.wait_ge(s[name].sem, s[name].part(i, n + 1))

                    def over_e(t):
                        return t.unsqueeze(2).to_broadcast([P, G, DH])
                    kh = bH[:, 0:P].rearrange("p (g e) -> p g e", g=G)
                    dve.wait_ge(s["KH"].sem, s["KH"].part(i, n + 1))
                    step("s1", nc.vector.tensor_reduce(m[:, 0], kh, AX, ALU.add))
                    step("xc", nc.vector.scalar_tensor_tensor(c1[:], over_e(m[:, 0]), -1.0 / DH, kh, ALU.mult, ALU.add))
                    step("sq", nc.vector.tensor_tensor(c2[:], c1[:], c1[:], ALU.mult))
                    step("s2", nc.vector.tensor_reduce(m[:, 1], c2[:], AX, ALU.add))
                    nc.vector.tensor_tensor(c3[:], c1[:], w2[:], ALU.mult).then_inc(s["xw"].sem, 1)
                    dve.wait_ge(s["sd"].sem, s["sd"].part(i, n + 1))
                    step("rs", nc.vector.reciprocal(m[:, 3], m[:, 2]))
                    if n % HALF == 0:
                        dve.wait_ge(s["neta"].sem, s["neta"].part(i, n // HALF + 1))
                        dve.wait_ge(s["bw"].sem, s["bw"].part(i, n // HALF + 1))
                    nc.vector.tensor_tensor(re[:], m[:, 3], neta[:, n], ALU.mult).then_inc(s["re"].sem, 1)
                    nc.vector.tensor_tensor(c1[:], c1[:], over_e(m[:, 3]), ALU.mult).then_inc(s["hat"].sem, 1)
                    dve.wait_ge(s["xw"].sem, s["xw"].part(i, n + 1))
                    step("t", nc.vector.tensor_tensor(c3[:], c3[:], over_e(m[:, 3]), ALU.mult))
                    step("gw", nc.vector.tensor_tensor(c3[:], c3[:], bw[:, n], ALU.add))
                    dve.wait_ge(s["hat"].sem, s["hat"].part(i, n + 1))
                    nc.vector.tensor_tensor(c2[:], c3[:], c1[:], ALU.mult).then_inc(s["p"].sem, 1)
                    nc.vector.tensor_reduce(m[:, 4], c3[:], AX, ALU.add).then_inc(s["r1"].sem, 1)
                    dve.wait_ge(s["p"].sem, s["p"].part(i, n + 1))
                    step("r2", nc.vector.tensor_reduce(m[:, 5], c2[:], AX, ALU.add))
                    dve.wait_ge(s["r1"].sem, s["r1"].part(i, n + 1))
                    nc.vector.scalar_tensor_tensor(c4[:], over_e(m[:, 4]), -1.0 / DH, c3[:], ALU.mult, ALU.add).then_inc(s["v1"].sem, 1)
                    step("q", nc.vector.tensor_tensor(c5[:], c1[:], over_e(m[:, 5]), ALU.mult))
                    dve.wait_ge(s["v1"].sem, s["v1"].part(i, n + 1))
                    step("v2", nc.vector.scalar_tensor_tensor(c6[:], c5[:], -1.0 / DH, c4[:], ALU.mult, ALU.add))
                    dve.wait_ge(s["re"].sem, s["re"].part(i, n + 1))
                    dve.wait_ge(s["SU"].sem, s["SU"].part(i, n))
                    dve.wait_ge(s["AU"].sem, s["AU"].part(i, n))
                    step("u", nc.vector.tensor_tensor(u[:], c6[:], over_e(re[:]), ALU.mult))
                    nc.vector.tensor_tensor(ub[:], u[:].unsqueeze(2).to_broadcast([P, G, B, DH]),
                                            seq[:].unsqueeze(1).unsqueeze(3).to_broadcast([P, G, B, DH]), ALU.mult).then_inc(s["ub"].sem, 1)
                    dve.wait_ge(s["A"].sem, s["A"].part(i, n + 1))
                    nc.vector.tensor_tensor(am[:], bA[:, 0:2 * P].rearrange("p (g n) -> p g n", g=G),
                                            tri[:].unsqueeze(1).to_broadcast([P, G, R64]), ALU.mult).then_inc(s["am"].sem, 1)
            nc.vector.memset(m[:, 1], 1.0).then_inc(s["s2"].sem, 1)

        @block.tensor
        def _(pe):
            pe.wait_ge(consts.sem, consts.now(1))
            pe.wait_ge(zeroed.sem, zeroed.now(1))
            pe.matmul(bS[:, 0:2 * P], zero[:, 0:P], zero[:], start=True, stop=False, skip_group_check=True).then_inc(s0_made.sem, 1)

            def keys_times_state(n):
                for g in range(G):
                    for b in range(B):
                        last = pe.matmul(bH[b * R64:(b + 1) * R64, g * DH:(g + 1) * DH], KB[n][:, g, b].rearrange("p j t -> p (j t)"),
                                         S[:, g, b, :], start=(g == 0), stop=False, skip_group_check=True)
                return last

            def scores(n, g, b):
                return pe.matmul(bA[b * R64:(b + 1) * R64, g * R64:(g + 1) * R64], KB[n][:, g, b].rearrange("p j t -> p (j t)"),
                                 QB[n][:, g, b].rearrange("p j t -> p (j t)"), start=True, stop=True, skip_group_check=True)

            def keys_times_next(n, g):
                return pe.matmul(bC[:, g * P:(g + 1) * P], KB[n][:].rearrange(both)[:, g],
                                 KB[(n + 1) % ST][:].rearrange(both)[:, g], start=True, stop=True, skip_group_check=True)

            both = "p g b j t -> p g (b j t)"

            pe.wait_ge(s["blocks"].sem, s["blocks"].part(1, 2))
            pe.wait_ge(s["S"].sem, s["S"].part(1, 1))
            keys_times_state(0)
            pe.matmul(bH[:, 0:P], zero[:, 0:P], zero[:, 0:P], start=False, stop=True, skip_group_check=True).then_inc(s["KH"].sem, 1)
            for g in range(G):
                for b in range(B):
                    last = scores(0, g, b)
            last.then_inc(s["A"].sem, 1)
            for g in range(G):
                last = pe.transpose(bK[:, g * P:(g + 1) * P], KB[0][:].rearrange(both)[:, g], ident[:])
            last.then_inc(s["KT"].sem, 1)
            for g in range(G):
                last = keys_times_next(0, g)
            last.then_inc(s["KK"].sem, 1)
            with pe.Fori(1, NI + 1) as i:
                for n in range(ST):
                    QBf = QB[n][:].rearrange("p g b j t -> p g b (j t)")
                    pe.wait_ge(s["S"].sem, s["S"].part(i, n + 1))
                    pe.wait_ge(s["xc"].sem, s["xc"].part(i, n + 1))
                    pe.wait_ge(s["blocks"].sem, s["blocks"].part(i, n + 2))
                    keys_times_state((n + 1) % ST).then_inc(s["KS"].sem, 1)
                    pe.wait_ge(s["qh"].sem, s["qh"].part(i, n))
                    for g in range(G):
                        for b in range(B):
                            last = pe.matmul(bQ[0:R64, (b * G + g) * DH:(b * G + g + 1) * DH], QBf[:, g, b, :], S[:, g, b, :],
                                             start=(g == 0 and b == 0), stop=False, skip_group_check=True)
                    last.then_inc(s["QS"].sem, 1)
                    pe.wait_ge(s["u"].sem, s["u"].part(i, n + 1))
                    pe.wait_ge(s["cross"].sem, s["cross"].part(i, n + 1))
                    for g in range(G):
                        last = pe.matmul(bH[:, g * DH:(g + 1) * DH], cross[:, g, :], u[:, g, :], start=False, stop=True, skip_group_check=True)
                    last.then_inc(s["KH"].sem, 1)
                    pe.wait_ge(s["ub"].sem, s["ub"].part(i, n + 1))
                    pe.wait_ge(s["kb"].sem, s["kb"].part(i, n + 1))
                    for g in range(G):
                        last = pe.matmul(bS[:, g * B * DH:(g + 1) * B * DH], kb[:, g, :], ub[:, g].rearrange("p b e -> p (b e)"),
                                         start=False, stop=False, skip_group_check=True)
                    last.then_inc(s["SU"].sem, 1)
                    pe.wait_ge(s["am"].sem, s["am"].part(i, n + 1))
                    for g in range(G):
                        last = pe.matmul(bQ[0:R64, 0:2 * P].rearrange("p (b g e) -> p g b e", b=B, g=G)[:, g], am[:, g, :],
                                         ub[:, g].rearrange("p b e -> p (b e)"),
                                         start=False, stop=(g == G - 1), skip_group_check=True)
                    last.then_inc(s["AU"].sem, 1)
                    for g in range(G):
                        for b in range(B):
                            last = scores((n + 1) % ST, g, b)
                    last.then_inc(s["A"].sem, 1)
                    for g in range(G):
                        last = pe.transpose(bK[:, g * P:(g + 1) * P], KB[(n + 1) % ST][:].rearrange(both)[:, g], ident[:])
                    last.then_inc(s["KT"].sem, 1)
                    pe.wait_ge(s["blocks"].sem, s["blocks"].part(i, n + 3))
                    for g in range(G):
                        last = keys_times_next((n + 1) % ST, g)
                    last.then_inc(s["KK"].sem, 1)
    ph.end()


def attention_output(nc, K, bank, a):
    top = ExitStack()
    wh = top.enter_context(nc.sbuf_tensor("out_w_hi", [P, KC, D], F32R))
    wl = top.enter_context(nc.sbuf_tensor("out_w_lo", [P, KC, D], F32R))
    load_split(nc, "out_w", [(a["Wo3"], wh[:].rearrange("p c n -> p (c n)"), wl[:].rearrange("p c n -> p (c n)"))])
    ph = Phase(nc, "out")
    bk = [bank[0:4], bank[4:8]]
    ident = ph.sb("ident", [P, P])
    w_all, b_all, norm_w = ph.sb("w_all", [P, D]), ph.sb("b_all", [P, D]), ph.sb("norm_w", [P, KC])
    eps6, eps5 = ph.sb("eps6", [P, 1]), ph.sb("eps5", [P, 1])
    names = ["qh", "q3", "sg", "x2"]
    t = {n: ph.sb2(n, [P, D]) for n in names}
    xc, sq, og, oT, r, x3T = (ph.sb2(n, [P, D]) for n in ("xc", "sq", "og", "oT", "r", "x3T"))
    wg, qg = ph.sb2("wg", [P, D]), ph.sb2("qg", [P, D])
    oh, ol = ph.sb2("oh", [P, KC, P], F32R), ph.sb2("ol", [P, KC, P], F32R)
    w = ph.sb2("w", [P, 8, H])
    st, mv = ph.sb2("st", [P, 6]), ph.sb2("mv", [P, 4])
    s = {}
    for n, per in [("in", 16 * 3), ("x2_in", 16), ("s1", 1), ("xc", 1), ("sq", 1), ("s2", 1), ("sd", 1), ("rs", 1), ("hat", 1), ("ow", 1), ("wg", 1),
                   ("qb", 1), ("qg", 1), ("og", 1), ("sq2", 1), ("s3", 1), ("sd2", 1), ("rs2", 1), ("o5", 1), ("oTp", 1), ("oT", 1), ("oh", 1), ("ol", 1),
                   ("o", 1), ("r", 1), ("st", 1), ("mv", 1), ("sd3", 1), ("rs3", 1), ("x3", 1), ("x3Tp", 1), ("x3T", 1), ("stored", 32)]:
        s[n] = ph.counters_of_two(n, per)
    consts = ph.counter("consts", 16 * 4)
    epsed = ph.counter("eps", 2)

    def rows(name, i, b):
        return a[name][bass.ds((i * 2 + (b - 2)) * P, P), :]

    def by_place(v):
        return v.rearrange("p (g j e) -> p j g e", g=KC, j=HG)

    def placed(v):
        return v.rearrange("p (j g e) -> p j g e", g=KC, j=HG)

    def each_head(v):
        return v.unsqueeze(2).to_broadcast([P, H, DH])

    with nc.Block() as block:
        @block.sync
        def _(sp):
            for dst, src in ((ident, K["ident"]), (w_all, a["w_all"]), (b_all, a["b_all"]), (norm_w, a["norm_w"])):
                sp.dma_start(dst[:], src).then_inc(consts.sem, 16)

            def load(b, i):
                sp.wait_ge(s["og"][b].sem, s["og"][b].last(i))
                for n in ("qh", "q3", "sg"):
                    sp.dma_start(t[n][b][:], rows(n, i, b)).then_inc(s["in"][b].sem, 16)

            def load_x2(b, i):
                sp.wait_ge(s["r"][b].sem, s["r"][b].last(i))
                sp.dma_start(t["x2"][b][:], rows("x2", i, b)).then_inc(s["x2_in"][b].sem, 16)

            def store(b, i):
                sp.wait_ge(s["x3"][b].sem, s["x3"][b].now(i))
                sp.dma_start(rows("x3", i, b), r[b][:]).then_inc(s["stored"][b].sem, 16)
                sp.wait_ge(s["x3T"][b].sem, s["x3T"][b].now(i))
                sp.dma_start(rows("x3T", i, b), x3T[b][:]).then_inc(s["stored"][b].sem, 16)

            for b in (1, 0):
                load(b, 1)
                load_x2(b, 1)
            with sp.Fori(1, NT) as i:
                for b in (1, 0):
                    load(b, i + 1)
                    store(b, i)
                    load_x2(b, i + 1)
            store(1, NT)
            store(0, NT)
            for b in range(2):
                sp.wait_ge(s["stored"][b].sem, s["stored"][b].now(NT))

        @block.gpsimd
        def _(pool):
            ph.credit(pool)
            nc.gpsimd.memset(eps6[:], 1e-6).then_inc(epsed.sem, 1)
            nc.gpsimd.memset(eps5[:], 1e-5).then_inc(epsed.sem, 1)
            pool.wait_ge(consts.sem, consts.now(1))

            def gated(b, i):
                def step(name, ins):
                    ins.then_inc(s[name][b].sem, 1)
                    pool.wait_ge(s[name][b].sem, s[name][b].now(i))
                pool.wait_ge(s["in"][b].sem, s["in"][b].now(i))
                pool.wait_ge(s["og"][b].sem, s["og"][b].last(i))
                nc.gpsimd.tensor_tensor(placed(wg[b][:]), placed(w_all[:]), by_place(t["sg"][b][:]), ALU.mult).then_inc(s["wg"][b].sem, 1)
                step("qb", nc.gpsimd.tensor_tensor(placed(qg[b][:]), placed(b_all[:]), by_place(t["q3"][b][:]), ALU.add))
                nc.gpsimd.tensor_tensor(placed(qg[b][:]), placed(qg[b][:]), by_place(t["sg"][b][:]), ALU.mult).then_inc(s["qg"][b].sem, 1)

            gated(1, 1)
            with pool.Fori(1, NT) as i:
                gated(0, i)
                gated(1, i + 1)
            gated(0, NT)

        @block.scalar
        def _(act):
            act.wait_ge(consts.sem, consts.now(1))
            act.wait_ge(epsed.sem, epsed.now(1))
            def square(b, i, src, got, made):
                act.wait_ge(s[got][b].sem, s[got][b].now(i))
                nc.scalar.activation(sq[b][:], src[b][:], ACT.Square).then_inc(s[made][b].sem, 1)

            def root(b, i, col, got, made):
                act.wait_ge(s[got][b].sem, s[got][b].now(i))
                nc.scalar.activation(w[b][:, col + 1], w[b][:, col], ACT.Sqrt, scale=1.0 / DH, bias=eps6[:, 0:1]).then_inc(s[made][b].sem, 1)

            def scaled(b, i):
                act.wait_ge(s["oTp"][b].sem, s["oTp"][b].now(i))
                for c in range(KC):
                    last = nc.scalar.activation(oT[b][:, c * P:(c + 1) * P], bk[b][0][:, c * P:(c + 1) * P], ACT.Identity,
                                                scale=norm_w[:, c:c + 1])
                last.then_inc(s["oT"][b].sem, 1)

            def root_x(b, i):
                act.wait_ge(s["mv"][b].sem, s["mv"][b].now(i))
                nc.scalar.activation(mv[b][:, 2:3], mv[b][:, 1:2], ACT.Sqrt, bias=eps5[:, 0:1]).then_inc(s["sd3"][b].sem, 1)

            def turned(b, i):
                act.wait_ge(s["x3Tp"][b].sem, s["x3Tp"][b].now(i))
                act.wait_ge(s["stored"][b].sem, s["stored"][b].last(i))
                nc.scalar.copy(x3T[b][:], bk[b][2][:]).then_inc(s["x3T"][b].sem, 1)

            def half(front, back):
                if back:
                    root(*back, 4, "s3", "sd2")
                    scaled(*back)
                if front:
                    square(*front, xc, "xc", "sq")
                    root(*front, 1, "s2", "sd")
                    square(*front, og, "og", "sq2")
                if back:
                    root_x(*back)
                    turned(*back)

            nc.scalar.preload_act_table_set("sqrt_and_others")
            half((1, 1), None)
            with act.Fori(1, NT) as i:
                half((0, i), (1, i))
                half((1, i + 1), (0, i))
            half((0, NT), (1, NT))
            half(None, (0, NT))

        @block.vector
        def _(dve):
            dve.wait_ge(consts.sem, consts.now(1))
            def step(name, b, i, ins):
                ins.then_inc(s[name][b].sem, 1)
                dve.wait_ge(s[name][b].sem, s[name][b].now(i))

            def centre(b, i):
                dve.wait_ge(s["in"][b].sem, s["in"][b].now(i))
                dve.wait_ge(s["og"][b].sem, s["og"][b].last(i))
                step("s1", b, i, nc.vector.tensor_reduce(w[b][:, 0], heads_of(t["qh"][b][:]), AX, ALU.add))
                step("xc", b, i, nc.vector.scalar_tensor_tensor(heads_of(xc[b][:]), each_head(w[b][:, 0]), -1.0 / DH,
                                                             heads_of(t["qh"][b][:]), ALU.mult, ALU.add))

            def unit(b, i):
                dve.wait_ge(s["sq"][b].sem, s["sq"][b].now(i))
                step("s2", b, i, nc.vector.tensor_reduce(w[b][:, 1], heads_of(sq[b][:]), AX, ALU.add))
                dve.wait_ge(s["sd"][b].sem, s["sd"][b].now(i))
                step("rs", b, i, nc.vector.reciprocal(w[b][:, 3], w[b][:, 2]))
                step("hat", b, i, nc.vector.tensor_tensor(heads_of(xc[b][:]), heads_of(xc[b][:]), each_head(w[b][:, 3]), ALU.mult))
                dve.wait_ge(s["wg"][b].sem, s["wg"][b].now(i))
                step("ow", b, i, nc.vector.tensor_tensor(xc[b][:], xc[b][:], wg[b][:], ALU.mult))
                dve.wait_ge(s["qg"][b].sem, s["qg"][b].now(i))
                dve.wait_ge(s["oTp"][b].sem, s["oTp"][b].last(i))
                nc.vector.tensor_tensor(by_place(og[b][:]), placed(xc[b][:]), placed(qg[b][:]), ALU.add).then_inc(s["og"][b].sem, 1)

            def rms(b, i):
                dve.wait_ge(s["sq2"][b].sem, s["sq2"][b].now(i))
                step("s3", b, i, nc.vector.tensor_reduce(w[b][:, 4], heads_of(sq[b][:]), AX, ALU.add))
                dve.wait_ge(s["sd2"][b].sem, s["sd2"][b].now(i))
                step("rs2", b, i, nc.vector.reciprocal(w[b][:, 6], w[b][:, 5]))
                nc.vector.tensor_tensor(heads_of(og[b][:]), heads_of(og[b][:]), each_head(w[b][:, 6]), ALU.mult).then_inc(s["o5"][b].sem, 1)

            def split(b, i):
                dve.wait_ge(s["oT"][b].sem, s["oT"][b].now(i))
                step("oh", b, i, nc.vector.tensor_copy(oh[b][:].rearrange("p c t -> p (c t)"), oT[b][:]))
                nc.vector.tensor_tensor(ol[b][:].rearrange("p c t -> p (c t)"), oT[b][:],
                                        oh[b][:].bitcast(F32).rearrange("p c t -> p (c t)"), ALU.subtract).then_inc(s["ol"][b].sem, 1)

            def norm(b, i):
                dve.wait_ge(s["o"][b].sem, s["o"][b].now(i))
                dve.wait_ge(s["x2_in"][b].sem, s["x2_in"][b].now(i))
                dve.wait_ge(s["stored"][b].sem, s["stored"][b].last(i))
                step("r", b, i, nc.vector.tensor_tensor(r[b][:], bk[b][1][:], t["x2"][b][:], ALU.add))
                step("st", b, i, nc.vector.bn_stats(st[b][:], r[b][:]))
                nc.vector.memset(mv[b][:, 3:4], 0.0)
                nc.vector.bn_aggr(mv[b][:, 0:2], st[b][:]).then_inc(s["mv"][b].sem, 1)
                dve.wait_ge(s["sd3"][b].sem, s["sd3"][b].now(i))
                step("rs3", b, i, nc.vector.reciprocal(mv[b][:, 3:4], mv[b][:, 2:3]))
                nc.vector.tensor_scalar(r[b][:], r[b][:], mv[b][:, 0:1], mv[b][:, 3:4], ALU.subtract, ALU.mult).then_inc(s["x3"][b].sem, 1)

            def half(front, back):
                if back:
                    rms(*back)
                    split(*back)
                if front:
                    centre(*front)
                    unit(*front)
                if back:
                    norm(*back)

            half((1, 1), None)
            with dve.Fori(1, NT) as i:
                half((0, i), (1, i))
                half((1, i + 1), (0, i))
            half((0, NT), (1, NT))
            half(None, (0, NT))

        @block.tensor
        def _(pe):
            pe.wait_ge(consts.sem, consts.now(1))
            def back(b, i):
                pe.wait_ge(s["o5"][b].sem, s["o5"][b].now(i))
                for c in range(KC):
                    last = pe.transpose(bk[b][0][:, c * P:(c + 1) * P], og[b][:, c * P:(c + 1) * P], ident[:])
                last.then_inc(s["oTp"][b].sem, 1)
                pe.wait_ge(s["ol"][b].sem, s["ol"][b].now(i))
                exact3(pe, bk[b][1][:], lambda c: oh[b][:, c, :], lambda c: ol[b][:, c, :],
                       lambda c: wh[:, c, :], lambda c: wl[:, c, :]).then_inc(s["o"][b].sem, 1)
                pe.wait_ge(s["x3"][b].sem, s["x3"][b].now(i))
                for c in range(KC):
                    last = pe.transpose(bk[b][2][:, c * P:(c + 1) * P], r[b][:, c * P:(c + 1) * P], ident[:])
                last.then_inc(s["x3Tp"][b].sem, 1)

            with pe.Fori(1, NT + 1) as i:
                back(1, i)
                back(0, i)
    ph.end()
    top.close()


class Routing:

    def __init__(self, nc, ph, dve, bank, w6, slot6, expert_row):
        N = B * NT
        self.nc, self.dve, self.bank, self.w6, self.slot6, self.expert_row = nc, dve, bank, w6, slot6, expert_row
        self.bias = ph.sb("bias", [P, MOE_E])
        self.low4, self.low16 = ph.sb("low4", [P, 16]), ph.sb("low16", [P, MOE_E * MOE_E])
        self.order, self.token = ph.sb("order", [P, EXPERTS]), ph.sb("token", [P, 1])
        self.filled, self.tiles = ph.sb("filled", [P, N * P // SLOTS]), ph.sb("tiles", [P, TILES])
        self.sc, self.sfc = ph.sb("sc", [P, N, MOE_E]), ph.sb("sfc", [P, N, MOE_E])
        self.pairs, self.gs = ph.sb("pairs", [P, N * MOE_G, 6]), ph.sb("gs", [P, N, MOE_G])
        self.c1, self.c2 = ph.sb("c1", [P, N, MOE_E, MOE_E]), ph.sb("c2", [P, N // 2, MOE_E, MOE_E])
        self.rank, self.sel = ph.sb("rank", [P, N, MOE_E]), ph.sb("sel", [P, N, MOE_E])
        self.tot, self.inv = ph.sb("tot", [P, N]), ph.sb("inv", [P, N])
        self.each, self.slot = ph.sb("each", [P, N, MOE_E]), ph.sb("slot", [P, N, MOE_E])
        self.load, self.taken, self.base = ph.sb("load", [P, MOE_E]), ph.sb("taken", [P, MOE_E]), ph.sb("base", [P, MOE_E])
        self.slot_f, self.of_tile, self.row = ph.sb("slot_f", [P, N, TOP]), ph.sb("of_tile", [P, TILES]), ph.sb("row", [P, TILES])
        self.scored, self.chain, self.chosen, self.counted, self.counts_read, self.placed = (
            nc.alloc_semaphore(name=f"route_{n}") for n in ("scored", "chain", "chosen", "counted", "counts_read", "placed"))
        self.count = 0

    def semaphores(self):
        return [self.scored, self.chain, self.chosen, self.counted, self.counts_read, self.placed]

    def link(self, ins):
        self.count += 1
        ins.then_inc(self.chain, 1)
        self.dve.wait_ge(self.chain, self.count)

    def view(self, c, *dims):
        n = int(np.prod(dims))
        names = "abc"[:len(dims)]
        flat = c[:].rearrange("p n e f -> p (n e f)")[:, 0:n]
        return flat.rearrange("p (" + " ".join(names) + ") -> p " + " ".join(names), **dict(zip(names, dims)))

    def groups(self):
        nc, N = self.nc, B * NT
        self.dve.wait_ge(self.scored, 1)
        self.link(nc.vector.tensor_tensor(self.sfc[:], self.sc[:], self.bias[:].unsqueeze(1).to_broadcast([P, N, MOE_E]), ALU.add))
        v, pairs = self.sfc[:].rearrange("p n (g k) -> p (n g) k", g=MOE_G), self.pairs
        nc.vector.tensor_tensor(pairs[:, :, 0:3], v[:, :, 0:3], v[:, :, 1:4], ALU.add)
        nc.vector.tensor_tensor(pairs[:, :, 3:5], v[:, :, 0:2], v[:, :, 2:4], ALU.add)
        self.link(nc.vector.tensor_tensor(pairs[:, :, 5:6], v[:, :, 0:1], v[:, :, 3:4], ALU.add))
        self.link(nc.vector.tensor_reduce(self.gs[:].rearrange("p n g -> p (n g)"), pairs[:], AX, ALU.max))

    def equal_before(self, vals, m, lower):
        shape, a1 = [P, B * NT, m, m], self.view(self.c1, B * NT, m * m)
        a4 = a1.rearrange("p n (e f) -> p n e f", e=m)
        self.link(self.nc.vector.tensor_tensor(a4, vals.unsqueeze(2).to_broadcast(shape), vals.unsqueeze(3).to_broadcast(shape), ALU.is_equal))
        self.link(self.nc.vector.tensor_tensor(a1, a1, lower[:].unsqueeze(1).to_broadcast([P, B * NT, m * m]), ALU.mult))

    def larger(self, vals, m):
        half = B * NT // 2
        shape, a1, a2 = [P, half, m, m], self.view(self.c1, B * NT, m * m), self.view(self.c2, half, m * m)
        a4 = a2.rearrange("p n (e f) -> p n e f", e=m)
        for n in (slice(0, half), slice(half, None)):
            v = vals[:, n]
            self.link(self.nc.vector.tensor_tensor(a4, v.unsqueeze(2).to_broadcast(shape), v.unsqueeze(3).to_broadcast(shape), ALU.is_gt))
            self.link(self.nc.vector.tensor_tensor(a1[:, n], a1[:, n], a2, ALU.add))

    def ranks(self, m):
        N = B * NT
        out = self.rank[:].rearrange("p n e -> p (n e)")[:, 0:N * m]
        self.link(self.nc.vector.tensor_reduce(out, self.view(self.c1, N * m, m), AX, ALU.add))
        return out

    def group_choice(self):
        nc = self.nc
        self.equal_before(self.gs[:], MOE_G, self.low4)
        self.larger(self.gs[:], MOE_G)
        g_rank, gs = self.ranks(MOE_G), self.gs[:].rearrange("p n g -> p (n g)")
        self.link(nc.vector.tensor_scalar(gs, g_rank, 1.5, None, ALU.is_lt))
        v = self.sfc[:].rearrange("p n (g k) -> p (n g) k", g=MOE_G)
        self.link(nc.vector.tensor_tensor(v, v, gs.unsqueeze(2).to_broadcast([P, B * NT * MOE_G, MOE_E // MOE_G]), ALU.mult))

    def choice(self):
        self.ranks(MOE_E)
        self.nc.vector.tensor_scalar(self.sel[:], self.rank[:], TOP - 0.5, None, ALU.is_lt).then_inc(self.chosen, 1)

    def weights(self):
        nc, N, sc = self.nc, B * NT, self.sc
        self.dve.wait_ge(self.chosen, 1)
        self.link(nc.vector.tensor_tensor(sc[:], self.sel[:], sc[:], ALU.mult))
        self.link(nc.vector.tensor_reduce(self.tot[:], sc[:], AX, ALU.add))
        self.link(nc.vector.tensor_scalar(self.tot[:], self.tot[:], 1e-20, None, ALU.add))
        self.link(nc.vector.reciprocal(self.inv[:], self.tot[:]))
        self.link(nc.vector.tensor_scalar(self.inv[:], self.inv[:], 2.5, None, ALU.mult))
        self.link(nc.vector.tensor_tensor(sc[:], sc[:], self.inv[:].unsqueeze(2).to_broadcast([P, N, MOE_E]), ALU.mult))

    def counts(self):
        nc, N = self.nc, B * NT
        self.dve.wait_ge(self.counted, 2)
        nc.vector.tensor_copy(self.slot[:].rearrange("p n e -> p (n e)"), self.bank[6][:, 0:N * MOE_E]).then_inc(self.counts_read, 1)
        nc.vector.tensor_copy(self.each[:].rearrange("p n e -> p (n e)"), self.bank[7][:, 0:N * MOE_E]).then_inc(self.counts_read, 1)

    def earlier_tiles(self):
        nc, N = self.nc, B * NT
        self.dve.wait_ge(self.counts_read, 2)
        shape, low = [P, N, MOE_E, N], self.low16[:].rearrange("p (n m) -> p n m", n=N)
        self.link(nc.vector.tensor_tensor(self.c1[:], self.each[:].rearrange("p n e -> p e n").unsqueeze(1).to_broadcast(shape),
                                          low.unsqueeze(2).to_broadcast(shape), ALU.mult))

    def place_in_expert(self):
        nc = self.nc
        earlier = self.view(self.c2, B * NT, MOE_E)
        self.link(nc.vector.tensor_reduce(earlier, self.c1[:], AX, ALU.add))
        self.link(nc.vector.tensor_tensor(self.slot[:], self.slot[:], earlier, ALU.add))

    def slots(self):
        nc, N, NK = self.nc, B * NT, B * NT * P // SLOTS
        self.link(nc.vector.tensor_reduce(self.load[:], self.each[:].rearrange("p n e -> p e n"), AX, ALU.add))
        a1 = self.view(self.c1, MOE_E, NK)
        self.link(nc.vector.tensor_tensor(a1, self.load[:].unsqueeze(2).to_broadcast([P, MOE_E, NK]),
                                          self.filled[:].unsqueeze(1).to_broadcast([P, MOE_E, NK]), ALU.is_gt))
        self.link(nc.vector.tensor_reduce(self.taken[:], a1, AX, ALU.add))
        self.link(nc.vector.tensor_tensor(self.c1[:, 0], self.taken[:].unsqueeze(1).to_broadcast([P, MOE_E, MOE_E]),
                                          self.low16[:].rearrange("p (e f) -> p e f", e=MOE_E), ALU.mult))
        self.link(nc.vector.tensor_reduce(self.base[:], self.c1[:, 0], AX, ALU.add))
        self.link(nc.vector.tensor_tensor(self.taken[:], self.taken[:], self.base[:], ALU.add))
        self.link(nc.vector.scalar_tensor_tensor(self.slot[:], self.base[:].unsqueeze(1).to_broadcast([P, N, MOE_E]), float(SLOTS), self.slot[:],
                                                 ALU.mult, ALU.add))

    def slots_of_tokens(self):
        nc, shape = self.nc, [P, B * NT, TOP, MOE_E]
        a1, a2 = self.view(self.c1, *shape[1:]), self.view(self.c2, *shape[1:])
        self.link(nc.vector.tensor_tensor(a1, self.rank[:].unsqueeze(2).to_broadcast(shape),
                                          self.order[:, 0:TOP].unsqueeze(1).unsqueeze(3).to_broadcast(shape), ALU.is_equal))
        self.link(nc.vector.tensor_tensor(a2, a1, self.slot[:].unsqueeze(2).to_broadcast(shape), ALU.mult))
        self.link(nc.vector.tensor_reduce(self.slot_f[:], a2, AX, ALU.add))
        nc.vector.tensor_copy(self.slot6[:], self.slot_f[:]).then_inc(self.placed, 1)

    def weights_of_tokens(self):
        nc, shape = self.nc, [P, B * NT, TOP, MOE_E]
        a1, a2 = self.view(self.c1, *shape[1:]), self.view(self.c2, *shape[1:])
        self.link(nc.vector.tensor_tensor(a1, self.rank[:].unsqueeze(2).to_broadcast(shape),
                                          self.order[:, 0:TOP].unsqueeze(1).unsqueeze(3).to_broadcast(shape), ALU.is_equal))
        self.link(nc.vector.tensor_tensor(a2, a1, self.sc[:].unsqueeze(2).to_broadcast(shape), ALU.mult))
        self.link(nc.vector.tensor_reduce(self.w6[:], a2, AX, ALU.add))

    def rows_of_tiles(self):
        nc, a1, row, of_tile = self.nc, self.view(self.c1, TILES, MOE_E), self.row, self.of_tile
        self.link(nc.vector.tensor_tensor(a1, self.taken[:].unsqueeze(1).to_broadcast([P, TILES, MOE_E]),
                                          self.tiles[:].unsqueeze(2).to_broadcast([P, TILES, MOE_E]), ALU.is_le))
        self.link(nc.vector.tensor_reduce(of_tile[:], a1, AX, ALU.add))
        self.link(nc.vector.tensor_scalar(of_tile[:], of_tile[:], MOE_E - 1.0, None, ALU.min))
        self.link(nc.vector.memset(row[:, 0:2], 0.0))
        self.link(nc.vector.tensor_tensor(row[:, 2:], of_tile[:, 2:], of_tile[:, 0:TILES - 2], ALU.is_equal))
        self.link(nc.vector.tensor_scalar(row[:], row[:], float(NOWHERE), self.token[:, 0:1], ALU.mult, ALU.add))
        self.link(nc.vector.scalar_tensor_tensor(row[:], of_tile[:], float(P), row[:], ALU.mult, ALU.add))
        self.link(nc.vector.tensor_copy(self.expert_row[:], row[:]))


def shared_experts(nc, K, bank, a, acc, w6, slot6, x_row, y_row, expert_row, xh, xl):
    N, NB = B * NT, 4
    TB = N * P // NB
    ph = Phase(nc, "moe")
    GU, DN = 2 * KC * MOE_I, 3 * D
    guf, guh, gul = ph.sb("guf", [P, GU]), ph.sb("guh", [P, 2, KC, MOE_I], F32R), ph.sb("gul", [P, 2, KC, MOE_I], F32R)
    dnf, dnh, dnl = ph.sb("dnf", [P, DN]), ph.sb("dnh", [P, 3, D], F32R), ph.sb("dnl", [P, 3, D], F32R)
    ih, il = ph.sb("ih", [P, 3, TB], F32R), ph.sb("il", [P, 3, TB], F32R)
    sil = ph.sb2("sil", [P, TB])
    gh, gl, gf = ph.sb("gh", [P, KC, MOE_E], F32R), ph.sb("gl", [P, KC, MOE_E], F32R), ph.sb("gf", [P, KC * MOE_E])
    before, ones = ph.sb("before", [P, P]), ph.sb("ones", [P, P])
    ident, pair, table = ph.sb("ident", [P, P]), ph.sb("pair", [P, N, TOP, 2]), ph.sb("table", [TILES, SLOTS, 2])
    NH = 3 * NB
    s = {n: ph.counter(n, per) for n, per in
         [("acc_in", 16), ("gu_in", 16), ("dn_in", 16), ("guh", 1), ("gul", 1), ("dnh", 1), ("dnl", 1), ("gu", NH), ("sil", NH), ("prod", NH),
          ("ih", NH), ("il", NH), ("dn", N), ("acc", N)]}
    gate_in, consts, freed, lead, trail, logits_made, logits_out, logits_turned, given, listed, turned, rows_made = (
        nc.alloc_semaphore(name=f"slots_{n}") for n in
        ("gate_in", "consts", "freed", "lead", "trail", "logits_made", "logits_out", "logits_turned", "given", "listed", "turned", "rows_made"))
    with nc.Block() as block:
        routing = Routing(nc, ph, nc.vector, bank, w6, slot6, expert_row)
        logits = routing.view(routing.c1, N * P)[0:MOE_E]

        @block.sync
        def _(sp):
            sp.dma_start(gf[:], a["gate_w"]).then_inc(gate_in, 16)
            with sp.Fori(1, NS + 1) as i:
                sp.wait_ge(s["gul"].sem, s["gul"].last(i))
                sp.wait_ge(s["guh"].sem, s["guh"].last(i))
                sp.dma_start(guf[:], a["GU"][bass.ds((i + (MOE_E - 1)) * P, P), :]).then_inc(s["gu_in"].sem, 16)
                sp.wait_ge(s["dnl"].sem, s["dnl"].last(i))
                sp.wait_ge(s["dnh"].sem, s["dnh"].last(i))
                sp.dma_start(dnf[:], a["DN"][bass.ds((i + (MOE_E - 1)) * P, P), :]).then_inc(s["dn_in"].sem, 16)
            sp.wait_ge(given, 16 * N * TOP)
            sp.dma_start(table[:].rearrange("t s k -> t (s k)"), a["slots"].rearrange("(t s) k -> t (s k)", s=SLOTS)).then_inc(listed, 16)

        @block.gpsimd
        def _(pool):
            ph.credit(pool)
            pool.wait_ge(freed, 16)
            pool.wait_ge(consts, 16 * 11)
            pool.wait_ge(routing.placed, 1)
            for n in range(N):
                for j in range(TOP):
                    nc.gpsimd.indirect_dma_start(a["slots"], bass.IndirectOffsetOnAxis(ap=slot6[:, n, j:j + 1], axis=0), pair[:, n, j], None).then_inc(given, 16)
            pool.wait_ge(given, 16 * N * TOP)

        def hidden():
            k = 0
            for blk in range(NB):
                for c, (at_, m) in enumerate(ICH):
                    yield k, blk, c, at_, m
                    k += 1

        @block.scalar
        def _(act):
            for dst, src in ((ident, K["ident"]), (routing.bias, a["gate_b"]), (routing.low4, K["low4"]),
                             (routing.low16, K["low16"]), (before, K["before"]), (ones, K["ones"]), (routing.order, K["order"]),
                             (routing.token, K["token"]), (routing.filled, K["filled"]), (routing.tiles, K["tiles"])):
                act.dma_start(dst[:], src).then_inc(consts, 16)
            act.dma_start(pair[:].rearrange("p n j k -> p (n j k)"), K["pair"]).then_inc(consts, 16)
            act.dma_start(acc[:], a["x3"].rearrange("(n p) d -> p n d", p=P)).then_inc(s["acc_in"].sem, 16)
            act.dma_start(a["slots"], K["free"]).then_inc(freed, 16)

            def lead_of_weights(i):
                act.wait_ge(s["gu_in"].sem, s["gu_in"].now(i))
                act.wait_ge(s["gu"].sem, s["gu"].part(i, 0))
                nc.scalar.copy(guh[:].rearrange("p a c n -> p (a c n)"), guf[:]).then_inc(s["guh"].sem, 1)

            def expert(i):
                for k, blk, c, o, m in hidden():
                    act.wait_ge(s["gu"].sem, s["gu"].part(i, k + 1))
                    act.wait_ge(s["il"].sem, s["il"].part(i, k - 1))
                    nc.scalar.activation(sil[k % 2][0:m], bank[2 * (k % 3)][0:m, :], ACT.Silu).then_inc(s["sil"].sem, 1)
                    act.wait_ge(s["prod"].sem, s["prod"].part(i, k + 1))
                    act.wait_ge(s["dn"].sem, s["dn"].part(i, blk * TB // P))
                    nc.scalar.copy(ih[0:m, c], sil[k % 2][0:m]).then_inc(s["ih"].sem, 1)
                    if k == 1:
                        act.wait_ge(s["dn_in"].sem, s["dn_in"].now(i))
                        nc.scalar.copy(dnh[:].rearrange("p c n -> p (c n)"), dnf[:]).then_inc(s["dnh"].sem, 1)

            lead_of_weights(1)
            for blk in range(NB):
                act.wait_ge(logits_made, blk + 1)
                nc.scalar.copy(logits[:, blk * TB:(blk + 1) * TB], bank[blk][0:MOE_E, :]).then_inc(logits_out, 1)
            act.wait_ge(logits_turned, 1)
            nc.scalar.activation(routing.sc[:].rearrange("p n e -> p (n e)"), bank[4][:, 0:N * MOE_E], ACT.Sigmoid).then_inc(routing.scored, 1)
            nc.scalar.preload_act_table_set("silu_and_others")
            expert(1)
            lead_of_weights(2)
            expert(2)

        @block.vector
        def _(dve):
            def add(i, blk):
                for n in range(blk * TB // P, (blk + 1) * TB // P):
                    if n == N - 2 and i < NS:
                        trail_of_weights(i + 1)
                    dve.wait_ge(s["dn"].sem, s["dn"].part(i, n + 1))
                    dve.wait_ge(s["acc"].sem, s["acc"].part(i, n + 1 - N))
                    nc.vector.tensor_tensor(acc[:, n], bank[6 + n % 2][:], acc[:, n], ALU.add).then_inc(s["acc"].sem, 1)

            def trail_of_weights(i):
                dve.wait_ge(s["guh"].sem, s["guh"].now(i))
                nc.vector.tensor_tensor(gul[:].rearrange("p a c n -> p (a c n)"), guf[:],
                                        guh[:].bitcast(F32).rearrange("p a c n -> p (a c n)"), ALU.subtract).then_inc(s["gul"].sem, 1)

            def expert(i, beside):
                for k, blk, c, o, m in hidden():
                    dve.wait_ge(s["sil"].sem, s["sil"].part(i, k + 1))
                    nc.vector.tensor_tensor(sil[k % 2][0:m], sil[k % 2][0:m], bank[2 * (k % 3) + 1][0:m, :], ALU.mult).then_inc(s["prod"].sem, 1)
                    if blk and c == 0:
                        add(i, blk - 1)
                    dve.wait_ge(s["ih"].sem, s["ih"].part(i, k + 1))
                    nc.vector.tensor_tensor(il[0:m, c], sil[k % 2][0:m], ih[0:m, c].bitcast(F32), ALU.subtract).then_inc(s["il"].sem, 1)
                    if k == 1:
                        dve.wait_ge(s["dnh"].sem, s["dnh"].now(i))
                        nc.vector.tensor_tensor(dnl[:].rearrange("p c n -> p (c n)"), dnf[:],
                                                dnh[:].bitcast(F32).rearrange("p c n -> p (c n)"), ALU.subtract).then_inc(s["dnl"].sem, 1)
                    if blk == NB - 1 and c == 2:
                        add(i, blk)
                    if k in beside:
                        beside[k]()

            dve.wait_ge(gate_in, 16)
            flat = "p c e -> p (c e)"
            nc.vector.tensor_copy(gh[:].rearrange(flat), gf[:]).then_inc(lead, 1)
            dve.wait_ge(lead, 1)
            nc.vector.tensor_tensor(gl[:].rearrange(flat), gf[:], gh[:].bitcast(F32).rearrange(flat), ALU.subtract).then_inc(trail, 1)
            trail_of_weights(1)
            dve.wait_ge(consts, 16 * 11)
            dve.wait_ge(s["acc_in"].sem, s["acc_in"].now(1))
            expert(1, {
                0: routing.groups,
                1: routing.group_choice,
                2: lambda: routing.equal_before(routing.sfc[:], MOE_E, routing.low16),
                3: lambda: routing.larger(routing.sfc[:], MOE_E),
                4: routing.choice,
                5: routing.counts,
                6: routing.earlier_tiles,
                7: routing.place_in_expert,
                8: routing.slots,
                9: routing.slots_of_tokens,
            })
            expert(2, {0: routing.weights, 1: routing.weights_of_tokens, 3: routing.rows_of_tiles})
            nc.vector.memset(y_row[:, :, 0:1], NOWHERE).then_inc(rows_made, 1)
            dve.wait_ge(turned, 2)
            nc.vector.tensor_copy(x_row[:], bank[0][:, 0:2 * TILES].rearrange("p (h t) -> p h t", h=2)).then_inc(rows_made, 1)
            nc.vector.tensor_copy(y_row[:, :, 1:], bank[1][:, 0:2 * TILES].rearrange("p (h t) -> p h t", h=2)).then_inc(rows_made, 1)
            dve.wait_ge(rows_made, 3)

        @block.tensor
        def _(pe):
            def down(i, blk):
                pe.wait_ge(s["dnl"].sem, s["dnl"].now(i))
                pe.wait_ge(s["il"].sem, s["il"].part(i, len(ICH) * (blk + 1)))
                for n in range(blk * TB // P, (blk + 1) * TB // P):
                    pe.wait_ge(s["acc"].sem, s["acc"].part(i, n - 1))
                    t = slice(n * P - blk * TB, (n + 1) * P - blk * TB)
                    for q, (o, m) in enumerate(ICH):
                        last = exact3(pe, bank[6 + n % 2][:], lambda _: ih[0:m, q, t], lambda _: il[0:m, q, t],
                                      lambda _: dnh[0:m, q, :], lambda _: dnl[0:m, q, :], start=(q == 0), stop=(q == 2), n=1)
                    last.then_inc(s["dn"].sem, 1)

            def expert(i, beside):
                pe.wait_ge(s["gul"].sem, s["gul"].now(i))
                for k, blk, c, o, m in hidden():
                    pe.wait_ge(s["prod"].sem, s["prod"].part(i, k - 2))
                    for u in range(2):
                        last = exact3(pe, bank[2 * (k % 3) + u][0:m, :], lambda q: guh[:, u, q, o:o + m], lambda q: gul[:, u, q, o:o + m],
                                      lambda q: xh[:, q, blk * TB:(blk + 1) * TB], lambda q: xl[:, q, blk * TB:(blk + 1) * TB])
                    last.then_inc(s["gu"].sem, 1)
                    if blk and c == 0:
                        if blk - 1 in beside:
                            beside[blk - 1]()
                        down(i, blk - 1)
                down(i, NB - 1)

            def counts():
                pe.wait_ge(routing.chosen, 1)
                pe.wait_ge(s["acc"].sem, s["acc"].part(1, N // NB))
                for k, m in ((6, before), (7, ones)):
                    pe.matmul(bank[k][:, 0:N * MOE_E], m[:], routing.sel[:].rearrange("p n e -> p (n e)"), start=True, stop=True).then_inc(routing.counted, 1)
                pe.wait_ge(routing.counts_read, 2)

            pe.wait_ge(trail, 1)
            for blk in range(NB):
                exact3(pe, bank[blk][0:MOE_E, :], lambda c: gh[:, c, :], lambda c: gl[:, c, :], lambda c: xh[:, c, blk * TB:(blk + 1) * TB],
                       lambda c: xl[:, c, blk * TB:(blk + 1) * TB]).then_inc(logits_made, 1)
            pe.wait_ge(consts, 16 * 11)
            pe.wait_ge(logits_out, NB)
            for n in range(N):
                last = pe.transpose(bank[4][:, n * MOE_E:(n + 1) * MOE_E], logits[:, n * P:(n + 1) * P], ident[0:MOE_E, 0:MOE_E])
            last.then_inc(logits_turned, 1)
            pe.wait_ge(routing.scored, 1)
            expert(1, {1: counts})
            expert(2, {})
            pe.wait_ge(listed, 16)
            for k in range(2):
                for h in range(2):
                    last = pe.transpose(bank[k][:, h * TILES:(h + 1) * TILES], table[:, h * P:(h + 1) * P, k], ident[0:TILES, 0:TILES])
                last.then_inc(turned, 1)
    nc.clear_and_free_semaphores([gate_in, consts, freed, lead, trail, logits_made, logits_out, logits_turned, given, listed, turned, rows_made,
                                  *routing.semaphores()])
    ph.end()


def routed_experts(nc, K, bank, a, x_row, y_row, expert_row):
    ph = Phase(nc, "routed")
    GU, DN, NR = 2 * KC * MOE_I, 3 * D, (MOE_E + NS) * P
    guf, dnf = ph.sb2("guf", [P, GU]), ph.sb2("dnf", [P, DN])
    guh, gul = ph.sb2("guh", [P, 2, KC, MOE_I], F32R), ph.sb2("gul", [P, 2, KC, MOE_I], F32R)
    dnh, dnl = ph.sb2("dnh", [P, 3, D], F32R), ph.sb2("dnl", [P, 3, D], F32R)
    x, xh, xl = ph.sb2("x", [P, 2, D]), ph.sb2("xh", [P, KC, SLOTS], F32R), ph.sb2("xl", [P, KC, SLOTS], F32R)
    ih, il = ph.sb2("ih", [P, 3, SLOTS], F32R), ph.sb2("il", [P, 3, SLOTS], F32R)
    sil = ph.sb2("sil", [P, SLOTS])
    y = ph.sb2("y", [P, 2, D])
    zero, ident = ph.sb("zero", [P, DN]), ph.sb("ident", [P, P])
    xi, yi, wi = ph.sb2("xi", [P, 2], U32), ph.sb2("yi", [P, 2], U32), ph.sb2("wi", [P, 1], U32)
    gu_bank, y_bank, t_bank = bank[0:3], bank[3:5], bank[5:7]
    s = {n: ph.counter(n, per) for n, per in
         [("rows", 2), ("turned", 2), ("xh", 2), ("xl", 2), ("guh", 2), ("gul", 2), ("dnh", 2), ("dnl", 2), ("gu", 6), ("sil", 6), ("prod", 6),
          ("ih", 6), ("il", 6), ("dn", 4), ("y", 4)]}
    x_in, gu_in, dn_in, y_out = ([nc.alloc_semaphore(name=f"routed_{n}{q}") for q in range(2)] for n in ("x_in", "gu_in", "dn_in", "y_out"))
    asked, consts, zeroed = (nc.alloc_semaphore(name=f"routed_{n}") for n in ("asked", "consts", "zeroed"))

    with nc.Block() as block:
        @block.sync
        def _(sp):
            sp.dma_start(ident[:], K["ident"]).then_inc(consts, 16)

        @block.gpsimd
        def _(pool):
            ph.credit(pool)

            def tokens(q):
                for h in range(2):
                    nc.gpsimd.indirect_dma_start(x[q][:, h], None, a["x3"], bass.IndirectOffsetOnAxis(ap=xi[q][:, h:h + 1], axis=0)).then_inc(x_in[q], 16)

            def weights(dst, src, q, landed):
                nc.gpsimd.indirect_dma_start(dst[q][:], None, a[src], bass.IndirectOffsetOnAxis(ap=wi[q][:], axis=0),
                                             bounds_check=NR - 1, oob_is_err=False).then_inc(landed[q], 16)

            def products(q):
                for h in range(2):
                    nc.gpsimd.indirect_dma_start(a["y"], bass.IndirectOffsetOnAxis(ap=yi[q][:, h:h + 1], axis=0), y[q][:, h], None,
                                                 bounds_check=B * L * TOP - 1, oob_is_err=False).then_inc(y_out[q], 16)

            pool.wait_ge(zeroed, 6)
            for q in range(2):
                tokens(q)
                weights(guf, "GU", q, gu_in)
                weights(dnf, "DN", q, dn_in)
            pool.wait_ge(zeroed, 13)
            for q in range(2):
                products(q)
            with pool.Fori(1, PAIRS + 1) as i:
                for r in range(2):
                    pool.wait_ge(s["rows"].sem, s["rows"].part(i, r + 1))
                    pool.sem_inc(asked, 1)
                    tokens(r)
                    pool.wait_ge(s["gul"].sem, s["gul"].part(i, r + 1))
                    pool.sem_inc(asked, 1)
                    weights(guf, "GU", r, gu_in)
                    pool.wait_ge(s["dnl"].sem, s["dnl"].part(i, r + 1))
                    pool.sem_inc(asked, 1)
                    weights(dnf, "DN", r, dn_in)
                    pool.wait_ge(s["y"].sem, s["y"].part(i, 2 * r + 2))
                    pool.sem_inc(asked, 1)
                    products(r)
            for q in range(2):
                pool.wait_ge(y_out[q], 32 * (PAIRS + 1))
                pool.wait_ge(x_in[q], 32 * (PAIRS + 1))
                pool.wait_ge(gu_in[q], 16 * (PAIRS + 1))
                pool.wait_ge(dn_in[q], 16 * (PAIRS + 1))

        @block.scalar
        def _(act):
            nc.scalar.preload_act_table_set("silu_and_others")

            def turned_lead(q, done):
                for k in range(2):
                    last = nc.scalar.copy(xh[q][:, 2 * k:2 * k + 2].rearrange("p c t -> p (c t)"), t_bank[k][:])
                last.then_inc(done, 1)

            act.wait_ge(gu_in[0], 16)
            nc.scalar.copy(guh[0][:].rearrange("p a c n -> p (a c n)"), guf[0][:]).then_inc(s["guh"].sem, 1)
            act.wait_ge(s["turned"].sem, s["turned"].part(1, 1))
            turned_lead(0, s["xh"].sem)
            with act.Fori(1, PAIRS + 1) as i:
                for r in range(2):
                    q = 1 - r
                    act.wait_ge(gu_in[q], 16 * (i + r))
                    act.wait_ge(s["gu"].sem, s["gu"].part(i, 3 * r))
                    nc.scalar.copy(guh[q][:].rearrange("p a c n -> p (a c n)"), guf[q][:]).then_inc(s["guh"].sem, 1)
                    for c, (o, m) in enumerate(ICH):
                        act.wait_ge(s["gu"].sem, s["gu"].part(i, 3 * r + c + 1))
                        act.wait_ge(s["il"].sem, s["il"].part(i, 3 * r + c - 1))
                        nc.scalar.activation(sil[(3 * r + c) % 2][0:m], gu_bank[c][0:m, 0:SLOTS], ACT.Silu).then_inc(s["sil"].sem, 1)
                        if c == 0:
                            act.wait_ge(dn_in[r], 16 * i)
                            act.wait_ge(s["dn"].sem, s["dn"].part(i, 2 * r))
                            nc.scalar.copy(dnh[r][:].rearrange("p c n -> p (c n)"), dnf[r][:]).then_inc(s["dnh"].sem, 1)
                        act.wait_ge(s["prod"].sem, s["prod"].part(i, 3 * r + c + 1))
                        nc.scalar.copy(ih[r][0:m, c], sil[(3 * r + c) % 2][0:m]).then_inc(s["ih"].sem, 1)
                    act.wait_ge(s["turned"].sem, s["turned"].part(i, r + 2))
                    turned_lead(q, s["xh"].sem)
                    act.wait_ge(y_out[r], 32 * i)
                    for h in range(2):
                        act.wait_ge(s["dn"].sem, s["dn"].part(i, 2 * r + h + 1))
                        nc.scalar.copy(y[r][:, h], y_bank[h][:]).then_inc(s["y"].sem, 1)

        @block.vector
        def _(dve):
            def turned_trail(q, done):
                for k in range(2):
                    c = slice(2 * k, 2 * k + 2)
                    last = nc.vector.tensor_tensor(xl[q][:, c].rearrange("p c t -> p (c t)"), t_bank[k][:],
                                                   xh[q][:, c].bitcast(F32).rearrange("p c t -> p (c t)"), ALU.subtract)
                last.then_inc(done, 1)

            for q in range(2):
                nc.vector.tensor_copy(xi[q][:], x_row[:, :, q]).then_inc(zeroed, 1)
                nc.vector.tensor_copy(wi[q][:], expert_row[:, q:q + 1]).then_inc(zeroed, 1)
                nc.vector.tensor_copy(yi[q][:], y_row[:, :, 0]).then_inc(zeroed, 1)
            nc.vector.memset(zero[:], 0.0).then_inc(zeroed, 1)
            dve.wait_ge(zeroed, 7)
            for dst in (dnh[1], dnl[1], ih[1], il[1]):
                nc.vector.tensor_copy(dst[:].rearrange("p c n -> p (c n)"), zero[:, 0:3 * dst.shape[2]]).then_inc(zeroed, 1)
            for q in range(2):
                nc.vector.tensor_copy(y[q][:].rearrange("p h d -> p (h d)"), zero[:, 0:2 * D]).then_inc(zeroed, 1)
            dve.wait_ge(s["guh"].sem, s["guh"].part(1, 1))
            nc.vector.tensor_tensor(gul[0][:].rearrange("p a c n -> p (a c n)"), guf[0][:],
                                    guh[0][:].bitcast(F32).rearrange("p a c n -> p (a c n)"), ALU.subtract).then_inc(s["gul"].sem, 1)
            dve.wait_ge(s["xh"].sem, s["xh"].part(1, 1))
            turned_trail(0, s["xl"].sem)
            with dve.Fori(1, PAIRS + 1) as i:
                for r in range(2):
                    q = 1 - r
                    dve.wait_ge(s["turned"].sem, s["turned"].part(i, r + 1))
                    dve.wait_ge(s["guh"].sem, s["guh"].part(i, r + 1))
                    dve.wait_ge(dn_in[r], 16 * i)
                    dve.wait_ge(y_out[r], 32 * i)
                    nc.vector.tensor_copy(xi[r][:], x_row[:, :, bass.ds(i * 2 + r, 1)].rearrange("p h o -> p (h o)"))
                    nc.vector.tensor_copy(yi[r][:], y_row[:, :, bass.ds(i * 2 + (r - 2), 1)].rearrange("p h o -> p (h o)"))
                    nc.vector.tensor_copy(wi[r][:], expert_row[:, bass.ds(i * 2 + r, 1)]).then_inc(s["rows"].sem, 1)
                    dve.wait_ge(s["guh"].sem, s["guh"].part(i, r + 2))
                    nc.vector.tensor_tensor(gul[q][:].rearrange("p a c n -> p (a c n)"), guf[q][:],
                                            guh[q][:].bitcast(F32).rearrange("p a c n -> p (a c n)"), ALU.subtract).then_inc(s["gul"].sem, 1)
                    for c, (o, m) in enumerate(ICH):
                        k = (3 * r + c) % 2
                        dve.wait_ge(s["sil"].sem, s["sil"].part(i, 3 * r + c + 1))
                        nc.vector.tensor_tensor(sil[k][0:m], sil[k][0:m], gu_bank[c][0:m, SLOTS:], ALU.mult).then_inc(s["prod"].sem, 1)
                        if c == 0:
                            dve.wait_ge(s["dnh"].sem, s["dnh"].part(i, r + 1))
                            nc.vector.tensor_tensor(dnl[r][:].rearrange("p c n -> p (c n)"), dnf[r][:],
                                                    dnh[r][:].bitcast(F32).rearrange("p c n -> p (c n)"), ALU.subtract).then_inc(s["dnl"].sem, 1)
                        dve.wait_ge(s["ih"].sem, s["ih"].part(i, 3 * r + c + 1))
                        nc.vector.tensor_tensor(il[r][0:m, c], sil[k][0:m], ih[r][0:m, c].bitcast(F32), ALU.subtract).then_inc(s["il"].sem, 1)
                    dve.wait_ge(s["xh"].sem, s["xh"].part(i, r + 2))
                    turned_trail(q, s["xl"].sem)

        @block.tensor
        def _(pe):
            def turn(q):
                for c in range(KC):
                    for h in range(2):
                        o = (c % 2) * SLOTS + h * P
                        last = pe.transpose(t_bank[c // 2][:, o:o + P], x[q][:, h, c * P:(c + 1) * P], ident[:])
                last.then_inc(s["turned"].sem, 1)

            pe.wait_ge(consts, 16)
            pe.wait_ge(zeroed, 13)
            pe.wait_ge(x_in[0], 32)
            turn(0)
            with pe.Fori(1, PAIRS + 1) as i:
                for r in range(2):
                    q = 1 - r
                    pe.wait_ge(s["gul"].sem, s["gul"].part(i, r + 1))
                    pe.wait_ge(s["xl"].sem, s["xl"].part(i, r + 1))
                    for c, (o, m) in enumerate(ICH):
                        pe.wait_ge(s["prod"].sem, s["prod"].part(i, 3 * r + c - 2))
                        for u in range(2):
                            last = exact3(pe, gu_bank[c][0:m, u * SLOTS:(u + 1) * SLOTS], lambda k: guh[r][:, u, k, o:o + m],
                                          lambda k: gul[r][:, u, k, o:o + m], lambda k: xh[r][:, k, :], lambda k: xl[r][:, k, :])
                        last.then_inc(s["gu"].sem, 1)
                    pe.wait_ge(x_in[q], 32 * (i + r))
                    turn(q)
                    pe.wait_ge(s["dnl"].sem, s["dnl"].part(i, r))
                    pe.wait_ge(s["il"].sem, s["il"].part(i, 3 * r))
                    for h in range(2):
                        pe.wait_ge(s["y"].sem, s["y"].part(i, 2 * r + h - 1))
                        t = slice(h * P, (h + 1) * P)
                        for c, (o, m) in enumerate(ICH):
                            last = exact3(pe, y_bank[h][:], lambda k: ih[q][0:m, c, t], lambda k: il[q][0:m, c, t],
                                          lambda k: dnh[q][0:m, c, :], lambda k: dnl[q][0:m, c, :], start=(c == 0), stop=(c == 2), n=1)
                        last.then_inc(s["dn"].sem, 1)
    nc.clear_and_free_semaphores([*x_in, *gu_in, *dn_in, *y_out, asked, consts, zeroed])
    ph.end()


def experts(nc, K, bank, a):
    N = B * NT
    top = ExitStack()
    acc = top.enter_context(nc.sbuf_tensor("moe_acc", [P, N, D], F32))
    w6 = top.enter_context(nc.sbuf_tensor("moe_w6", [P, N, TOP], F32))
    slot6 = top.enter_context(nc.sbuf_tensor("moe_slot6", [P, N, TOP], U32))
    x_row = top.enter_context(nc.sbuf_tensor("moe_x_row", [P, 2, TILES], U32))
    y_row = top.enter_context(nc.sbuf_tensor("moe_y_row", [P, 2, TILES + 1], U32))
    expert_row = top.enter_context(nc.sbuf_tensor("moe_expert_row", [P, TILES], U32))
    columns = ExitStack()
    xh = columns.enter_context(nc.sbuf_tensor("moe_xh", [P, KC, N * P], F32R))
    xl = columns.enter_context(nc.sbuf_tensor("moe_xl", [P, KC, N * P], F32R))
    load_split(nc, "moe_x", [(a["x3T"][n * P:(n + 1) * P, :], xh[:, :, n * P:(n + 1) * P], xl[:, :, n * P:(n + 1) * P])
                             for n in range(N)], stage_cols=D)
    shared_experts(nc, K, bank, a, acc, w6, slot6, x_row, y_row, expert_row, xh, xl)
    columns.close()
    routed_experts(nc, K, bank, a, x_row, y_row, expert_row)

    ph = Phase(nc, "last")
    y = [ph.sb(f"y{k}", [P, TOP, D]) for k in range(4)]
    st, mv, rs, eps = ph.sb("st", [P, N, 6]), ph.sb("mv", [P, N, 2]), ph.sb("rs", [P, 2, N]), ph.sb("eps", [P, 1])
    less = ph.sb("less", [P, N])
    added, stats, aggr, root, negated, centred, inv, done, stored = (
        nc.alloc_semaphore(name=f"last_{n}") for n in ("added", "stats", "aggr", "root", "negated", "centred", "inv", "done", "stored"))
    y_in = [nc.alloc_semaphore(name=f"last_y_in{k}") for k in range(4)]
    with nc.Block() as block:
        @block.sync
        def _(sp):
            rows = a["y"].rearrange("(n p j) d -> n p (j d)", p=P, j=TOP)
            for n in range(N):
                if n >= 4:
                    sp.wait_ge(added, ((n - 4) // 2 + 1) * 2 * TOP)
                sp.dma_start(y[n % 4][:].rearrange("p j d -> p (j d)"), rows[n]).then_inc(y_in[n % 4], 16)

        @block.vector
        def _(dve):
            nc.vector.memset(eps[:], 1e-5)

            def inverse(m):
                dve.wait_ge(root, 2 * m + 2)
                nc.vector.reciprocal(rs[:, 1, 2 * m:2 * m + 2], rs[:, 0, 2 * m:2 * m + 2]).then_inc(inv, 1)

            for m in range(N // 2):
                for j in range(TOP):
                    for n in (2 * m, 2 * m + 1):
                        if j == 0:
                            dve.wait_ge(y_in[n % 4], 16 * (n // 4 + 1))
                        else:
                            dve.wait_ge(added, 2 * (m * TOP + j) - 1 + n % 2)
                        nc.vector.scalar_tensor_tensor(acc[:, n], y[n % 4][:, j], w6[:, n, j:j + 1], acc[:, n], ALU.mult, ALU.add).then_inc(added, 1)
                for n in (2 * m, 2 * m + 1):
                    dve.wait_ge(added, 2 * (m + 1) * TOP - 1 + n % 2)
                    nc.vector.bn_stats(st[:, n], acc[:, n]).then_inc(stats, 1)
                for n in (2 * m, 2 * m + 1):
                    dve.wait_ge(stats, n + 1)
                    nc.vector.bn_aggr(mv[:, n], st[:, n]).then_inc(aggr, 1)
                if m:
                    inverse(m - 1)
            inverse(N // 2 - 1)

        @block.scalar
        def _(act):
            nc.scalar.preload_act_table_set("sqrt_and_others")

            def roots(m):
                for n in (2 * m, 2 * m + 1):
                    act.wait_ge(aggr, n + 1)
                    nc.scalar.activation(rs[:, 0, n:n + 1], mv[:, n, 1:2], ACT.Sqrt, bias=eps[:, 0:1]).then_inc(root, 1)
                    nc.scalar.mul(less[:, n:n + 1], mv[:, n, 0:1], -1.0).then_inc(negated, 1)

            def normed(m):
                for n in (2 * m, 2 * m + 1):
                    act.wait_ge(negated, n + 1)
                    nc.scalar.activation(acc[:, n], acc[:, n], ACT.Identity, bias=less[:, n:n + 1]).then_inc(centred, 1)
                act.wait_ge(inv, m + 1)
                for n in (2 * m, 2 * m + 1):
                    act.wait_ge(centred, n + 1)
                    nc.scalar.activation(acc[:, n], acc[:, n], ACT.Copy, scale=rs[:, 1, n:n + 1]).then_inc(done, 1)

            for m in range(N // 2):
                roots(m)
                if m:
                    normed(m - 1)
            normed(N // 2 - 1)

        @block.gpsimd
        def _(pool):
            for n in range(N):
                i, b = n // B, n % B
                pool.wait_ge(done, n + 1)
                pool.dma_start(a["out"][b, i * P:(i + 1) * P, :], acc[:, n]).then_inc(stored, 16)
            pool.wait_ge(stored, 16 * N)
    ph.stack.close()
    top.close()


def shape_constants():
    N = B * NT
    tok = np.arange(P)
    sub, mid = tok // SUB, (tok // SUB) * SUB + SUB // 2 - 1
    src, dst = tok[:, None], tok[None, :]
    same = sub[:, None] == sub[None, :]
    m = mid[None, :]
    cum = same * (((src > m) & (src <= dst)) * 1.0 - ((src > dst) & (src <= m)) * 1.0)
    edges = [-1, *(np.arange(NSUB) * SUB + SUB // 2 - 1), P - 1]
    sel = np.stack([(tok > lo) & (tok <= hi) for lo, hi in zip(edges[:-1], edges[1:])], 1)
    return {
        "ident": np.eye(P),
        "cum": cum,
        "sel": sel,
        "causal": same & (src <= dst),
        "tri": ((tok[:, None] // TTT) % HG == tok[None, :HG * TTT] // TTT) & (tok[:, None] % TTT <= tok[None, :HG * TTT] % TTT),
        "seq": tok[:, None] // (HG * TTT) == np.arange(2)[None, :],
        "low4": np.broadcast_to(np.tri(MOE_G, k=-1).reshape(1, -1), (P, MOE_G ** 2)),
        "low16": np.broadcast_to(np.tri(MOE_E, k=-1).reshape(1, -1), (P, MOE_E ** 2)),
        "own": tok[:, None] // DH == np.arange(HG)[None, :],
        "order": np.broadcast_to(np.arange(EXPERTS), (P, EXPERTS)),
        "before": src < dst,
        "ones": np.ones((P, P)),
        "token": tok[:, None],
        "filled": np.broadcast_to(np.arange(B * L // SLOTS) * SLOTS, (P, B * L // SLOTS)),
        "tiles": np.broadcast_to(np.arange(TILES), (P, TILES)),
        "pair": np.stack(np.broadcast_arrays((np.arange(N)[None, :] * P + tok[:, None])[:, :, None],
                                             ((np.arange(N)[None, :] * P + tok[:, None]) * TOP)[:, :, None] + np.arange(TOP)), 3).reshape(P, -1),
        "free": np.stack(np.broadcast_arrays(0, NOWHERE + np.arange(TILES * SLOTS)), 1),
        "heads": (tok[:, None] // DH) == (tok[None, :] // DH),
    }


def by_feature(w):
    n = w.shape[0] // P
    return np.ascontiguousarray(w.reshape(n, P, -1).transpose(1, 0, 2).reshape(P, -1))


def layout(x):
    x = {k: np.asarray(v) for k, v in x.items()}
    tok = x["L0_attn_x"].reshape(B, NT, P, D).transpose(1, 0, 2, 3)
    a = {"x": tok.reshape(-1, D)}
    a["xT"] = tok.reshape(NT, B, P, KC, P).transpose(0, 1, 4, 3, 2).reshape(-1, D)
    for n in ("Wq", "Wk", "Wv", "Wg", "Wo"):
        a[n] = by_feature(x[f"L0_attn_{n}"].T)
    for n in ("gamma", "beta"):
        a[n] = x[f"L0_attn_{n}"].reshape(KC, P).T
    def on_all(v):
        return np.broadcast_to(v, (P, v.size))
    a["base"] = by_feature(x["L0_ffn_base_w"].T)
    a["base_b"], a["router_b"] = on_all(x["L0_ffn_base_b"]), on_all(x["L0_ffn_router_b"])
    ar = np.concatenate([x["L0_ffn_lora_A"].transpose(1, 0, 2).reshape(D, -1), x["L0_ffn_router_w"].T], 1)
    a["AR"] = by_feature(np.pad(ar, ((0, 0), (0, FULL_RATE - ar.shape[1]))))
    a["loraB"] = x["L0_ffn_lora_B"].reshape(EXPERTS * RANK, D)
    for n in ("Wq", "Wk", "Wv"):
        a[n + "3"] = by_feature(x[f"L1_attn_{n}"])
    a["Wo3"] = by_feature(x["L1_attn_Wo"])
    a["BG"] = by_feature(np.concatenate([x["L1_attn_Wbeta"], x["L1_attn_Wg1"]], 1))
    a["Wg2"] = x["L1_attn_Wg2"]
    for n in ("ln_w", "ln_b"):
        v = x[f"L1_attn_{n}"].reshape(KC, HG, DH).transpose(1, 0, 2).reshape(1, HG, 1, KC * DH)
        a[n] = np.broadcast_to(v, (B, HG, TTT, KC * DH)).reshape(P, KC * DH)
    for n in ("w", "b"):
        a[n + "_all"] = on_all(x["L1_attn_ln_" + n].reshape(KC, HG, DH).transpose(1, 0, 2).reshape(-1))
    a["gate_w"], a["gate_b"] = by_feature(x["L1_ffn_gate_weight"].T), on_all(x["L1_ffn_e_score_correction_bias"])
    f = "L1_ffn_"
    gu = [np.concatenate([x[f + n], x[f + "shared_" + m].reshape(2, MOE_I, D)]) for n, m in (("gate_proj", "gate_w"), ("up_proj", "up_w"))]
    gu = np.stack(gu, 1).reshape(-1, 2, MOE_I, KC, P)
    a["GU"] = gu.transpose(0, 4, 1, 3, 2).reshape(-1, 2 * KC * MOE_I)
    dn = np.concatenate([x[f + "down_proj"], x[f + "shared_down_w"].reshape(D, 2, MOE_I).transpose(1, 0, 2)]).transpose(0, 2, 1)
    dn = np.pad(dn, ((0, 0), (0, 3 * P - MOE_I), (0, 0))).reshape(-1, 3, P, D)
    a["DN"] = dn.transpose(0, 2, 1, 3).reshape(-1, 3 * D)
    a["norm_w"] = x["L1_attn_norm_w"].reshape(KC, P).T
    a = {k: np.ascontiguousarray(v) for k, v in a.items()}
    a.update({k: np.ascontiguousarray(v.astype(np.float32)) for k, v in shape_constants().items()})
    return a


def build(nc, a, out):
    N = B * L
    for name, cols in (("x1", D), ("x2", D), ("q3", D), ("qT", D), ("kT", D), ("te", H * (DH + 1)), ("sg", D), ("qh", D),
                       ("x3", D), ("x3T", D)):
        a[name] = nc.dram_tensor(f"mid_{name}", (N, cols), F32).ap()
    a["slots"] = nc.dram_tensor("mid_slots", (TILES * SLOTS, 2), F32).ap()
    a["y"] = nc.dram_tensor("mid_y", (N * TOP, D), F32).ap()
    a["out"] = out
    with ExitStack() as ctx:
        bank = [ctx.enter_context(nc.psum_tensor(f"bank{k}", [P, D], F32)) for k in range(8)]
        gated_recurrence(nc, a, bank, a)
        lora_and_projections(nc, a, bank, a)
        ttt_recurrence(nc, a, bank, a)
        attention_output(nc, a, bank, a)
        experts(nc, a, bank, a)


def kernel(**inputs):
    import concourse.bacc as bacc
    from concourse.bass_utils import run_bass_kernel_spmd

    nc = bacc.Bacc("TRN2", target_bir_lowering=False, num_devices=1)
    arrays = layout(inputs)
    a = {n: nc.dram_tensor(f"in_{n}", v.shape, F32, kind="ExternalInput").ap() for n, v in arrays.items()}
    out = nc.dram_tensor("out", (B, L, D), F32, kind="ExternalOutput").ap()
    build(nc, a, out)
    r = run_bass_kernel_spmd(nc, [{f"in_{n}": v for n, v in arrays.items()}], core_ids=[0])
    return r.results[0]["out"]
```
